# Optimizing a Trainium2 kernel written in Bass

```python
import numpy as np
import jax
import jax.numpy as jnp

def _softmax(x, axis=-1):
    return jax.nn.softmax(x, axis=axis)

def _gelu(x):
    return jax.nn.gelu(x, approximate=True)

def _silu(x):
    return jax.nn.silu(x)

def _sigmoid(x):
    return jax.nn.sigmoid(x)

def _layernorm(x, axis=-1, eps=1e-05):
    m = jnp.mean(x, axis=axis, keepdims=True)
    v = jnp.var(x, axis=axis, keepdims=True)
    return (x - m) / jnp.sqrt(v + eps)

def _scatter_add(tgt, idx, src, axis=0):
    return tgt.at[idx].add(src)

def _segment_sum(src, seg, n):
    return jax.ops.segment_sum(src, seg, n)
kernel_name = 'mk_macaron_d2_jaxref_r8_1e267e'

def setup_inputs(seed: int=0):
    np.random.seed(seed)
    _w = jnp.asarray

    def _L0_attn_setup():
        import jax, jax.numpy as jnp
        import numpy as np
        B, S, D, H, L, F = (4, 256, 128, 16, 8, 512)
        DH = D // H

        def _ln(x, g, b):
            m = jnp.mean(x, axis=-1, keepdims=True)
            v = jnp.mean((x - m) ** 2, axis=-1, keepdims=True)
            return (x - m) * jax.lax.rsqrt(v + 1e-05) * g + b

        def _phi(t):
            return jax.nn.elu(t) + 1.0
        key = jax.random.key(seed)
        ks = jax.random.split(key, 12)
        s = 0.02
        n = jax.random.normal
        return {'x': n(ks[0], (B, S, D), jnp.float32), 'Wq': n(ks[1], (L, D, D), jnp.float32) * s, 'bq': jnp.zeros((L, D), jnp.float32), 'Wk': n(ks[2], (L, D, D), jnp.float32) * s, 'bk': jnp.zeros((L, D), jnp.float32), 'Wv': n(ks[3], (L, D, D), jnp.float32) * s, 'bv': jnp.zeros((L, D), jnp.float32), 'Wo': n(ks[4], (L, D, D), jnp.float32) * s, 'bo': jnp.zeros((L, D), jnp.float32), 'g1': jnp.ones((L, D), jnp.float32), 'be1': jnp.zeros((L, D), jnp.float32), 'g2': jnp.ones((L, D), jnp.float32), 'be2': jnp.zeros((L, D), jnp.float32), 'W1': n(ks[5], (L, D, F), jnp.float32) * s, 'c1': jnp.zeros((L, F), jnp.float32), 'W2': n(ks[6], (L, F, D), jnp.float32) * s, 'c2': jnp.zeros((L, D), jnp.float32), 'gf': jnp.ones((D,), jnp.float32), 'bef': jnp.zeros((D,), jnp.float32)}
    _L0_attn_in = _L0_attn_setup()

    def _L0_ffn_setup():
        import jax, jax.numpy as jnp
        import numpy as np
        EMBED_DIM = 128
        HIDDEN_DIM = 512
        NUM_EXPERTS = 8
        TOP_K = 2
        key = jax.random.key(seed)
        k_x, k_g, k_w1, k_w2 = jax.random.split(key, 4)
        x = jax.random.normal(k_x, (2, 64, EMBED_DIM), dtype=jnp.float32)
        gate_w = jax.random.normal(k_g, (NUM_EXPERTS, EMBED_DIM), dtype=jnp.float32) * (1.0 / np.sqrt(EMBED_DIM))
        w1 = jax.random.normal(k_w1, (NUM_EXPERTS, EMBED_DIM, HIDDEN_DIM), dtype=jnp.float32) * np.sqrt(2.0 / EMBED_DIM)
        b1 = jnp.zeros((NUM_EXPERTS, HIDDEN_DIM), dtype=jnp.float32)
        w2 = jax.random.normal(k_w2, (NUM_EXPERTS, HIDDEN_DIM, EMBED_DIM), dtype=jnp.float32) * np.sqrt(2.0 / HIDDEN_DIM)
        b2 = jnp.zeros((NUM_EXPERTS, EMBED_DIM), dtype=jnp.float32)
        return {'x': x, 'gate_w': gate_w, 'w1': w1, 'b1': b1, 'w2': w2, 'b2': b2}
    _L0_ffn_in = _L0_ffn_setup()

    def _L1_attn_setup():
        import math
        import jax, jax.numpy as jnp
        import numpy as np
        B_SZ, L_SEQ, D_MODEL, N_STATE = (4, 512, 128, 16)
        DT_RANK = math.ceil(D_MODEL / 16)
        CONV_K = 3
        DT_MIN, DT_MAX = (0.001, 0.1)

        def _inverse_softplus(x):
            return x + jnp.log(1.0 - jnp.exp(-x))

        def _largest_factor_up_to(b, n):
            if n < 2:
                return n
            k = b
            while n % k != 0:
                k -= 1
            return k

        def _ssm_chunked_scan(x, A, Bc, Cc, dt):
            B, L, D = x.shape
            N = A.shape[-1]
            chunk = _largest_factor_up_to(int(math.sqrt(L)), L)
            nc = L // chunk
            r3 = lambda t, F: t.reshape(B, nc, chunk, F).transpose(1, 2, 0, 3)
            xc, dtc = (r3(x, D), r3(dt, D))
            bc, cc = (r3(Bc, N), r3(Cc, N))

            def assoc(lft, rgt):
                g_l, h_l = lft
                g_r, h_r = rgt
                return (g_l * g_r, g_r * h_l + h_r)

            def scan_chunk(carry, ch):
                g0, h0 = carry
                xk, bk, ck, dk = ch
                dA = jnp.exp(jnp.einsum('dn,lbd->lbdn', A, dk))
                dB = jnp.einsum('lbn,lbd,lbd->lbdn', bk, xk, dk)
                gs, hs = jax.lax.associative_scan(assoc, (dA, dB))
                hs = gs * h0 + hs
                yk = jnp.einsum('lbn,lbdn->lbd', ck, hs)
                return ((gs[-1:] * g0, hs[-1:]), yk)
            init = (jnp.ones((1, B, D, N), x.dtype), jnp.zeros((1, B, D, N), x.dtype))
            _, yc = jax.lax.scan(scan_chunk, init, (xc, bc, cc, dtc))
            return yc.transpose(2, 0, 1, 3).reshape(B, L, D)
        key = jax.random.key(seed)
        ks = jax.random.split(key, 6)
        x = jax.random.normal(ks[0], (B_SZ, L_SEQ, D_MODEL), dtype=jnp.float32)
        conv_w = jax.random.normal(ks[1], (CONV_K, D_MODEL), dtype=jnp.float32) / jnp.sqrt(3.0)
        W_bc = jax.random.normal(ks[2], (D_MODEL, 2 * N_STATE), dtype=jnp.float32) / jnp.sqrt(float(D_MODEL))
        b_bc = jnp.zeros((2 * N_STATE,), dtype=jnp.float32)
        W_dt = jax.random.normal(ks[3], (D_MODEL, DT_RANK), dtype=jnp.float32) / jnp.sqrt(float(D_MODEL))
        b_dt = jnp.zeros((DT_RANK,), dtype=jnp.float32)
        W_dtp = jax.random.normal(ks[4], (DT_RANK, D_MODEL), dtype=jnp.float32) / jnp.sqrt(float(DT_RANK))
        u0 = jax.random.uniform(ks[5], (D_MODEL,), dtype=jnp.float32, minval=DT_MIN, maxval=DT_MAX)
        b_dtp = _inverse_softplus(u0)
        A_log = jnp.log(jnp.tile(jnp.arange(1, N_STATE + 1, dtype=jnp.float32)[None, :], (D_MODEL, 1)))
        Dcoeff = jnp.ones((D_MODEL,), dtype=jnp.float32)
        return dict(x=x, conv_w=conv_w, W_bc=W_bc, b_bc=b_bc, W_dt=W_dt, b_dt=b_dt, W_dtp=W_dtp, b_dtp=b_dtp, A_log=A_log, Dcoeff=Dcoeff)
    _L1_attn_in = _L1_attn_setup()

    def _L1_ffn_setup():
        import jax, jax.numpy as jnp
        import numpy as np
        EPS = 1e-05

        def _layernorm(x, w, b):
            mu = jnp.mean(x, axis=-1, keepdims=True)
            var = jnp.mean((x - mu) ** 2, axis=-1, keepdims=True)
            return (x - mu) * jax.lax.rsqrt(var + EPS) * w + b

        def _rope_tables(T, D, base=10000.0):
            inv_freq = 1.0 / base ** (jnp.arange(0, D, 2, dtype=jnp.float32) / D)
            t = jnp.arange(T, dtype=jnp.float32)
            freqs = jnp.einsum('i,j->ij', t, inv_freq)
            emb = jnp.concatenate([freqs, freqs], axis=-1)
            return (jnp.cos(emb), jnp.sin(emb))

        def _rotate_half(x):
            x1, x2 = (x[..., :x.shape[-1] // 2], x[..., x.shape[-1] // 2:])
            return jnp.concatenate([-x2, x1], axis=-1)

        def _attn(x, ln_w, ln_b, conv_w, attn_w, proj_w, n_head):
            B, T, C = x.shape
            D = C // n_head
            h = _layernorm(x, ln_w, ln_b)
            hc = jnp.transpose(h, (0, 2, 1))
            hc = jnp.pad(hc, ((0, 0), (0, 0), (2, 0)))
            hc = jax.lax.conv_general_dilated(hc, conv_w, window_strides=(1,), padding='VALID', dimension_numbers=('NCH', 'OIH', 'NCH'), feature_group_count=C)
            h = jnp.transpose(hc, (0, 2, 1))
            qkv = h @ attn_w
            q, k, v = jnp.split(qkv, 3, axis=-1)
            q = q.reshape(B, T, n_head, D)
            k = k.reshape(B, T, n_head, D)
            v = v.reshape(B, T, n_head, D)
            cos, sin = _rope_tables(T, D)
            cos = cos[None, :, None, :]
            sin = sin[None, :, None, :]
            q = q * cos + _rotate_half(q) * sin
            k = k * cos + _rotate_half(k) * sin
            scores = jnp.einsum('bqhd,bkhd->bhqk', q, k) / jnp.sqrt(jnp.float32(D))
            causal = jnp.tril(jnp.ones((T, T), dtype=bool))
            scores = jnp.where(causal, scores, jnp.float32(-1e+30))
            p = jax.nn.softmax(scores, axis=-1)
            y = jnp.einsum('bhqk,bkhd->bqhd', p, v).reshape(B, T, C)
            return y @ proj_w

        def _moe(x, ln_w, ln_b, router_w, expert_wv, expert_proj):
            h = _layernorm(x, ln_w, ln_b)
            logits = h @ router_w
            expert_idx = jnp.argmax(logits, axis=-1)
            E = router_w.shape[-1]
            out = jnp.zeros_like(x)
            for e in range(E):
                gv = h @ expert_wv[e]
                gate_raw, value = jnp.split(gv, 2, axis=-1)
                y = gate_raw * jax.nn.sigmoid(gate_raw) * value @ expert_proj[e]
                out = out + jnp.where((expert_idx == e)[..., None], y, 0.0)
            return out
        C, H, E, B, T = (128, 16, 4, 4, 128)
        Dff = 4 * C
        key = jax.random.key(seed)
        ks = jax.random.split(key, 8)
        s = 0.02
        return {'x': jax.random.normal(ks[0], (B, T, C), dtype=jnp.float32), 'ln1_w': jnp.ones((C,), jnp.float32), 'ln1_b': jnp.zeros((C,), jnp.float32), 'ln2_w': jnp.ones((C,), jnp.float32), 'ln2_b': jnp.zeros((C,), jnp.float32), 'conv_w': jax.random.normal(ks[1], (C, 1, 3), dtype=jnp.float32) * 0.1, 'attn_w': jax.random.normal(ks[2], (C, 3 * C), dtype=jnp.float32) * s, 'proj_w': jax.random.normal(ks[3], (C, C), dtype=jnp.float32) * s, 'router_w': jax.random.normal(ks[4], (C, E), dtype=jnp.float32) * s, 'expert_wv': jax.random.normal(ks[5], (E, C, 2 * Dff), dtype=jnp.float32) * s, 'expert_proj': jax.random.normal(ks[6], (E, Dff, C), dtype=jnp.float32) * s}
    _L1_ffn_in = _L1_ffn_setup()
    _d = {'L0_attn_x': _L0_attn_in['x'], 'L0_attn_Wq': _L0_attn_in['Wq'], 'L0_attn_bq': _L0_attn_in['bq'], 'L0_attn_Wk': _L0_attn_in['Wk'], 'L0_attn_bk': _L0_attn_in['bk'], 'L0_attn_Wv': _L0_attn_in['Wv'], 'L0_attn_bv': _L0_attn_in['bv'], 'L0_attn_Wo': _L0_attn_in['Wo'], 'L0_attn_bo': _L0_attn_in['bo'], 'L0_attn_g1': _L0_attn_in['g1'], 'L0_attn_be1': _L0_attn_in['be1'], 'L0_attn_g2': _L0_attn_in['g2'], 'L0_attn_be2': _L0_attn_in['be2'], 'L0_attn_W1': _L0_attn_in['W1'], 'L0_attn_c1': _L0_attn_in['c1'], 'L0_attn_W2': _L0_attn_in['W2'], 'L0_attn_c2': _L0_attn_in['c2'], 'L0_attn_gf': _L0_attn_in['gf'], 'L0_attn_bef': _L0_attn_in['bef'], 'L0_ffn_gate_w': _L0_ffn_in['gate_w'], 'L0_ffn_w1': _L0_ffn_in['w1'], 'L0_ffn_b1': _L0_ffn_in['b1'], 'L0_ffn_w2': _L0_ffn_in['w2'], 'L0_ffn_b2': _L0_ffn_in['b2'], 'L1_attn_conv_w': _L1_attn_in['conv_w'], 'L1_attn_W_bc': _L1_attn_in['W_bc'], 'L1_attn_b_bc': _L1_attn_in['b_bc'], 'L1_attn_W_dt': _L1_attn_in['W_dt'], 'L1_attn_b_dt': _L1_attn_in['b_dt'], 'L1_attn_W_dtp': _L1_attn_in['W_dtp'], 'L1_attn_b_dtp': _L1_attn_in['b_dtp'], 'L1_attn_A_log': _L1_attn_in['A_log'], 'L1_attn_Dcoeff': _L1_attn_in['Dcoeff'], 'L1_ffn_ln1_w': _L1_ffn_in['ln1_w'], 'L1_ffn_ln1_b': _L1_ffn_in['ln1_b'], 'L1_ffn_ln2_w': _L1_ffn_in['ln2_w'], 'L1_ffn_ln2_b': _L1_ffn_in['ln2_b'], 'L1_ffn_conv_w': _L1_ffn_in['conv_w'], 'L1_ffn_attn_w': _L1_ffn_in['attn_w'], 'L1_ffn_proj_w': _L1_ffn_in['proj_w'], 'L1_ffn_router_w': _L1_ffn_in['router_w'], 'L1_ffn_expert_wv': _L1_ffn_in['expert_wv'], 'L1_ffn_expert_proj': _L1_ffn_in['expert_proj']}
    _x0 = _d['L0_attn_x']
    _d['L0_attn_x'] = jax.random.normal(jax.random.fold_in(jax.random.key(seed), 1), (4, 512, 128), dtype=_x0.dtype)
    del _x0
    return _d

def reference(L0_attn_x, L0_attn_Wq, L0_attn_bq, L0_attn_Wk, L0_attn_bk, L0_attn_Wv, L0_attn_bv, L0_attn_Wo, L0_attn_bo, L0_attn_g1, L0_attn_be1, L0_attn_g2, L0_attn_be2, L0_attn_W1, L0_attn_c1, L0_attn_W2, L0_attn_c2, L0_attn_gf, L0_attn_bef, L0_ffn_gate_w, L0_ffn_w1, L0_ffn_b1, L0_ffn_w2, L0_ffn_b2, L1_attn_conv_w, L1_attn_W_bc, L1_attn_b_bc, L1_attn_W_dt, L1_attn_b_dt, L1_attn_W_dtp, L1_attn_b_dtp, L1_attn_A_log, L1_attn_Dcoeff, L1_ffn_ln1_w, L1_ffn_ln1_b, L1_ffn_ln2_w, L1_ffn_ln2_b, L1_ffn_conv_w, L1_ffn_attn_w, L1_ffn_proj_w, L1_ffn_router_w, L1_ffn_expert_wv, L1_ffn_expert_proj):

    def _L0_attn_ref(x, Wq, bq, Wk, bk, Wv, bv, Wo, bo, g1, be1, g2, be2, W1, c1, W2, c2, gf, bef):
        import jax, jax.numpy as jnp
        import numpy as np
        B, S, D, H, L, F = (4, 256, 128, 16, 8, 512)
        DH = D // H

        def _ln(x, g, b):
            m = jnp.mean(x, axis=-1, keepdims=True)
            v = jnp.mean((x - m) ** 2, axis=-1, keepdims=True)
            return (x - m) * jax.lax.rsqrt(v + 1e-05) * g + b

        def _phi(t):
            return jax.nn.elu(t) + 1.0
        b, s, d = x.shape

        def layer(h, p):
            wq, bq_, wk, bk_, wv, bv_, wo, bo_, g1_, be1_, g2_, be2_, w1, c1_, w2, c2_ = p
            q = _phi((h @ wq + bq_).reshape(b, s, H, DH))
            k = _phi((h @ wk + bk_).reshape(b, s, H, DH))
            v = (h @ wv + bv_).reshape(b, s, H, DH)
            kv = jnp.einsum('bshd,bshm->bhdm', k, v)
            z = 1.0 / (jnp.einsum('bshd,bhd->bsh', q, k.sum(axis=1)) + 1e-06)
            att = jnp.einsum('bshd,bhdm,bsh->bshm', q, kv, z).reshape(b, s, d)
            h = h + att @ wo + bo_
            h = _ln(h, g1_, be1_)
            y = jax.nn.gelu(h @ w1 + c1_, approximate=False) @ w2 + c2_
            return (_ln(h + y, g2_, be2_), None)
        params = (Wq, bq, Wk, bk, Wv, bv, Wo, bo, g1, be1, g2, be2, W1, c1, W2, c2)
        h, _ = jax.lax.scan(layer, x, params)
        return _ln(h, gf, bef)

    def _L0_ffn_ref(x, gate_w, w1, b1, w2, b2):
        import jax, jax.numpy as jnp
        import numpy as np
        EMBED_DIM = 128
        HIDDEN_DIM = 512
        NUM_EXPERTS = 8
        TOP_K = 2
        orig_shape = x.shape
        xt = x.reshape(-1, EMBED_DIM)
        logits = xt @ gate_w.T
        probs = jax.nn.softmax(logits, axis=-1)
        top_w, top_i = jax.lax.top_k(probs, TOP_K)
        top_w = top_w / (top_w.sum(axis=-1, keepdims=True) + 1e-09)
        h = jnp.einsum('td,ndh->tnh', xt, w1) + b1
        h = jax.nn.gelu(h, approximate=False)
        out_all = jnp.einsum('tnh,nhd->tnd', h, w2) + b2
        sel = jnp.take_along_axis(out_all, top_i[:, :, None], axis=1)
        out = (sel * top_w[:, :, None]).sum(axis=1)
        return out.reshape(orig_shape)

    def _L1_attn_ref(x, conv_w, W_bc, b_bc, W_dt, b_dt, W_dtp, b_dtp, A_log, Dcoeff):
        import math
        import jax, jax.numpy as jnp
        import numpy as np
        B_SZ, L_SEQ, D_MODEL, N_STATE = (4, 512, 128, 16)
        DT_RANK = math.ceil(D_MODEL / 16)
        CONV_K = 3
        DT_MIN, DT_MAX = (0.001, 0.1)

        def _inverse_softplus(x):
            return x + jnp.log(1.0 - jnp.exp(-x))

        def _largest_factor_up_to(b, n):
            if n < 2:
                return n
            k = b
            while n % k != 0:
                k -= 1
            return k

        def _ssm_chunked_scan(x, A, Bc, Cc, dt):
            B, L, D = x.shape
            N = A.shape[-1]
            chunk = _largest_factor_up_to(int(math.sqrt(L)), L)
            nc = L // chunk
            r3 = lambda t, F: t.reshape(B, nc, chunk, F).transpose(1, 2, 0, 3)
            xc, dtc = (r3(x, D), r3(dt, D))
            bc, cc = (r3(Bc, N), r3(Cc, N))

            def assoc(lft, rgt):
                g_l, h_l = lft
                g_r, h_r = rgt
                return (g_l * g_r, g_r * h_l + h_r)

            def scan_chunk(carry, ch):
                g0, h0 = carry
                xk, bk, ck, dk = ch
                dA = jnp.exp(jnp.einsum('dn,lbd->lbdn', A, dk))
                dB = jnp.einsum('lbn,lbd,lbd->lbdn', bk, xk, dk)
                gs, hs = jax.lax.associative_scan(assoc, (dA, dB))
                hs = gs * h0 + hs
                yk = jnp.einsum('lbn,lbdn->lbd', ck, hs)
                return ((gs[-1:] * g0, hs[-1:]), yk)
            init = (jnp.ones((1, B, D, N), x.dtype), jnp.zeros((1, B, D, N), x.dtype))
            _, yc = jax.lax.scan(scan_chunk, init, (xc, bc, cc, dtc))
            return yc.transpose(2, 0, 1, 3).reshape(B, L, D)
        xp = jnp.pad(x, ((0, 0), (1, 1), (0, 0)))
        u = xp[:, :-2] * conv_w[0] + xp[:, 1:-1] * conv_w[1] + xp[:, 2:] * conv_w[2]
        u = jax.nn.silu(u)
        BC = u @ W_bc + b_bc
        Bcoeff, Ccoeff = jnp.split(BC, 2, axis=-1)
        A = -jnp.exp(A_log)
        dt = jax.nn.softplus((u @ W_dt + b_dt) @ W_dtp + b_dtp)
        y = _ssm_chunked_scan(x, A, Bcoeff, Ccoeff, dt)
        return y + x * Dcoeff

    def _L1_ffn_ref(x, ln1_w, ln1_b, ln2_w, ln2_b, conv_w, attn_w, proj_w, router_w, expert_wv, expert_proj):
        import jax, jax.numpy as jnp
        import numpy as np
        EPS = 1e-05

        def _layernorm(x, w, b):
            mu = jnp.mean(x, axis=-1, keepdims=True)
            var = jnp.mean((x - mu) ** 2, axis=-1, keepdims=True)
            return (x - mu) * jax.lax.rsqrt(var + EPS) * w + b

        def _rope_tables(T, D, base=10000.0):
            inv_freq = 1.0 / base ** (jnp.arange(0, D, 2, dtype=jnp.float32) / D)
            t = jnp.arange(T, dtype=jnp.float32)
            freqs = jnp.einsum('i,j->ij', t, inv_freq)
            emb = jnp.concatenate([freqs, freqs], axis=-1)
            return (jnp.cos(emb), jnp.sin(emb))

        def _rotate_half(x):
            x1, x2 = (x[..., :x.shape[-1] // 2], x[..., x.shape[-1] // 2:])
            return jnp.concatenate([-x2, x1], axis=-1)

        def _attn(x, ln_w, ln_b, conv_w, attn_w, proj_w, n_head):
            B, T, C = x.shape
            D = C // n_head
            h = _layernorm(x, ln_w, ln_b)
            hc = jnp.transpose(h, (0, 2, 1))
            hc = jnp.pad(hc, ((0, 0), (0, 0), (2, 0)))
            hc = jax.lax.conv_general_dilated(hc, conv_w, window_strides=(1,), padding='VALID', dimension_numbers=('NCH', 'OIH', 'NCH'), feature_group_count=C)
            h = jnp.transpose(hc, (0, 2, 1))
            qkv = h @ attn_w
            q, k, v = jnp.split(qkv, 3, axis=-1)
            q = q.reshape(B, T, n_head, D)
            k = k.reshape(B, T, n_head, D)
            v = v.reshape(B, T, n_head, D)
            cos, sin = _rope_tables(T, D)
            cos = cos[None, :, None, :]
            sin = sin[None, :, None, :]
            q = q * cos + _rotate_half(q) * sin
            k = k * cos + _rotate_half(k) * sin
            scores = jnp.einsum('bqhd,bkhd->bhqk', q, k) / jnp.sqrt(jnp.float32(D))
            causal = jnp.tril(jnp.ones((T, T), dtype=bool))
            scores = jnp.where(causal, scores, jnp.float32(-1e+30))
            p = jax.nn.softmax(scores, axis=-1)
            y = jnp.einsum('bhqk,bkhd->bqhd', p, v).reshape(B, T, C)
            return y @ proj_w

        def _moe(x, ln_w, ln_b, router_w, expert_wv, expert_proj):
            h = _layernorm(x, ln_w, ln_b)
            logits = h @ router_w
            expert_idx = jnp.argmax(logits, axis=-1)
            E = router_w.shape[-1]
            out = jnp.zeros_like(x)
            for e in range(E):
                gv = h @ expert_wv[e]
                gate_raw, value = jnp.split(gv, 2, axis=-1)
                y = gate_raw * jax.nn.sigmoid(gate_raw) * value @ expert_proj[e]
                out = out + jnp.where((expert_idx == e)[..., None], y, 0.0)
            return out
        n_head = 16
        x = x + _attn(x, ln1_w, ln1_b, conv_w, attn_w, proj_w, n_head)
        x = x + _moe(x, ln2_w, ln2_b, router_w, expert_wv, expert_proj)
        return x
    x = L0_attn_x
    x = x + 0.5 * _L0_ffn_ref(_layernorm(x, axis=-1), L0_ffn_gate_w, L0_ffn_w1, L0_ffn_b1, L0_ffn_w2, L0_ffn_b2)
    x = x + _L0_attn_ref(_layernorm(x, axis=-1), L0_attn_Wq, L0_attn_bq, L0_attn_Wk, L0_attn_bk, L0_attn_Wv, L0_attn_bv, L0_attn_Wo, L0_attn_bo, L0_attn_g1, L0_attn_be1, L0_attn_g2, L0_attn_be2, L0_attn_W1, L0_attn_c1, L0_attn_W2, L0_attn_c2, L0_attn_gf, L0_attn_bef)
    x = x + 0.5 * _L0_ffn_ref(_layernorm(x, axis=-1), L0_ffn_gate_w, L0_ffn_w1, L0_ffn_b1, L0_ffn_w2, L0_ffn_b2)
    x = x + 0.5 * _L1_ffn_ref(_layernorm(x, axis=-1), L1_ffn_ln1_w, L1_ffn_ln1_b, L1_ffn_ln2_w, L1_ffn_ln2_b, L1_ffn_conv_w, L1_ffn_attn_w, L1_ffn_proj_w, L1_ffn_router_w, L1_ffn_expert_wv, L1_ffn_expert_proj)
    x = x + _L1_attn_ref(_layernorm(x, axis=-1), L1_attn_conv_w, L1_attn_W_bc, L1_attn_b_bc, L1_attn_W_dt, L1_attn_b_dt, L1_attn_W_dtp, L1_attn_b_dtp, L1_attn_A_log, L1_attn_Dcoeff)
    x = x + 0.5 * _L1_ffn_ref(_layernorm(x, axis=-1), L1_ffn_ln1_w, L1_ffn_ln1_b, L1_ffn_ln2_w, L1_ffn_ln2_b, L1_ffn_conv_w, L1_ffn_attn_w, L1_ffn_proj_w, L1_ffn_router_w, L1_ffn_expert_wv, L1_ffn_expert_proj)
    return x

_drawn_inputs = setup_inputs


def setup_inputs(seed=0):
    import zlib

    import numpy as np

    out = dict(_drawn_inputs(seed))
    spreads = {'L0_attn_bq': (0.0, 0.8),
     'L0_attn_bk': (0.0, 0.8),
     'L0_attn_bv': (0.0, 0.1),
     'L0_attn_bo': (0.0, 0.1),
     'L0_attn_g1': (1.0, 0.2),
     'L0_attn_be1': (0.0, 0.1),
     'L0_attn_g2': (1.0, 0.2),
     'L0_attn_be2': (0.0, 0.1),
     'L0_attn_c1': (0.0, 0.1),
     'L0_attn_c2': (0.0, 0.1),
     'L0_attn_gf': (1.0, 0.2),
     'L0_attn_bef': (0.0, 0.1),
     'L0_ffn_b1': (0.0, 0.1),
     'L0_ffn_b2': (0.0, 0.1),
     'L1_attn_b_bc': (0.0, 0.649),
     'L1_attn_b_dt': (0.0, 0.8),
     'L1_attn_Dcoeff': (1.0, 0.2),
     'L1_ffn_ln1_w': (1.0, 0.6),
     'L1_ffn_ln1_b': (0.0, 0.8),
     'L1_ffn_ln2_w': (1.0, 0.6),
     'L1_ffn_ln2_b': (0.0, 0.8)}
    factors = {'L0_attn_Wq': 8.0,
     'L0_attn_Wk': 8.0,
     'L1_attn_W_dt': 2.813,
     'L1_attn_W_dtp': 2.907,
     'L1_attn_b_dtp': 3.153,
     'L1_attn_A_log': 2.831,
     'L1_ffn_conv_w': 8.0,
     'L1_ffn_attn_w': 8.0,
     'L1_ffn_proj_w': 8.0,
     'L1_ffn_router_w': 8.0,
     'L1_ffn_expert_wv': 8.0,
     'L1_ffn_expert_proj': 8.0}
    for name, (base, spread) in spreads.items():
        noise = np.random.default_rng([zlib.crc32(name.encode()), seed]).standard_normal(out[name].shape)
        drawn = base * np.exp(spread * noise) if base else spread * noise
        out[name] = jnp.asarray(drawn.astype(out[name].dtype))
    for name, factor in factors.items():
        out[name] = (out[name] * factor).astype(out[name].dtype)
    return out
```

```python
from contextlib import ExitStack

import numpy as np
import concourse.bass as bass
from concourse import mybir

ALU = mybir.AluOpType
ACT = mybir.ActivationFunctionType
F32 = mybir.dt.float32
BF16 = mybir.dt.bfloat16
AX_X = mybir.AxisListType.X

P = 128
NB, SEQ = 4, 512
TILES = NB * SEQ // P
TPB = SEQ // P
F = 512
FC = F // P
EXPERTS0, EXPERTS1 = 8, 4
LAYERS = 8
HEADS, DH = 16, 8
PAIRS = HEADS // 2
NSTATE, DT_RANK = 16, 8
NEG = -1e30

A_W1, A_W2, A_B1, A_B2, A_COLS = 0, 512, 1024, 1028, 1029
B_WQ, B_WKV, B_WO, B_W1, B_W2, B_KVB, B_VEC = 0, 128, 384, 512, 1024, 1536, 1792
B_BQ, B_BO, B_C1, B_C2, B_G1, B_BE1, B_G2, B_BE2, B_COLS = (B_VEC + i for i in (0, 1, 2, 6, 7, 8, 9, 10, 11))
C_WV, C_PROJ, C_COLS = 0, 1024, 1536
SLOT_COLS = B_COLS

PARAMS = [
    ("gate", EXPERTS0), ("gf", 1), ("bef", 1), ("ln1_w", 1), ("ln1_b", 1), ("ln2_w", 1), ("ln2_b", 1),
    ("conv_c", 3), ("wqkv", 3 * P), ("proj", P), ("router", EXPERTS1), ("conv_d", 3), ("w_bc", 2 * NSTATE),
    ("b_bc", 1), ("w_dt", DT_RANK), ("b_dt", 1), ("w_dtp", P), ("b_dtp", 1), ("a_log", NSTATE), ("dcoef", 1),
]
CONSTS = [("ident", P), ("mean", P), ("block", P), ("cos", TPB * DH), ("sin", TPB * DH), ("desc8", 8),
          ("desc4", 4), ("mask_qk", P), ("tri", P), ("ones", P), ("eps", 1), ("tiny", 1)]


def columns(table):
    at, out = 0, {}
    for name, n in table:
        out[name] = (at, at + n)
        at += n
    return out, at


def build(nc, x_in, pack_a, pack_b, pack_c, params, consts, out, dbg=None, stages="ABACDC"):
    par_at, par_cols = columns(PARAMS)
    con_at, con_cols = columns(CONSTS)
    with ExitStack() as ctx:
        def sb(name, shape, dt=F32):
            return ctx.enter_context(nc.sbuf_tensor(name, shape, dt))

        sems = {}

        def sem(name):
            sems[name] = ctx.enter_context(nc.semaphore(name))
            return sems[name]

        gates_dram = nc.dram_tensor("gates_dram", (4, P, P), F32, kind="Internal").ap()
        bc_dram = nc.dram_tensor("bc_dram", (2 * NSTATE, NB * SEQ), F32, kind="Internal").ap()

        par = sb("par", [P, par_cols])
        con = sb("con", [P, con_cols])
        mask_qk16 = sb("mask_qk16", [P, P], BF16)
        ident16 = sb("ident16", [P, P], BF16)
        x = sb("x", [P, NB, SEQ])
        ha = sb("ha", [P, NB, SEQ])
        hb = sb("hb", [P, NB, SEQ])
        res = sb("res", [P, NB, SEQ])
        xc = sb("xc", [P, NB, SEQ])
        sq = sb("sq", [P, NB, SEQ])
        rstd = sb("rstd", [P, NB, SEQ])
        wslot = sb("wslot", [P, 2, SLOT_COLS])
        gate_bc = sb("gate_bc", [P, 2, TILES, P])
        arena = sb("arena", [P, 17 * 1024])
        ps = ctx.enter_context(nc.psum_tensor("ps", [P, 8, 512], F32))

        def pcol(name):
            a, b = par_at[name]
            return par[:, a:b]

        def ccol(name):
            a, b = con_at[name]
            return con[:, a:b]

        def view(at, *shape):
            n = int(np.prod(shape))
            v = arena[:, at:at + n]
            if len(shape) == 1:
                return v
            names = "abcd"[:len(shape)]
            return v.rearrange(f"p ({' '.join(names)}) -> p {' '.join(names)}",
                               **{k: s for k, s in zip(names[1:], shape[1:])})

        def view16(at, *shape):
            n = int(np.prod(shape))
            names = "abcd"[:len(shape)]
            return arena[:, at:at + n // 2].bitcast(BF16).rearrange(
                f"p ({' '.join(names)}) -> p {' '.join(names)}", **{k: s for k, s in zip(names[1:], shape[1:])})

        ident, mean_w, block = ccol("ident"), ccol("mean"), ccol("block")
        eps, tiny = ccol("eps"), ccol("tiny")

        hid = view(0, 2, FC, SEQ)
        gated = view(4096, 2, SEQ)
        silu = view(5120, 2, SEQ)
        rt = [view(8192 + 128 * i, TILES, 8) for i in range(8)]
        rs = [view(8192 + 1024 + 16 * i, TILES) for i in range(8)]
        gate_t = view(8192 + 1536, P)
        q_exp, q_relu = view(0, NB, SEQ), view(2048, NB, SEQ)
        qf = view(4096, NB, SEQ)
        kf = view(6144, NB, TPB, P)
        v_aug = view(8192, NB, TPB, P + 1)
        kv_bd, ks_bd = view(10368, NB, P), view(10880, NB, P)
        hid_b = view(11392, 2, FC, SEQ)
        k_exp, k_relu = view(0, NB, TPB, P), view(2048, NB, TPB, P)
        den, att = view(0, NB, SEQ), view(2048, NB, SEQ)
        hc = view(0, SEQ)
        qk16 = view16(512, TPB, 2 * HEADS, 64)
        vc = view(4608, TPB, HEADS, DH + 1)
        kt_s, qt_s, q2_s = view16(5184, PAIRS, SEQ), view16(7232, PAIRS, SEQ), view16(9280, PAIRS, SEQ)
        NPT = 4
        pt = view(11328, NPT, 2, SEQ)
        rope1, rope2 = view(15424, 2, 2 * HEADS, DH), view(15936, 2, 2 * HEADS, DH)
        rden = view(16448, TPB, HEADS)
        neg_max = view(16448, TPB, HEADS)
        y_tok = view(16512, TPB, HEADS, DH)
        y_t = view(15424, SEQ)
        dt_s, dtx = xc, sq
        da = view(0, 2, NB, SEQ)
        db = view(4096, 2, NB, SEQ)
        hst = view(8192, 2, NB, SEQ)
        ch = view(12288, 2, NB, SEQ)
        bc_row = sb("bc_row", [1, 2, 2, NB, SEQ])
        bc_s = view(0, NB, SEQ)[0:2 * NSTATE]
        t1_s = view(2048, NB, SEQ)[0:DT_RANK]
        soft_a, soft_e, soft_l, soft_r = view(4096, NB, SEQ), view(6144, NB, SEQ), view(8192, NB, SEQ), view(10240, NB, SEQ)
        a_neg = view(16384, NSTATE)
        diag_d = view(16400, P)

        names = """params_in x_in w_in0 w_in1 gates_out gate_in0 gate_in1 x_out bc_out bc_in0 bc_in1
            x_tr x_cp consts16 ln_mean ln_xc ln_sq ln_var ln_log ln_rs ln_scaled ln_out
            logits lg_sub lg_exp gate_ok gate_tr gate_cp dve_chain
            up_mm hid_ok down_mm gated_ok added gv_mm silu_ok
            q_mm q_act qf_ok kv_mm kv_ok k_act kf_ok kvs_mm kvbd_ok att_mm den_ok rz_ok att_ok o_mm res1_ok
            ff1_mm gelu_ok ff2_mm res2_ok x_ok
            hc_ok qkv_mm rope_mid rope_ok part1_ok rest_ok part2_ok split_ok k_tr q_tr kt_ok qt_ok m1_ok m_ok sel_ok s1_mm s1_max q2_tr q2_ok s2_mm exp_ok pv_mm
            rden_ok y_ok y_tr yt_ok proj_mm x1_ok pad_ok
            conv_ok u_ok bc_mm bc_ok t1_mm t1_ok z_mm z_act soft_u soft_log dt_ok dtx_ok a_exp a_ok diag_ok
            bb_mm cb_mm da_ok db_ok scan_ok ch_ok sum_mm tr_out cp_out""".split()
        S = {n: sem(n) for n in names}

        order = []
        count = dict(ln=0, lns=0, x_upd=0, moe=0, added=0, moe1=0, moe_call=0, w=0, g=0, up=0, hid=0, down=0,
                     gv=0, attn=0, ffn1=0)
        for kind in stages:
            order.append((kind, dict(count)))
            if kind == "A":
                count["ln"] += 1
                count["moe_call"] += 1
                count["w"] += EXPERTS0
                count["g"] += EXPERTS0
                count["added"] += NB * EXPERTS0
                count["up"] += NB * EXPERTS0
            elif kind == "B":
                count["ln"] += 2 + 2 * LAYERS
                count["lns"] += 1 + 2 * LAYERS
                count["w"] += LAYERS
                count["x_upd"] += 1
            elif kind == "C":
                count["ln"] += 3
                count["lns"] += 2
                count["moe_call"] += 1
                count["w"] += EXPERTS1
                count["g"] += EXPERTS1
                count["added"] += NB * EXPERTS1
                count["moe1"] += NB * EXPERTS1
                count["attn"] += 1
                count["x_upd"] += 1
            elif kind == "D":
                count["ln"] += 1
                count["x_upd"] += 1

        def pe_ln(pe, n, src, ready):
            for t in range(NB):
                ready(pe, t)
                pe.matmul(ps[:, t, :], mean_w, src[:, t, :], start=True, stop=True).then_inc(S["ln_mean"], 1)
            for t in range(NB):
                pe.wait_ge(S["ln_sq"], 4 * n + t + 1)
                pe.matmul(ps[:, 4 + t, :], mean_w, sq[:, t, :], start=True, stop=True).then_inc(S["ln_var"], 1)

        def act_ln(act, n):
            for t in range(NB):
                act.wait_ge(S["ln_xc"], 4 * n + t + 1)
                act.activation(sq[:, t, :], xc[:, t, :], ACT.Square).then_inc(S["ln_sq"], 1)
            for t in range(NB):
                act.wait_ge(S["ln_var"], 4 * n + t + 1)
                act.activation(rstd[:, t, :], ps[:, 4 + t, :], ACT.Ln, bias=eps).then_inc(S["ln_log"], 1)
            for t in range(NB):
                act.wait_ge(S["ln_log"], 4 * n + t + 1)
                act.activation(rstd[:, t, :], rstd[:, t, :], ACT.Exp, scale=-0.5).then_inc(S["ln_rs"], 1)

        def dve_ln(dve, n, src, dst, affine=None):
            for t in range(NB):
                dve.wait_ge(S["ln_mean"], 4 * n + t + 1)
                dve.tensor_tensor(xc[:, t, :], src[:, t, :], ps[:, t, :], ALU.subtract).then_inc(S["ln_xc"], 1)
            for t in range(NB):
                dve.wait_ge(S["ln_rs"], 4 * n + t + 1)
                if affine is None:
                    dve.tensor_tensor(dst[:, t, :], xc[:, t, :], rstd[:, t, :], ALU.mult).then_inc(S["ln_out"], 1)
                else:
                    m, g, b = affine
                    dve.scalar_tensor_tensor(out=dst[:, t, :], in0=xc[:, t, :], scalar=g, in1=rstd[:, t, :],
                                             op0=ALU.mult, op1=ALU.mult).then_inc(S["ln_scaled"], 1)
            if affine is not None:
                for t in range(NB):
                    dve.wait_ge(S["ln_scaled"], 4 * m + t + 1)
                    dve.tensor_scalar(dst[:, t, :], dst[:, t, :], b, None, ALU.add).then_inc(S["ln_out"], 1)

        def x_ready(c):
            def wait(pe, t):
                if c["x_upd"] == 0:
                    pe.wait_ge(S["x_cp"], 4)
                else:
                    pe.wait_ge(S["x_ok"], 4 * c["x_upd"] - 4 + t + 1)
            return wait

        def pe_router(pe, n, call, w, experts):
            pe.wait_ge(S["ln_out"], 4 * n + 4)
            for i in range(TILES):
                mm = pe.matmul(ps[:, 0, experts * i:experts * (i + 1)],
                               ha[:, i // TPB, (i % TPB) * P:(i % TPB + 1) * P], w, start=True, stop=True)
            mm.then_inc(S["logits"], 1)
            pe.wait_ge(S["gate_ok"], call + 1)
            pe.transpose(ps[0:TILES * experts, 1, 0:P], gates_view(experts), ident).then_inc(S["gate_tr"], 1)

        def gates_view(experts):
            return arena[:, 8192 + 128 * 7:8192 + 128 * 7 + TILES * experts]

        def act_router(act, call):
            if call is not None:
                act.wait_ge(S["lg_sub"], call + 1)
                act.activation(rt[1], rt[0], ACT.Exp).then_inc(S["lg_exp"], 1)

        chain = [0]

        def dve_router(dve, call, exp_call, experts, top):
            def link(ins):
                chain[0] += 1
                ins.then_inc(S["dve_chain"], 1)
                dve.wait_ge(S["dve_chain"], chain[0])

            def bc(v):
                return v.unsqueeze(2).to_broadcast([P, TILES, experts])

            def tile3(i):
                return arena[:, 8192 + 128 * i:8192 + 128 * i + TILES * experts].rearrange("p (t e) -> p t e", e=experts)

            desc = ccol("desc8" if experts == 8 else "desc4").unsqueeze(1).to_broadcast([P, TILES, experts])
            dve.wait_ge(S["logits"], call + 1)
            lg = ps[:, 0, 0:TILES * experts].rearrange("p (t e) -> p t e", e=experts)
            val = tile3(0)
            if top == 2:
                link(dve.tensor_reduce(rs[0], lg, AX_X, ALU.max))
                dve.tensor_tensor(val, lg, bc(rs[0]), ALU.subtract).then_inc(S["lg_sub"], 1)
                dve.wait_ge(S["lg_exp"], exp_call + 1)
                e = tile3(1)
                link(dve.tensor_reduce(rs[0], e, AX_X, ALU.add))
                link(dve.reciprocal(rs[0], rs[0]))
                link(dve.tensor_tensor(val, e, bc(rs[0]), ALU.mult))
            else:
                link(dve.tensor_copy(val, lg))

            def first_max(src, best, hot):
                link(dve.tensor_reduce(best, src, AX_X, ALU.max))
                link(dve.tensor_tensor(tile3(3), src, bc(best), ALU.is_equal))
                link(dve.tensor_tensor(tile3(3), tile3(3), desc, ALU.mult))
                link(dve.tensor_reduce(rs[3], tile3(3), AX_X, ALU.max))
                link(dve.tensor_tensor(hot, tile3(3), bc(rs[3]), ALU.is_equal))

            first_max(val, rs[1], tile3(4))
            out_g = tile3(7)
            if top == 1:
                dve.tensor_copy(out_g, tile3(4)).then_inc(S["gate_ok"], 1)
            else:
                link(dve.scalar_tensor_tensor(out=tile3(5), in0=tile3(4), scalar=-2.0, in1=val, op0=ALU.mult, op1=ALU.add))
                first_max(tile3(5), rs[2], tile3(6))
                link(dve.tensor_tensor(tile3(4), tile3(4), tile3(6), ALU.add))
                link(dve.tensor_tensor(tile3(4), tile3(4), val, ALU.mult))
                link(dve.tensor_tensor(rs[4], rs[1], rs[2], ALU.add))
                link(dve.tensor_scalar(rs[4], rs[4], 1e-9, None, ALU.add))
                link(dve.reciprocal(rs[4], rs[4]))
                dve.scalar_tensor_tensor(out=out_g, in0=tile3(4), scalar=0.5, in1=bc(rs[4]),
                                         op0=ALU.mult, op1=ALU.mult).then_inc(S["gate_ok"], 1)
            dve.wait_ge(S["gate_tr"], call + 1)
            dve.tensor_copy(gate_t[0:TILES * experts], ps[0:TILES * experts, 1, 0:P]).then_inc(S["gate_cp"], 1)

        def sp_gates(sp, call, experts):
            sp.wait_ge(S["gate_cp"], call + 1)
            sp.dma_start(gates_dram[call, 0:TILES * experts, :], gate_t[0:TILES * experts]).then_inc(S["gates_out"], 16)
            sp.wait_ge(S["gates_out"], 16 * call + 16)

        def gate_src(call, experts, r, s):
            rows = gates_dram[call, 0:TILES * experts, :].rearrange("(t r s) p -> s r t p", r=experts // 2, s=2)
            return rows[s, r].partition_broadcast(P)


        ITEMS = [(s, t) for s in range(2) for t in range(NB)]

        def sp_moe(sp, c, pack, cols, experts, slot_free):
            pairs = pack.rearrange("(r s) p n -> s r p n", s=2)
            for s in range(2):
                slot_free(sp, s)
                sp.dma_start(wslot[:, s, 0:cols], pack[s]).then_inc(S[f"w_in{s}"], 16)
            sp_gates(sp, c["moe_call"], experts)
            for s in range(2):
                sp.dma_start(gate_bc[:, s], gate_src(c["moe_call"], experts, 0, s)).then_inc(S[f"gate_in{s}"], 16)
            with sp.Fori(1, experts // 2) as r:
                e = 2 * r
                for s in range(2):
                    sp.wait_ge(S["gated_ok"], c["added"] + 4 * e + 4 * (s - 1))
                    sp.dma_start(wslot[:, s, 0:cols], pairs[s, r]).then_inc(S[f"w_in{s}"], 16)
                    sp.dma_start(gate_bc[:, s], gate_src(c["moe_call"], experts, r, s)).then_inc(S[f"gate_in{s}"], 16)

        def w_count(c, e):
            return 8 * c["w"] + 8 * e + 16

        def pe_down(pe, c, e, item, at):
            s, t = ITEMS[item]
            base = c["added"] + 4 * e
            if item >= 4:
                pe.wait_ge(S["gated_ok"], base + item - 4 + 1)
            elif item == 3:
                pe.wait_ge(S["gated_ok"], base + 1)
            for k in range(FC):
                pe.wait_ge(S["hid_ok"], 4 * base + 4 * item + k + 1)
                mm = pe.matmul(ps[:, 4 + item % 4, :], wslot[:, s, at + k * P:at + (k + 1) * P],
                               hid[:, item % 2, k, :], start=(k == 0), stop=(k == FC - 1))
            mm.then_inc(S["down_mm"], 1)

        def pe_experts0(pe, c):
            with pe.Fori(0, EXPERTS0 // 2) as r:
                e = 2 * r
                hid0 = 4 * (c["added"] + 4 * e)

                def up(item):
                    s, t = ITEMS[item]
                    if t == 0:
                        pe.wait_ge(S[f"w_in{s}"], w_count(c, e))
                    for k in range(FC):
                        if item:
                            pe.wait_ge(S["hid_ok"], hid0 + 4 * (item - 1) + k + 1)
                        pe.matmul(ps[:, k, :], wslot[:, s, A_W1 + k * P:A_W1 + (k + 1) * P], ha[:, t, :],
                                  start=True, stop=True).then_inc(S["up_mm"], 1)

                up(0)
                for item in range(1, 8):
                    up(item)
                    pe_down(pe, c, e, item - 1, A_W2)
                pe_down(pe, c, e, 7, A_W2)
                pe.wait_ge(S["gated_ok"], c["added"] + 4 * e + 7)

        def act_experts0(act, c):
            with act.Fori(0, EXPERTS0 // 2) as r:
                e = 2 * r
                for item, (s, t) in enumerate(ITEMS):
                    for k in range(FC):
                        act.wait_ge(S["up_mm"], 4 * (c["up"] + 4 * e + item) + k + 1)
                        act.activation(hid[:, item % 2, k, :], ps[:, k, :], ACT.Gelu,
                                       bias=wslot[:, s, A_B1 + k:A_B1 + k + 1]).then_inc(S["hid_ok"], 1)

        def dve_gate(dve, c, e, item, bias, dst):
            s, t = ITEMS[item]
            if t == 0:
                dve.wait_ge(S[f"gate_in{s}"], 8 * c["g"] + 8 * e + 16)
            g = gate_bc[:, s, TPB * t:TPB * t + TPB, :].rearrange("p a b -> p (a b)")
            dve.wait_ge(S["down_mm"], c["added"] + 4 * e + item + 1)
            if bias:
                ins = dve.scalar_tensor_tensor(out=gated[:, item % 2, :], in0=ps[:, 4 + item % 4, :],
                                               scalar=wslot[:, s, A_B2:A_B2 + 1], in1=g, op0=ALU.add, op1=ALU.mult)
            else:
                ins = dve.tensor_tensor(gated[:, item % 2, :], ps[:, 4 + item % 4, :], g, ALU.mult)
            ins.then_inc(S["gated_ok"], 1)
            dve.wait_ge(S["gated_ok"], c["added"] + 4 * e + item + 1)
            dve.tensor_tensor(dst[:, t, :], dst[:, t, :], gated[:, item % 2, :], ALU.add).then_inc(S["added"], 1)

        def pe_experts1(pe, c):
            with pe.Fori(0, EXPERTS1 // 2) as r:
                e = 2 * r
                hid0 = 4 * (c["added"] + 4 * e)

                def up(item):
                    s, t = ITEMS[item]
                    if t == 0:
                        pe.wait_ge(S[f"w_in{s}"], w_count(c, e))
                    for k in range(FC):
                        if 4 * item + k >= 2:
                            pe.wait_ge(S["hid_ok"], hid0 + 4 * item + k - 2 + 1)
                        bank = 2 * (k % 2)
                        pe.matmul(ps[:, bank, :], wslot[:, s, C_WV + k * P:C_WV + (k + 1) * P], ha[:, t, :],
                                  start=True, stop=True)
                        pe.matmul(ps[:, bank + 1, :], wslot[:, s, C_WV + F + k * P:C_WV + F + (k + 1) * P],
                                  ha[:, t, :], start=True, stop=True).then_inc(S["gv_mm"], 1)

                up(0)
                for item in range(1, 8):
                    up(item)
                    pe_down(pe, c, e, item - 1, C_PROJ)
                pe_down(pe, c, e, 7, C_PROJ)
                pe.wait_ge(S["gated_ok"], c["added"] + 4 * e + 7)

        def act_experts1(act, c):
            with act.Fori(0, EXPERTS1 // 2) as r:
                e = 2 * r
                for item in range(8):
                    for k in range(FC):
                        act.wait_ge(S["gv_mm"], 4 * (c["moe1"] + 4 * e + item) + k + 1)
                        act.activation(silu[:, k % 2, :], ps[:, 2 * (k % 2), :], ACT.Silu).then_inc(S["silu_ok"], 1)

        def dve_experts1(dve, c, dst):
            with dve.Fori(0, EXPERTS1 // 2) as r:
                e = 2 * r
                def hidden(item):
                    for k in range(FC):
                        dve.wait_ge(S["silu_ok"], 4 * (c["moe1"] + 4 * e + item) + k + 1)
                        dve.tensor_tensor(hid[:, item % 2, k, :], silu[:, k % 2, :], ps[:, 2 * (k % 2) + 1, :],
                                          ALU.mult).then_inc(S["hid_ok"], 1)

                hidden(0)
                for item in range(1, 8):
                    hidden(item)
                    dve_gate(dve, c, e, item - 1, False, dst)
                dve_gate(dve, c, e, 7, False, dst)

        def dve_experts0(dve, c, dst):
            with dve.Fori(0, EXPERTS0 // 2) as r:
                e = 2 * r
                for item in range(8):
                    dve_gate(dve, c, e, item, True, dst)

        def pe_layers(pe, c):
            n0 = c["ln"] + 1
            with pe.Fori(0, LAYERS // 2) as r:
                l = 2 * r
                for s in range(2):
                    m = 4 * (l + s)
                    w = wslot[:, s, :]
                    nd = n0 + 2 * (l + s)
                    pe.wait_ge(S[f"w_in{s}"], w_count(c, l))
                    for b in range(NB):
                        pe.wait_ge(S["ln_out"], 4 * nd - 4 + b + 1)
                        pe.matmul(ps[:, b, :], w[:, B_WQ:B_WQ + P], ha[:, b, :], start=True,
                                  stop=True).then_inc(S["q_mm"], 1)
                    for b in range(NB):
                        bank = 4 + 2 * (b % 2)
                        if b >= 2:
                            pe.wait_ge(S["kv_ok"], m + b - 2 + 1)
                        for i in range(TPB):
                            mm = pe.matmul(ps[:, bank + i // 2, 256 * (i % 2):256 * (i % 2) + 256],
                                           ha[:, b, i * P:(i + 1) * P], w[:, B_WKV:B_WKV + 2 * P],
                                           start=True, stop=True)
                        mm.then_inc(S["kv_mm"], 1)
                    for b in range(NB):
                        pe.wait_ge(S["kf_ok"], m + b + 1)
                        pe.wait_ge(S["qf_ok"], m + b + 1)
                        for i in range(TPB):
                            mm = pe.matmul(ps[:, b, 0:P + 1], kf[:, b, i, :], v_aug[:, b, i, :],
                                           start=(i == 0), stop=(i == TPB - 1))
                        mm.then_inc(S["kvs_mm"], 1)
                    for b in range(NB):
                        bank = 4 + 2 * (b % 2)
                        pe.wait_ge(S["kvbd_ok"], m + b + 1)
                        if b >= 2:
                            pe.wait_ge(S["att_ok"], m + b - 2 + 1)
                        pe.matmul(ps[:, bank, :], kv_bd[:, b, :], qf[:, b, :], start=True, stop=True)
                        pe.matmul(ps[:, bank + 1, :], ks_bd[:, b, :], qf[:, b, :], start=True,
                                  stop=True).then_inc(S["att_mm"], 1)
                    for b in range(NB):
                        pe.wait_ge(S["att_ok"], m + b + 1)
                        pe.matmul(ps[:, b, :], w[:, B_WO:B_WO + P], att[:, b, :], start=True,
                                  stop=True).then_inc(S["o_mm"], 1)
                    pe_ln(pe, nd, res, lambda pe, t: pe.wait_ge(S["res1_ok"], m + t + 1))

                    def ff1(b):
                        pe.wait_ge(S["ln_out"], 4 * nd + b + 1)
                        for k in range(FC):
                            if b:
                                pe.wait_ge(S["gelu_ok"], 4 * m + 4 * (b - 1) + k + 1)
                            pe.matmul(ps[:, k, :], w[:, B_W1 + k * P:B_W1 + (k + 1) * P], hb[:, b, :],
                                      start=True, stop=True).then_inc(S["ff1_mm"], 1)

                    def ff2(b):
                        pe.wait_ge(S["ln_rs"], 4 * nd + b + 1)
                        for k in range(FC):
                            pe.wait_ge(S["gelu_ok"], 4 * m + 4 * b + k + 1)
                            mm = pe.matmul(ps[:, 4 + b, :], w[:, B_W2 + k * P:B_W2 + (k + 1) * P],
                                           hid_b[:, b % 2, k, :], start=(k == 0), stop=(k == FC - 1))
                        mm.then_inc(S["ff2_mm"], 1)

                    ff1(0)
                    for b in range(1, NB):
                        ff1(b)
                        ff2(b - 1)
                    ff2(NB - 1)
                    pe_ln(pe, nd + 1, res, lambda pe, t: pe.wait_ge(S["res2_ok"], m + t + 1))

        def act_layers(act, c):
            n0 = c["ln"] + 1
            with act.Fori(0, LAYERS // 2) as r:
                l = 2 * r
                for s in range(2):
                    m = 4 * (l + s)
                    w = wslot[:, s, :]
                    nd = n0 + 2 * (l + s)
                    for b in range(NB):
                        act.wait_ge(S["q_mm"], m + b + 1)
                        act.activation(q_exp[:, b, :], ps[:, b, :], ACT.Exp, bias=w[:, B_BQ:B_BQ + 1])
                        act.activation(q_relu[:, b, :], ps[:, b, :], ACT.Relu,
                                       bias=w[:, B_BQ:B_BQ + 1]).then_inc(S["q_act"], 1)
                    for b in range(NB):
                        act.wait_ge(S["kv_ok"], m + b + 1)
                        act.activation(k_exp[:, b], kf[:, b], ACT.Exp)
                        act.activation(k_relu[:, b], kf[:, b], ACT.Relu).then_inc(S["k_act"], 1)
                    for b in range(NB):
                        act.wait_ge(S["att_mm"], m + b + 1)
                        act.activation(den[:, b, :], ps[:, 5 + 2 * (b % 2), :], ACT.Identity,
                                       bias=tiny).then_inc(S["den_ok"], 1)
                    act_ln(act, nd)
                    for b in range(NB):
                        for k in range(FC):
                            act.wait_ge(S["ff1_mm"], 4 * m + 4 * b + k + 1)
                            act.activation(hid_b[:, b % 2, k, :], ps[:, k, :], ACT.Gelu,
                                           bias=w[:, B_C1 + k:B_C1 + k + 1]).then_inc(S["gelu_ok"], 1)
                    act_ln(act, nd + 1)

        def dve_layers(dve, c):
            n0, m0 = c["ln"] + 1, c["lns"]
            with dve.Fori(0, LAYERS // 2) as r:
                l = 2 * r
                for s in range(2):
                    m = 4 * (l + s)
                    w = wslot[:, s, :]
                    nd, na = n0 + 2 * (l + s), m0 + 2 * (l + s)
                    for b in range(NB):
                        dve.wait_ge(S["q_act"], m + b + 1)
                        dve.scalar_tensor_tensor(out=qf[:, b, :], in0=q_exp[:, b, :], scalar=1.0,
                                                 in1=q_relu[:, b, :], op0=ALU.min, op1=ALU.add).then_inc(S["qf_ok"], 1)
                    bias = w[:, B_KVB:B_KVB + 2 * P].unsqueeze(1).to_broadcast([P, 4, 2 * P])
                    for b in range(NB):
                        bank = 4 + 2 * (b % 2)
                        kv = ps[:, bank:bank + 2, :].rearrange("p a (i n) -> p (a i) n", i=2)
                        dve.wait_ge(S["kv_mm"], m + b + 1)
                        dve.tensor_tensor(kf[:, b], kv[:, :, 0:P], bias[:, :, 0:P], ALU.add)
                        dve.tensor_tensor(v_aug[:, b, :, 0:P], kv[:, :, P:2 * P], bias[:, :, P:2 * P],
                                          ALU.add).then_inc(S["kv_ok"], 1)
                    for b in range(NB):
                        dve.wait_ge(S["k_act"], m + b + 1)
                        dve.scalar_tensor_tensor(out=kf[:, b], in0=k_exp[:, b], scalar=1.0, in1=k_relu[:, b],
                                                 op0=ALU.min, op1=ALU.add).then_inc(S["kf_ok"], 1)
                    for b in range(NB):
                        dve.wait_ge(S["kvs_mm"], m + b + 1)
                        dve.tensor_tensor(kv_bd[:, b, :], ps[:, b, 0:P], block, ALU.mult)
                        dve.tensor_scalar(ks_bd[:, b, :], block, ps[:, b, P:P + 1], None,
                                          ALU.mult).then_inc(S["kvbd_ok"], 1)
                    for b in range(NB):
                        dve.wait_ge(S["den_ok"], m + b + 1)
                        dve.reciprocal(den[:, b, :], den[:, b, :]).then_inc(S["rz_ok"], 1)
                        dve.wait_ge(S["rz_ok"], m + b + 1)
                        dve.tensor_tensor(att[:, b, :], ps[:, 4 + 2 * (b % 2), :], den[:, b, :],
                                          ALU.mult).then_inc(S["att_ok"], 1)
                    for b in range(NB):
                        dve.wait_ge(S["o_mm"], m + b + 1)
                        dve.scalar_tensor_tensor(out=res[:, b, :], in0=ps[:, b, :], scalar=w[:, B_BO:B_BO + 1],
                                                 in1=ha[:, b, :], op0=ALU.add, op1=ALU.add).then_inc(S["res1_ok"], 1)
                    dve_ln(dve, nd, res, hb, (na, w[:, B_G1:B_G1 + 1], w[:, B_BE1:B_BE1 + 1]))
                    for b in range(NB):
                        dve.wait_ge(S["ff2_mm"], m + b + 1)
                        dve.scalar_tensor_tensor(out=res[:, b, :], in0=ps[:, 4 + b, :], scalar=w[:, B_C2:B_C2 + 1],
                                                 in1=hb[:, b, :], op0=ALU.add, op1=ALU.add).then_inc(S["res2_ok"], 1)
                    dve_ln(dve, nd + 1, res, ha, (na + 1, w[:, B_G2:B_G2 + 1], w[:, B_BE2:B_BE2 + 1]))

        def sp_layers(sp, c, slot_free):
            pairs = pack_b.rearrange("(r s) p n -> s r p n", s=2)
            n0 = c["ln"] + 1
            for s in range(2):
                slot_free(sp, s)
                sp.dma_start(wslot[:, s, 0:B_COLS], pack_b[s]).then_inc(S[f"w_in{s}"], 16)
            with sp.Fori(1, LAYERS // 2) as r:
                l = 2 * r
                for s in range(2):
                    sp.wait_ge(S["ln_out"], 4 * (n0 + 2 * (l + s) - 4) + 8)
                    sp.dma_start(wslot[:, s, 0:B_COLS], pairs[s, r]).then_inc(S[f"w_in{s}"], 16)

        SCALE = DH ** -0.5
        QROWS = 6 * DH
        MROWS = QROWS + 2
        UNITS = [(i, hp) for i in range(TPB) for hp in range(PAIRS)]
        PV_LAG = 3

        def pe_attention(pe, c):
            pe.wait_ge(S["pad_ok"], 2 * c["attn"] + 2)
            with pe.Fori(0, NB) as b:
                q = 4 * c["attn"] + b
                pe.wait_ge(S["hc_ok"], q + 1)
                for i in range(TPB):
                    pe.matmul(ps[:, i, 0:3 * P], hc[:, i * P:(i + 1) * P], pcol("wqkv"), start=True,
                              stop=True).then_inc(S["qkv_mm"], 1)

                def turned(i, kind, bank):
                    to = ps[:, bank, :].bitcast(BF16)
                    for hp in range(PAIRS):
                        at = qk16[:, i, kind * HEADS + 2 * hp:kind * HEADS + 2 * hp + 2, :].rearrange("p h d -> p (h d)")
                        mm = pe.transpose(to[:, hp * P:(hp + 1) * P], at, ident16[:, :])
                    return mm

                for i in range(TPB):
                    pe.wait_ge(S["split_ok"], 4 * q + i + 1)
                    turned(i, 1, 4 + i).then_inc(S["k_tr"], 1)
                    turned(i, 0, i).then_inc(S["q_tr"], 1)
                pe.wait_ge(S["kt_ok"], 4 * q + 4)
                pe.wait_ge(S["qt_ok"], 4 * q + 4)
                for u, (i, hp) in enumerate(UNITS):
                    if u >= 3:
                        pe.wait_ge(S["s1_max"], 32 * q + u - 3 + 1)
                    for jj in range(2):
                        r0 = 64 * jj
                        pe.matmul(ps[:, 2 * (u % 3) + jj, 0:(i + 1) * P], qt_s[r0:r0 + QROWS, hp, i * P:(i + 1) * P],
                                  kt_s[r0:r0 + QROWS, hp, 0:(i + 1) * P], start=True, stop=False)
                    for jj in range(2):
                        mm = pe.matmul(ps[:, 2 * (u % 3) + jj, i * P:(i + 1) * P], ident16[:, :], mask_qk16[:, :],
                                       start=False, stop=True)
                    mm.then_inc(S["s1_mm"], 1)
                for i in range(TPB):
                    pe.wait_ge(S["m_ok"], 4 * q + i + 1)
                    if i >= 2:
                        pe.wait_ge(S["q2_ok"], 4 * q + i - 2 + 1)
                    turned(i, 0, 6 + i % 2).then_inc(S["q2_tr"], 1)

                def scores(u):
                    k, hp = UNITS[u]
                    n = SEQ - k * P
                    if u == 0:
                        pe.wait_ge(S["q2_ok"], 4 * q + 4)
                    for jj in range(2):
                        r0 = 64 * jj
                        mm = pe.matmul(ps[:, 2 * (u % 3) + jj, 0:n], kt_s[r0:r0 + MROWS, hp, k * P:(k + 1) * P],
                                       q2_s[r0:r0 + MROWS, hp, k * P:SEQ], start=True, stop=True)
                    mm.then_inc(S["s2_mm"], 1)

                def values(u):
                    k, hp = UNITS[u]
                    pe.wait_ge(S["sel_ok"], 32 * q + u + 1)
                    for jj in range(2):
                        h = 2 * hp + jj
                        for i in range(k, TPB):
                            at = (i % 2) * HEADS * (DH + 1) + h * (DH + 1)
                            mm = pe.matmul(ps[:, 6 + i // 2, at:at + DH + 1],
                                           pt[:, u % NPT, jj, (i - k) * P:(i - k + 1) * P], vc[:, k, h, :],
                                           start=(u == 0 and jj == 0 and i % 2 == 0), stop=(k == i),
                                           skip_group_check=True)
                    mm.then_inc(S["pv_mm"], 1)

                for u in range(32):
                    if u >= 3:
                        pe.wait_ge(S["exp_ok"], 32 * q + u - 3 + 1)
                    scores(u)
                    if u >= PV_LAG:
                        values(u - PV_LAG)
                for u in range(32 - PV_LAG, 32):
                    values(u)
                pe.wait_ge(S["y_ok"], q + 1)
                for i in range(TPB):
                    mm = pe.transpose(ps[:, 0, i * P:(i + 1) * P], y_tok[:, i].rearrange("p h d -> p (h d)"), ident)
                mm.then_inc(S["y_tr"], 1)
                pe.wait_ge(S["yt_ok"], q + 1)
                pe.matmul(ps[:, 1, :], pcol("proj"), y_t, start=True, stop=True).then_inc(S["proj_mm"], 1)

        def act_attention(act, c):
            with act.Fori(0, NB) as b:
                q = 4 * c["attn"] + b

                def part(i, which, src):
                    qs, ks = qk16[:, i, 0:HEADS, :], qk16[:, i, HEADS:2 * HEADS, :]
                    n, first = (3, 0) if which == 1 else (2, 3)
                    act.activation(qs[:, :, first * DH:(first + n) * DH].rearrange("p h (r d) -> p h r d", d=DH),
                                   src[:, 0:HEADS, :].unsqueeze(2).to_broadcast([P, HEADS, n, DH]), ACT.Copy)
                    at = (which - 1) * DH
                    ins = act.activation(ks[:, :, at:at + 6 * DH].rearrange("p h (r d) -> p h r d", d=3 * DH)[:, :, :, 0:DH],
                                         src[:, HEADS:2 * HEADS, :].unsqueeze(2).to_broadcast([P, HEADS, 2, DH]), ACT.Copy)
                    if which == 1:
                        ins = act.activation(ks[:, :, 5 * DH:6 * DH], src[:, HEADS:2 * HEADS, :], ACT.Copy)
                    return ins

                for i in range(TPB):
                    act.wait_ge(S["rope_ok"], 4 * q + i + 1)
                    part(i, 1, rope1[:, i % 2]).then_inc(S["part1_ok"], 1)
                    act.wait_ge(S["rest_ok"], 4 * q + i + 1)
                    part(i, 2, rope2[:, i % 2]).then_inc(S["part2_ok"], 1)
                for i in range(TPB):
                    act.wait_ge(S["k_tr"], 4 * q + i + 1)
                    act.activation(kt_s[:, :, i * P:(i + 1) * P],
                                   ps[:, 4 + i, :].bitcast(BF16).rearrange("p (a n) -> p a n", n=P),
                                   ACT.Copy).then_inc(S["kt_ok"], 1)
                for i in range(TPB):
                    act.wait_ge(S["q2_tr"], 4 * q + i + 1)
                    act.activation(q2_s[:, :, i * P:(i + 1) * P],
                                   ps[:, 6 + i % 2, :].bitcast(BF16).rearrange("p (a n) -> p a n", n=P),
                                   ACT.Copy).then_inc(S["q2_ok"], 1)
                for u, (k, hp) in enumerate(UNITS):
                    n = SEQ - k * P
                    act.wait_ge(S["s2_mm"], 32 * q + u + 1)
                    if u >= NPT:
                        act.wait_ge(S["pv_mm"], 32 * q + u - NPT + 1)
                    act.activation(pt[:, u % NPT, :, 0:n], ps[:, 2 * (u % 3):2 * (u % 3) + 2, 0:n], ACT.Exp,
                                   scale=SCALE).then_inc(S["exp_ok"], 1)
                act.wait_ge(S["y_tr"], q + 1)
                act.activation(y_t, ps[:, 0, :], ACT.Copy).then_inc(S["yt_ok"], 1)

        def dve_attention(dve, c):
            dve.memset(qk16, 0.0).then_inc(S["pad_ok"], 1)
            dve.wait_ge(S["pad_ok"], 2 * c["attn"] + 1)
            dve.memset(qk16[:, :, HEADS:2 * HEADS, QROWS:MROWS], 1.0)
            dve.memset(vc[:, :, :, DH:DH + 1], 1.0).then_inc(S["pad_ok"], 1)
            dve.wait_ge(S["pad_ok"], 2 * c["attn"] + 2)
            w = pcol("conv_c")
            with dve.Fori(0, NB) as b:
                q = 4 * c["attn"] + b
                h = ha[:, b, :]
                dve.tensor_scalar(hc, h, w[:, 2:3], None, ALU.mult).then_inc(S["conv_ok"], 1)
                for lag in (1, 2):
                    dve.wait_ge(S["conv_ok"], 2 * q + lag)
                    dve.scalar_tensor_tensor(out=hc[:, lag:SEQ], in0=ha[:, b, 0:SEQ - lag], scalar=w[:, 2 - lag:3 - lag],
                                             in1=hc[:, lag:SEQ], op0=ALU.mult,
                                             op1=ALU.add).then_inc(S["conv_ok" if lag == 1 else "hc_ok"], 1)
                cos, sin = ccol("cos"), ccol("sin")

                def rope(i):
                    dve.wait_ge(S["qkv_mm"], 4 * q + i + 1)
                    qk = ps[:, i, 0:2 * P].rearrange("p (h d) -> p h d", d=DH)
                    half = DH // 2

                    def row(table, a, n):
                        return table[:, i * DH + a:i * DH + a + n].unsqueeze(1).to_broadcast([P, 2 * HEADS, n])

                    if i >= 2:
                        dve.wait_ge(S["split_ok"], 4 * q + i - 2 + 1)
                    dve.tensor_tensor(rope1[:, i % 2], qk, row(cos, 0, DH), ALU.mult)
                    dve.tensor_tensor(rope2[:, i % 2, :, 0:half], qk[:, :, half:DH], row(sin, 0, half), ALU.mult)
                    dve.tensor_tensor(rope2[:, i % 2, :, half:DH], qk[:, :, 0:half], row(sin, half, half), ALU.mult)
                    dve.tensor_copy(vc[:, i, :, 0:DH], ps[:, i, 2 * P:3 * P].rearrange("p (h d) -> p h d", d=DH))\
                       .then_inc(S["rope_mid"], 1)
                    dve.wait_ge(S["rope_mid"], 4 * q + i + 1)
                    dve.tensor_tensor(rope1[:, i % 2], rope1[:, i % 2], rope2[:, i % 2],
                                      ALU.add).then_inc(S["rope_ok"], 1)

                def rest(i):
                    dve.wait_ge(S["part1_ok"], 4 * q + i + 1)
                    dve.tensor_tensor(rope2[:, i % 2], rope1[:, i % 2], qk16[:, i, :, 0:DH],
                                      ALU.subtract).then_inc(S["rest_ok"], 1)

                def part3(i):
                    dve.wait_ge(S["part2_ok"], 4 * q + i + 1)
                    left = rope2[:, i % 2]
                    dve.tensor_tensor(qk16[:, i, 0:HEADS, 5 * DH:6 * DH], left[:, 0:HEADS, :],
                                      qk16[:, i, 0:HEADS, 3 * DH:4 * DH], ALU.subtract)
                    dve.tensor_tensor(qk16[:, i, HEADS:2 * HEADS, 2 * DH:3 * DH], left[:, HEADS:2 * HEADS, :],
                                      qk16[:, i, HEADS:2 * HEADS, DH:2 * DH], ALU.subtract).then_inc(S["split_ok"], 1)

                rope(0)
                rope(1)
                for i in range(TPB):
                    rest(i)
                    if i >= 1:
                        part3(i - 1)
                    if 1 <= i < TPB - 1:
                        rope(i + 1)
                part3(TPB - 1)
                for i in range(TPB):
                    dve.wait_ge(S["q_tr"], 4 * q + i + 1)
                    dve.tensor_copy(qt_s[:, :, i * P:(i + 1) * P],
                                    ps[:, i, :].bitcast(BF16).rearrange("p (a n) -> p a n", n=P)).then_inc(S["qt_ok"], 1)
                for u, (i, hp) in enumerate(UNITS):
                    dve.wait_ge(S["s1_mm"], 32 * q + u + 1)
                    dve.tensor_reduce(neg_max[:, i, 2 * hp:2 * hp + 2],
                                      ps[:, 2 * (u % 3):2 * (u % 3) + 2, 0:(i + 1) * P], AX_X, ALU.max,
                                      negate=True).then_inc(S["s1_max"], 1)
                    if hp == PAIRS - 1:
                        m1 = qk16[:, i, 0:HEADS, QROWS:QROWS + 1]
                        m2 = qk16[:, i, 0:HEADS, QROWS + 1:QROWS + 2]
                        dve.wait_ge(S["s1_max"], 32 * q + u + 1)
                        dve.tensor_copy(m1, neg_max[:, i, :].unsqueeze(2)).then_inc(S["m1_ok"], 1)
                        dve.wait_ge(S["m1_ok"], 4 * q + i + 1)
                        dve.tensor_tensor(m2, neg_max[:, i, :].unsqueeze(2), m1, ALU.subtract).then_inc(S["m_ok"], 1)
                for u in range(32):
                    edge = pt[:, u % NPT, :, 0:P]
                    dve.wait_ge(S["exp_ok"], 32 * q + u + 1)
                    dve.scalar_tensor_tensor(out=edge, in0=edge, scalar=3e38,
                                             in1=ccol("tri").unsqueeze(1).to_broadcast([P, 2, P]), op0=ALU.min,
                                             op1=ALU.mult).then_inc(S["sel_ok"], 1)
                dve.wait_ge(S["pv_mm"], 32 * q + 32)
                for half in range(2):
                    pv = ps[:, 6 + half, 0:2 * HEADS * (DH + 1)].rearrange("p (i h d) -> p i h d", i=2, d=DH + 1)
                    dve.reciprocal(rden[:, 2 * half:2 * half + 2, :].unsqueeze(3), pv[:, :, :, DH:DH + 1]).then_inc(S["rden_ok"], 1)
                for half in range(2):
                    pv = ps[:, 6 + half, 0:2 * HEADS * (DH + 1)].rearrange("p (i h d) -> p i h d", i=2, d=DH + 1)
                    dve.wait_ge(S["rden_ok"], 2 * q + 2)
                    ins = dve.tensor_tensor(y_tok[:, 2 * half:2 * half + 2], pv[:, :, :, 0:DH],
                                            rden[:, 2 * half:2 * half + 2, :].unsqueeze(3).to_broadcast([P, 2, HEADS, DH]),
                                            ALU.mult)
                ins.then_inc(S["y_ok"], 1)
                dve.wait_ge(S["proj_mm"], q + 1)
                dve.tensor_tensor(hb[:, b, :], hb[:, b, :], ps[:, 1, :], ALU.add).then_inc(S["x1_ok"], 1)

        def dve_conv_d(dve, c):
            w = pcol("conv_d")
            for t in range(NB):
                dve.tensor_scalar(res[:, t, :], ha[:, t, :], w[:, 1:2], None, ALU.mult).then_inc(S["sc_a"], 1)
            for t in range(NB):
                dve.wait_ge(S["sc_a"], t + 1)
                dve.scalar_tensor_tensor(out=res[:, t, 1:SEQ], in0=ha[:, t, 0:SEQ - 1], scalar=w[:, 0:1],
                                         in1=res[:, t, 1:SEQ], op0=ALU.mult, op1=ALU.add).then_inc(S["sc_b"], 1)
            for t in range(NB):
                dve.wait_ge(S["sc_b"], t + 1)
                dve.scalar_tensor_tensor(out=res[:, t, 0:SEQ - 1], in0=ha[:, t, 1:SEQ], scalar=w[:, 2:3],
                                         in1=res[:, t, 0:SEQ - 1], op0=ALU.mult, op1=ALU.add).then_inc(S["sc_c"], 1)

        def pe_ssm(pe, c):
            for t in range(NB):
                pe.wait_ge(S["u_ok"], t + 1)
                pe.matmul(ps[0:2 * NSTATE, t, :], pcol("w_bc"), hb[:, t, :], start=True, stop=True).then_inc(S["bc_mm"], 1)
                pe.matmul(ps[0:DT_RANK, 4 + t, :], pcol("w_dt"), hb[:, t, :], start=True, stop=True).then_inc(S["t1_mm"], 1)
            for t in range(NB):
                pe.wait_ge(S["bc_ok"], t + 1)
                pe.wait_ge(S["t1_ok"], t + 1)
                pe.matmul(ps[:, t, :], pcol("w_dtp")[0:DT_RANK], t1_s[:, t, :], start=True, stop=True).then_inc(S["z_mm"], 1)
            pe.wait_ge(S["diag_ok"], 1)
            for t in range(NB):
                pe.matmul(ps[:, 4 + t, :], diag_d, ha[:, t, :], start=True, stop=False, skip_group_check=True)
            pe.wait_ge(S["z_act"], 4)
            with pe.Fori(0, NSTATE // 2) as r:
                n = 2 * r
                def sums(item):
                    s, t = ITEMS[item]
                    pe.wait_ge(S["ch_ok"], 4 * n + item + 1)
                    pe.matmul(ps[:, 4 + t, :], ident, ch[:, s, t, :], start=False, stop=False,
                              skip_group_check=True).then_inc(S["sum_mm"], 1)

                for item, (s, t) in enumerate(ITEMS):
                    if t == 0:
                        pe.wait_ge(S[f"bc_in{s}"], 8 * n + 16)
                    if item >= 2:
                        pe.wait_ge(S["db_ok"], 4 * n + item - 2 + 1)
                    pe.matmul(ps[:, item % 2, :], ccol("ones")[0:1], bc_row[:, s, 0, t, :], start=True,
                              stop=True).then_inc(S["bb_mm"], 1)
                    if item >= 2:
                        pe.wait_ge(S["ch_ok"], 4 * n + item - 2 + 1)
                    pe.matmul(ps[:, 2 + item % 2, :], ccol("ones")[0:1], bc_row[:, s, 1, t, :], start=True,
                              stop=True).then_inc(S["cb_mm"], 1)
                    if item:
                        sums(item - 1)
                sums(7)

        def act_ssm(act, c):
            act.activation(a_neg, pcol("a_log"), ACT.Exp).then_inc(S["a_exp"], 1)
            for t in range(NB):
                act.wait_ge(S["sc_c"], t + 1)
                act.activation(hb[:, t, :], res[:, t, :], ACT.Silu).then_inc(S["u_ok"], 1)
            for t in range(NB):
                act.wait_ge(S["bc_mm"], t + 1)
                act.activation(bc_s[:, t, :], ps[0:2 * NSTATE, t, :], ACT.Identity,
                               bias=pcol("b_bc")[0:2 * NSTATE]).then_inc(S["bc_ok"], 1)
                act.wait_ge(S["t1_mm"], t + 1)
                act.activation(t1_s[:, t, :], ps[0:DT_RANK, 4 + t, :], ACT.Identity,
                               bias=pcol("b_dt")[0:DT_RANK]).then_inc(S["t1_ok"], 1)
            for t in range(NB):
                act.wait_ge(S["z_mm"], t + 1)
                act.activation(soft_a[:, t, :], ps[:, t, :], ACT.Abs, bias=pcol("b_dtp"))
                act.activation(soft_r[:, t, :], ps[:, t, :], ACT.Relu, bias=pcol("b_dtp")).then_inc(S["z_act"], 1)
            for t in range(NB):
                act.wait_ge(S["z_act"], t + 1)
                act.activation(soft_e[:, t, :], soft_a[:, t, :], ACT.Exp, scale=-1.0).then_inc(S["soft_exp"], 1)
            for t in range(NB):
                act.wait_ge(S["soft_u"], t + 1)
                act.activation(soft_l[:, t, :], soft_a[:, t, :], ACT.Ln).then_inc(S["soft_log"], 1)
            act.wait_ge(S["a_ok"], 1)
            act.wait_ge(S["dt_ok"], 4)
            act.wait_ge(S["bc_out"], 16)

            def decay(r, s):
                act.activation(da[:, s], dt_s[:, :, :], ACT.Exp, scale=a_neg.rearrange("p (r s) -> p s r", s=2)[:, s, :].unsqueeze(2)[:, r, :]).then_inc(S["da_ok"], 1)

            for s in range(2):
                decay(0, s)
            with act.Fori(1, NSTATE // 2) as r:
                n = 2 * r
                for s in range(2):
                    act.wait_ge(S["scan_ok"], 4 * (n + s) - 4)
                    decay(r, s)

        def dve_ssm(dve, c):
            dve.wait_ge(S["a_exp"], 1)
            dve.tensor_scalar(a_neg, a_neg, -1.0, None, ALU.mult).then_inc(S["a_ok"], 1)
            dve.tensor_scalar(diag_d, ident, pcol("dcoef"), None, ALU.mult).then_inc(S["diag_ok"], 1)
            for t in range(NB):
                dve.wait_ge(S["soft_exp"], t + 1)
                dve.tensor_scalar(soft_a[:, t, :], soft_e[:, t, :], 1.0, None, ALU.add).then_inc(S["soft_u"], 1)
            for t in range(NB):
                dve.wait_ge(S["soft_u"], t + 1)
                dve.scalar_tensor_tensor(out=soft_e[:, t, :], in0=soft_a[:, t, :], scalar=-1.0, in1=soft_e[:, t, :],
                                         op0=ALU.add, op1=ALU.subtract).then_inc(S["soft_d"], 1)
            for t in range(NB):
                dve.wait_ge(S["soft_log"], t + 1)
                dve.wait_ge(S["soft_d"], t + 1)
                dve.tensor_tensor(soft_l[:, t, :], soft_l[:, t, :], soft_e[:, t, :], ALU.subtract).then_inc(S["soft_s"], 1)
            for t in range(NB):
                dve.wait_ge(S["soft_s"], t + 1)
                dve.tensor_tensor(dt_s[:, t, :], soft_l[:, t, :], soft_r[:, t, :], ALU.add).then_inc(S["dt_ok"], 1)
            for t in range(NB):
                dve.wait_ge(S["dt_ok"], t + 1)
                dve.tensor_tensor(dtx[:, t, :], dt_s[:, t, :], ha[:, t, :], ALU.mult).then_inc(S["dtx_ok"], 1)
            dve.wait_ge(S["dtx_ok"], 4)
            with dve.Fori(0, NSTATE // 2) as r:
                n = 2 * r
                for item, (s, t) in enumerate(ITEMS):
                    k = 4 * n + item + 1
                    dve.wait_ge(S["bb_mm"], k)
                    dve.tensor_tensor(db[:, s, t, :], dtx[:, t, :], ps[:, item % 2, :], ALU.mult).then_inc(S["db_ok"], 1)
                    if t == 0:
                        dve.wait_ge(S["da_ok"], n + s + 1)
                    dve.wait_ge(S["db_ok"], k)
                    dve.tensor_tensor_scan(hst[:, s, t, :], da[:, s, t, :], db[:, s, t, :], 0.0, ALU.mult,
                                           ALU.add).then_inc(S["scan_ok"], 1)
                    dve.wait_ge(S["cb_mm"], k)
                    dve.wait_ge(S["scan_ok"], k)
                    dve.tensor_tensor(ch[:, s, t, :], hst[:, s, t, :], ps[:, 2 + item % 2, :],
                                      ALU.mult).then_inc(S["ch_ok"], 1)

        def sp_ssm(sp, c):
            sp.wait_ge(S["bc_ok"], 4)
            sp.dma_start(bc_dram.rearrange("n (t q) -> n t q", t=NB), bc_s).then_inc(S["bc_out"], 16)
            sp.wait_ge(S["bc_out"], 16)
            rows = bc_dram.rearrange("(w r s) (t q) -> s r w t q", w=2, s=2, t=NB)
            for s in range(2):
                sp.dma_start(bc_row[0:1, s], rows[s, 0].unsqueeze(0)).then_inc(S[f"bc_in{s}"], 16)
            with sp.Fori(1, NSTATE // 2) as r:
                n = 2 * r
                for s in range(2):
                    sp.wait_ge(S["cb_mm"], 4 * (n + s) - 4)
                    sp.dma_start(bc_row[0:1, s], rows[s, r].unsqueeze(0)).then_inc(S[f"bc_in{s}"], 16)

        for extra in ("sc_a", "sc_b", "sc_c", "soft_exp", "soft_d", "soft_s"):
            S[extra] = sem(extra)

        block_ = ctx.enter_context(nc.Block())
        x_tok = res[:, :, :].rearrange("p b (i d) -> p (b i) d", d=P)

        def x_ready(c):
            def wait(eng, t):
                if c["prev"] == "":
                    eng.wait_ge(S["x_cp"], t + 1)
                elif c["prev"] == "A":
                    eng.wait_ge(S["added"], c["added"])
                else:
                    eng.wait_ge(S["x_ok"], 4 * c["x_upd"] - 4 + t + 1)
            return wait

        end = dict(count, prev=stages[-1:])
        order = [(kind, dict(c, prev=stages[i - 1:i] if i else "")) for i, (kind, c) in enumerate(order)]

        @block_.sync
        def _(sp):
            sp.dma_start(x_tok, x_in.rearrange("(i p) d -> p i d", p=P)).then_inc(S["x_in"], 16)
            sp.dma_start(con[:, :], consts).then_inc(S["params_in"], 16)
            sp.dma_start(par[:, :], params).then_inc(S["params_in"], 16)
            for kind, c in order:
                def slot_free(sp, s, c=c):
                    if c["prev"] in ("A", "C"):
                        sp.wait_ge(S["gated_ok"], c["added"] - 4 + 4 * s)
                    elif c["prev"] == "B":
                        sp.wait_ge(S["ln_out"], 4 * (c["ln"] - 1 - 2 * (1 - s)))
                    elif c["prev"] == "D":
                        sp.wait_ge(S["gated_ok"], c["added"])
                if kind == "A":
                    sp_moe(sp, c, pack_a, A_COLS, EXPERTS0, slot_free)
                elif kind == "B":
                    sp_layers(sp, c, slot_free)
                elif kind == "C":
                    sp_moe(sp, c, pack_c, C_COLS, EXPERTS1, slot_free)
                elif kind == "D":
                    sp_ssm(sp, c)
            for t in range(NB):
                sp.wait_ge(S["cp_out"], t + 1)
                sp.dma_start(out.rearrange("(i p) d -> p i d", p=P)[:, TPB * t:TPB * t + TPB, :],
                             x_tok[:, TPB * t:TPB * t + TPB, :]).then_inc(S["x_out"], 16)
            sp.wait_ge(S["x_out"], 64)

        @block_.tensor
        def _(pe):
            pe.wait_ge(S["params_in"], 32)
            pe.wait_ge(S["x_in"], 16)
            for t in range(NB):
                for i in range(TPB):
                    mm = pe.transpose(ps[:, t, i * P:(i + 1) * P], x_tok[:, TPB * t + i, :], ident)
                mm.then_inc(S["x_tr"], 1)
            pe.wait_ge(S["consts16"], 1)
            for kind, c in order:
                n = c["ln"]
                pe_ln(pe, n, x, x_ready(c))
                if kind == "A":
                    pe_router(pe, n, c["moe_call"], pcol("gate"), EXPERTS0)
                    pe.wait_ge(S["gate_cp"], c["moe_call"] + 1)
                    pe_experts0(pe, c)
                elif kind == "B":
                    pe_layers(pe, c)
                    last = n + 2 * LAYERS
                    pe_ln(pe, last + 1, ha, lambda pe, t: pe.wait_ge(S["ln_out"], 4 * last + t + 1))
                elif kind == "C":
                    pe_ln(pe, n + 1, hb, lambda pe, t: pe.wait_ge(S["ln_out"], 4 * n + t + 1))
                    pe.wait_ge(S["ln_out"], 4 * n + 8)
                    pe_attention(pe, c)
                    pe_ln(pe, n + 2, hb, lambda pe, t: pe.wait_ge(S["x1_ok"], 4 * c["attn"] + 4))
                    pe_router(pe, n + 2, c["moe_call"], pcol("router"), EXPERTS1)
                    pe.wait_ge(S["gate_cp"], c["moe_call"] + 1)
                    pe_experts1(pe, c)
                else:
                    pe_ssm(pe, c)
            for t in range(NB):
                x_ready(end)(pe, t)
                for i in range(TPB):
                    mm = pe.transpose(ps[:, t, i * P:(i + 1) * P], x[:, t, i * P:(i + 1) * P], ident)
                mm.then_inc(S["tr_out"], 1)

        @block_.scalar
        def _(act):
            act.wait_ge(S["params_in"], 32)
            exp_call = 0
            for kind, c in order:
                n = c["ln"]
                act_ln(act, n)
                if kind == "A":
                    act_router(act, exp_call)
                    exp_call += 1
                    act_experts0(act, c)
                elif kind == "B":
                    act_layers(act, c)
                    act_ln(act, n + 2 * LAYERS + 1)
                elif kind == "C":
                    act_ln(act, n + 1)
                    act_attention(act, c)
                    act_ln(act, n + 2)
                    act_experts1(act, c)
                else:
                    act_ssm(act, c)

        @block_.vector
        def _(dve):
            dve.wait_ge(S["params_in"], 32)
            dve.tensor_copy(ident16[:, :], ident)
            dve.tensor_copy(mask_qk16[:, :], ccol("mask_qk")).then_inc(S["consts16"], 1)
            for t in range(NB):
                dve.wait_ge(S["x_tr"], t + 1)
                dve.tensor_copy(x[:, t, :], ps[:, t, :]).then_inc(S["x_cp"], 1)
            exp_call = 0
            for kind, c in order:
                n = c["ln"]
                x_ready(c)(dve, NB - 1)
                if kind == "A":
                    dve_ln(dve, n, x, ha)
                    dve_router(dve, c["moe_call"], exp_call, EXPERTS0, 2)
                    exp_call += 1
                    dve_experts0(dve, c, x)
                elif kind == "B":
                    dve_ln(dve, n, x, ha)
                    dve.memset(v_aug[:, :, :, P:P + 1], 1.0)
                    dve_layers(dve, c)
                    last = n + 2 * LAYERS + 1
                    dve_ln(dve, last, ha, hb, (c["lns"] + 2 * LAYERS, pcol("gf"), pcol("bef")))
                    for t in range(NB):
                        dve.wait_ge(S["ln_out"], 4 * last + t + 1)
                        dve.tensor_tensor(x[:, t, :], x[:, t, :], hb[:, t, :], ALU.add).then_inc(S["x_ok"], 1)
                elif kind == "C":
                    dve_ln(dve, n, x, hb)
                    dve.wait_ge(S["ln_out"], 4 * n + 4)
                    dve_ln(dve, n + 1, hb, ha, (c["lns"], pcol("ln1_w"), pcol("ln1_b")))
                    dve.wait_ge(S["ln_out"], 4 * n + 8)
                    dve_attention(dve, c)
                    dve.wait_ge(S["x1_ok"], 4 * c["attn"] + 4)
                    dve_ln(dve, n + 2, hb, ha, (c["lns"] + 1, pcol("ln2_w"), pcol("ln2_b")))
                    dve_router(dve, c["moe_call"], None, EXPERTS1, 1)
                    dve_experts1(dve, c, hb)
                    dve.wait_ge(S["added"], c["added"] + NB * EXPERTS1)
                    for t in range(NB):
                        dve.scalar_tensor_tensor(out=x[:, t, :], in0=hb[:, t, :], scalar=0.5, in1=x[:, t, :],
                                                 op0=ALU.mult, op1=ALU.add).then_inc(S["x_ok"], 1)
                else:
                    dve_ln(dve, n, x, ha)
                    dve.wait_ge(S["ln_out"], 4 * n + 4)
                    dve_conv_d(dve, c)
                    dve_ssm(dve, c)
                    dve.wait_ge(S["sum_mm"], NB * NSTATE)
                    for t in range(NB):
                        dve.tensor_tensor(x[:, t, :], x[:, t, :], ps[:, 4 + t, :], ALU.add).then_inc(S["x_ok"], 1)
            for t in range(NB):
                dve.wait_ge(S["tr_out"], t + 1)
                dve.tensor_copy(x_tok[:, TPB * t:TPB * t + TPB, :].rearrange("p i d -> p (i d)"),
                                ps[:, t, :]).then_inc(S["cp_out"], 1)


def shape_constants():
    at, n = columns(CONSTS)
    c = np.zeros((P, n), np.float32)

    def put(name, v):
        c[:, at[name][0]:at[name][1]] = v

    i = np.arange(P)
    put("ident", np.eye(P))
    put("mean", 1.0 / P)
    put("block", i[:, None] // DH == i[None, :] // DH)
    inv = (np.float32(1.0) / np.float32(10000.0) ** (np.arange(0, DH, 2, dtype=np.float32) / np.float32(DH))).astype(np.float32)
    angle = (np.arange(SEQ, dtype=np.float32)[:, None] * inv[None, :]).astype(np.float32)
    angle = np.concatenate([angle, angle], 1).astype(np.float64)
    sign = np.where(np.arange(DH) < DH // 2, -1.0, 1.0)
    put("cos", np.cos(angle).reshape(TPB, P, DH).transpose(1, 0, 2).reshape(P, -1))
    put("sin", (np.sin(angle) * sign).reshape(TPB, P, DH).transpose(1, 0, 2).reshape(P, -1))
    put("desc8", 8.0 - np.arange(8))
    put("desc4", 4.0 - np.arange(4))
    put("mask_qk", np.where(i[None, :] <= i[:, None], 0.0, NEG))
    put("tri", i[None, :] >= i[:, None])
    put("ones", 1.0)
    put("eps", 1e-5)
    put("tiny", 1e-6)
    return c


def kernel(**inputs):
    import numpy as _np
    import concourse.bacc as _bacc
    from concourse.bass_utils import run_bass_kernel_spmd as _run

    a = {k: _np.asarray(v) for k, v in inputs.items()}

    def chunks(w):
        e, r, n = w.shape
        return w.reshape(e, r // P, P, n).transpose(0, 2, 1, 3).reshape(e, P, -1)

    def cols(v):
        return v.reshape(v.shape[0], -1, P).transpose(0, 2, 1)

    g = lambda n: a["L0_attn_" + n]
    pack_a = _np.concatenate([a["L0_ffn_w1"], chunks(a["L0_ffn_w2"]), cols(a["L0_ffn_b1"]), cols(a["L0_ffn_b2"])], 2)
    kv_bias = _np.concatenate([g("bk"), g("bv")], 1)[:, None, :]
    pack_b = _np.concatenate(
        [g("Wq"), g("Wk"), g("Wv"), g("Wo"), g("W1"), chunks(g("W2")), _np.broadcast_to(kv_bias, (LAYERS, P, 2 * P))]
        + [cols(g(n)) for n in ("bq", "bo", "c1", "c2", "g1", "be1", "g2", "be2")], 2)
    pack_c = _np.concatenate([a["L1_ffn_expert_wv"], chunks(a["L1_ffn_expert_proj"])], 2)
    at, n = columns(PARAMS)
    params = _np.zeros((P, n), _np.float32)

    def put(name, v):
        v = v.reshape(v.shape[0], -1)
        params[0:v.shape[0], at[name][0]:at[name][1]] = v

    put("gate", a["L0_ffn_gate_w"].T)
    put("gf", g("gf"))
    put("bef", g("bef"))
    for k in ("ln1_w", "ln1_b", "ln2_w", "ln2_b"):
        put(k, a["L1_ffn_" + k])
    put("conv_c", a["L1_ffn_conv_w"])
    put("wqkv", a["L1_ffn_attn_w"])
    put("proj", a["L1_ffn_proj_w"])
    put("router", a["L1_ffn_router_w"])
    put("conv_d", a["L1_attn_conv_w"].T)
    put("w_bc", a["L1_attn_W_bc"])
    put("b_bc", a["L1_attn_b_bc"])
    put("w_dt", a["L1_attn_W_dt"])
    put("b_dt", a["L1_attn_b_dt"])
    put("w_dtp", a["L1_attn_W_dtp"])
    put("b_dtp", a["L1_attn_b_dtp"])
    put("a_log", a["L1_attn_A_log"])
    put("dcoef", a["L1_attn_Dcoeff"])
    nc = _bacc.Bacc("TRN2", target_bir_lowering=False, num_devices=1)
    arrays = {"x_in": a["L0_attn_x"].reshape(NB * SEQ, P), "pack_a": pack_a, "pack_b": pack_b, "pack_c": pack_c,
              "params_dram": params, "consts_dram": shape_constants()}
    arrays = {k: _np.ascontiguousarray(v) for k, v in arrays.items()}
    args = [nc.dram_tensor(k, v.shape, F32, kind="ExternalInput").ap() for k, v in arrays.items()]
    args.append(nc.dram_tensor("out_dram", (NB * SEQ, P), F32, kind="ExternalOutput").ap())
    build(nc, *args)
    r = _run(nc, [arrays], core_ids=[0])
    return r.results[0]["out_dram"].reshape(NB, SEQ, P)
```

```python
from contextlib import ExitStack

import numpy as np
import concourse.bass as bass
from concourse import mybir

ALU = mybir.AluOpType
ACT = mybir.ActivationFunctionType
F32 = mybir.dt.float32
BF16 = mybir.dt.bfloat16
AX_X = mybir.AxisListType.X

P = 128
NB, SEQ = 4, 512
TILES = NB * SEQ // P
TPB = SEQ // P
F = 512
FC = F // P
EXPERTS0, EXPERTS1 = 8, 4
LAYERS = 8
HEADS, DH = 16, 8
PAIRS = HEADS // 2
NSTATE, DT_RANK = 16, 8
NEG = -1e30

A_W1, A_W2, A_B1, A_B2, A_COLS = 0, 512, 1024, 1028, 1029
B_WQ, B_WKV, B_WO, B_W1, B_W2, B_KVB, B_VEC = 0, 128, 384, 512, 1024, 1536, 1792
B_BQ, B_BO, B_C1, B_C2, B_G1, B_BE1, B_G2, B_BE2, B_COLS = (B_VEC + i for i in (0, 1, 2, 6, 7, 8, 9, 10, 11))
C_WV, C_PROJ, C_COLS = 0, 1024, 1536
SLOT_COLS = B_COLS

PARAMS = [
    ("gate", EXPERTS0), ("gf", 1), ("bef", 1), ("ln1_w", 1), ("ln1_b", 1), ("ln2_w", 1), ("ln2_b", 1),
    ("conv_c", 3), ("wqkv", 3 * P), ("proj", P), ("router", EXPERTS1), ("conv_d", 3), ("w_bc", 2 * NSTATE),
    ("b_bc", 1), ("w_dt", DT_RANK), ("b_dt", 1), ("w_dtp", P), ("b_dtp", 1), ("a_log", NSTATE), ("dcoef", 1),
]
CONSTS = [("ident", P), ("mean", P), ("block", P), ("head_sum", 32), ("head_spread", P), ("cos", TPB * DH), ("sin", TPB * DH), ("desc8", 8),
          ("desc4", 4), ("mask_qk", P), ("tri", P), ("eps", 1), ("tiny", 1)]


def columns(table):
    at, out = 0, {}
    for name, n in table:
        out[name] = (at, at + n)
        at += n
    return out, at


def build(nc, x_in, pack_a, pack_b, pack_c, params, consts, out, dbg=None, stages="ABACDC"):
    par_at, par_cols = columns(PARAMS)
    con_at, con_cols = columns(CONSTS)
    with ExitStack() as ctx:
        def sb(name, shape, dt=F32):
            return ctx.enter_context(nc.sbuf_tensor(name, shape, dt))

        sems = {}

        def sem(name):
            sems[name] = ctx.enter_context(nc.semaphore(name))
            return sems[name]

        gates_dram = nc.dram_tensor("gates_dram", (4, P, P), F32, kind="Internal").ap()
        bc_dram = nc.dram_tensor("bc_dram", (3, 2 * NSTATE, NB * SEQ), BF16, kind="Internal").ap()

        par = sb("par", [P, par_cols])
        con = sb("con", [P, con_cols])
        mask_qk16 = sb("mask_qk16", [P, P], BF16)
        ident16 = sb("ident16", [P, P], BF16)
        ones16 = sb("ones16", [P, P], BF16)
        x = sb("x", [P, NB, SEQ])
        ha = sb("ha", [P, NB, SEQ])
        hb = sb("hb", [P, NB, SEQ])
        res = sb("res", [P, NB, SEQ])
        xc = sb("xc", [P, NB, SEQ])
        sq = sb("sq", [P, NB, SEQ])
        rstd = sb("rstd", [P, NB, SEQ])
        wslot = sb("wslot", [P, 2, SLOT_COLS])
        gate_bc = sb("gate_bc", [P, 2, TILES, P])
        arena = sb("arena", [P, 17 * 1024])
        ps = ctx.enter_context(nc.psum_tensor("ps", [P, 8, 512], F32))

        def pcol(name):
            a, b = par_at[name]
            return par[:, a:b]

        def ccol(name):
            a, b = con_at[name]
            return con[:, a:b]

        def view(at, *shape):
            n = int(np.prod(shape))
            v = arena[:, at:at + n]
            if len(shape) == 1:
                return v
            names = "abcd"[:len(shape)]
            return v.rearrange(f"p ({' '.join(names)}) -> p {' '.join(names)}",
                               **{k: s for k, s in zip(names[1:], shape[1:])})

        def view16(at, *shape):
            n = int(np.prod(shape))
            names = "abcd"[:len(shape)]
            return arena[:, at:at + n // 2].bitcast(BF16).rearrange(
                f"p ({' '.join(names)}) -> p {' '.join(names)}", **{k: s for k, s in zip(names[1:], shape[1:])})

        ident, mean_w, block = ccol("ident"), ccol("mean"), ccol("block")
        eps, tiny = ccol("eps"), ccol("tiny")

        hid = view(0, 2, FC, SEQ)
        gated = view(4096, 2, SEQ)
        silu = view(5120, 2, SEQ)
        rt = [view(8192 + 128 * i, TILES, 8) for i in range(8)]
        rs = [view(8192 + 1024 + 16 * i, TILES) for i in range(8)]
        gate_t = view(8192 + 1536, P)
        q_exp, q_relu = view(0, NB, SEQ), view(2048, NB, SEQ)
        qf = view(4096, NB, SEQ)
        kf = view(6144, NB, TPB, P)
        v_aug = view(8192, NB, TPB, P + 1)
        kv_bd, ks_h = view(10368, NB, P), view(10880, NB, 32)
        hid_b = view(11392, 2, FC, SEQ)
        k_exp, k_relu = view(0, NB, TPB, P), view(2048, NB, TPB, P)
        rz, att = view(0, SEQ), view(2048, NB, SEQ)
        hc = view(0, SEQ)
        qk16 = view16(512, TPB, 2 * HEADS, 64)
        vc = view(4608, TPB, HEADS, 32)
        kt_s, qt_s, q2_s = view16(6656, PAIRS, SEQ), view16(8704, PAIRS, SEQ), view16(10752, PAIRS, SEQ)
        pv_s = view(6656, TPB, SEQ)
        y_tok = view(8704, TPB, HEADS, DH)
        y_t = view(9216, SEQ)
        NPT = 4
        pt = view(12800, NPT, 2, SEQ)
        rope1, rope2 = view(12800, 2, 2 * HEADS, DH), view(13312, 2, 2 * HEADS, DH)
        rden = view(16896, TPB * HEADS)
        neg_max = view(16960, TPB, HEADS)
        dt_s, dtx = xc, sq
        da = view(0, 2, NB, SEQ)
        db = view(4096, 2, NB, SEQ)
        hst = view(8192, 2, NB, SEQ)
        ch = view(12288, 2, NB, SEQ)
        bc_row = sb("bc_row", [3, 2, 2, NB, SEQ], BF16)
        bc_s = view(0, NB, SEQ)[0:2 * NSTATE]
        bc16 = view16(12288, 3, NB, SEQ)[0:2 * NSTATE]
        t1_s = view(2048, NB, SEQ)[0:DT_RANK]
        soft_a, soft_e, soft_l, soft_r = view(4096, NB, SEQ), view(6144, NB, SEQ), view(8192, NB, SEQ), view(10240, NB, SEQ)
        a_neg = view(16384, NSTATE)
        diag_d = view(16400, P)

        names = """params_in x_in w_in0 w_in1 gates_out gate_in0 gate_in1 x_out bc_out bc_in0 bc_in1
            x_tr x_cp consts16 ln_mean ln_xc ln_sq ln_var ln_log ln_rs ln_scaled ln_out
            logits lg_sub lg_exp gate_ok gate_tr gate_cp dve_chain
            up_mm hid_ok down_mm gated_ok added gv_mm silu_ok
            q_mm q_act qf_ok kv_mm kv_ok k_act kf_ok kvs_mm kvbd_ok den_mm den_ok att_mm num_ok rz_ok z_bc att_ok o_mm res1_ok
            ff1_mm gelu_ok ff2_mm res2_ok x_ok
            hc_ok qkv_mm rope_mid rope_ok part1_ok rest_ok part2_ok split_ok k_tr q_tr kt_ok qt_ok m1_ok m_ok sel_ok s1_mm s1_max q2_tr q2_ok s2_mm exp_ok pv_mm
            pvs_ok pv_tr rden_ok y_ok y_tr yt_ok proj_mm x1_ok pad_ok
            conv_ok u_ok bc_mm bc_ok bc_part1 bc_rest bc_part2 bc_split t1_mm t1_ok z_mm z_act soft_u soft_log dt_ok dtx_ok a_exp a_ok diag_ok
            bb_mm cb_mm da_ok db_ok scan_ok ch_ok sum_mm tr_out cp_out""".split()
        S = {n: sem(n) for n in names}

        order = []
        count = dict(ln=0, lns=0, x_upd=0, moe=0, added=0, moe1=0, moe_call=0, w=0, g=0, up=0, hid=0, down=0,
                     gv=0, attn=0, ffn1=0)
        for kind in stages:
            order.append((kind, dict(count)))
            if kind == "A":
                count["ln"] += 1
                count["moe_call"] += 1
                count["w"] += EXPERTS0
                count["g"] += EXPERTS0
                count["added"] += NB * EXPERTS0
                count["up"] += NB * EXPERTS0
            elif kind == "B":
                count["ln"] += 2 + 2 * LAYERS
                count["lns"] += 1 + 2 * LAYERS
                count["w"] += LAYERS
                count["x_upd"] += 1
            elif kind == "C":
                count["ln"] += 3
                count["lns"] += 2
                count["moe_call"] += 1
                count["w"] += EXPERTS1
                count["g"] += EXPERTS1
                count["added"] += NB * EXPERTS1
                count["moe1"] += NB * EXPERTS1
                count["attn"] += 1
                count["x_upd"] += 1
            elif kind == "D":
                count["ln"] += 1
                count["x_upd"] += 1

        def pe_ln(pe, n, src, ready):
            for t in range(NB):
                ready(pe, t)
                pe.matmul(ps[:, t, :], mean_w, src[:, t, :], start=True, stop=True).then_inc(S["ln_mean"], 1)
            for t in range(NB):
                pe.wait_ge(S["ln_sq"], 4 * n + t + 1)
                pe.matmul(ps[:, 4 + t, :], mean_w, sq[:, t, :], start=True, stop=True).then_inc(S["ln_var"], 1)

        def act_ln(act, n):
            act.preload_act_table_set("natural_log_exp_and_others")
            for t in range(NB):
                act.wait_ge(S["ln_xc"], 4 * n + t + 1)
                act.activation(sq[:, t, :], xc[:, t, :], ACT.Square).then_inc(S["ln_sq"], 1)

            def root(t):
                act.wait_ge(S["ln_log"], 4 * n + t + 1)
                act.activation(rstd[:, t, :], rstd[:, t, :], ACT.Exp, scale=-0.5).then_inc(S["ln_rs"], 1)

            for t in range(NB):
                act.wait_ge(S["ln_var"], 4 * n + t + 1)
                act.activation(rstd[:, t, :], ps[:, 4 + t, :], ACT.Ln, bias=eps).then_inc(S["ln_log"], 1)
                if t:
                    root(t - 1)
            root(NB - 1)

        def dve_ln(dve, n, src, dst, affine=None):
            for t in range(NB):
                dve.wait_ge(S["ln_mean"], 4 * n + t + 1)
                dve.tensor_tensor(xc[:, t, :], src[:, t, :], ps[:, t, :], ALU.subtract).then_inc(S["ln_xc"], 1)

            def shift(t):
                m, g, b = affine
                dve.wait_ge(S["ln_scaled"], 4 * m + t + 1)
                dve.tensor_scalar(dst[:, t, :], dst[:, t, :], b, None, ALU.add).then_inc(S["ln_out"], 1)

            for t in range(NB):
                dve.wait_ge(S["ln_rs"], 4 * n + t + 1)
                if affine is None:
                    dve.tensor_tensor(dst[:, t, :], xc[:, t, :], rstd[:, t, :], ALU.mult).then_inc(S["ln_out"], 1)
                else:
                    dve.scalar_tensor_tensor(out=dst[:, t, :], in0=xc[:, t, :], scalar=affine[1], in1=rstd[:, t, :],
                                             op0=ALU.mult, op1=ALU.mult).then_inc(S["ln_scaled"], 1)
                    if t:
                        shift(t - 1)
            if affine is not None:
                shift(NB - 1)

        def x_ready(c):
            def wait(pe, t):
                if c["x_upd"] == 0:
                    pe.wait_ge(S["x_cp"], 4)
                else:
                    pe.wait_ge(S["x_ok"], 4 * c["x_upd"] - 4 + t + 1)
            return wait

        def pe_router(pe, n, call, w, experts):
            pe.wait_ge(S["ln_out"], 4 * n + 4)
            for i in range(TILES):
                mm = pe.matmul(ps[:, 0, experts * i:experts * (i + 1)],
                               ha[:, i // TPB, (i % TPB) * P:(i % TPB + 1) * P], w, start=True, stop=True)
            mm.then_inc(S["logits"], 1)
            pe.wait_ge(S["gate_ok"], call + 1)
            pe.transpose(ps[0:TILES * experts, 1, 0:P], gates_view(experts), ident).then_inc(S["gate_tr"], 1)

        def gates_view(experts):
            return arena[:, 8192 + 128 * 7:8192 + 128 * 7 + TILES * experts]

        def act_router(act, call):
            if call is not None:
                act.wait_ge(S["lg_sub"], call + 1)
                act.activation(rt[1], rt[0], ACT.Exp).then_inc(S["lg_exp"], 1)

        chain = [0]

        def dve_router(dve, call, exp_call, experts, top):
            def link(ins):
                chain[0] += 1
                ins.then_inc(S["dve_chain"], 1)
                dve.wait_ge(S["dve_chain"], chain[0])

            def bc(v):
                return v.unsqueeze(2).to_broadcast([P, TILES, experts])

            def tile3(i):
                return arena[:, 8192 + 128 * i:8192 + 128 * i + TILES * experts].rearrange("p (t e) -> p t e", e=experts)

            desc = ccol("desc8" if experts == 8 else "desc4").unsqueeze(1).to_broadcast([P, TILES, experts])
            dve.wait_ge(S["logits"], call + 1)
            lg = ps[:, 0, 0:TILES * experts].rearrange("p (t e) -> p t e", e=experts)
            val = tile3(0)
            if top == 2:
                link(dve.tensor_reduce(rs[0], lg, AX_X, ALU.max))
                dve.tensor_tensor(val, lg, bc(rs[0]), ALU.subtract).then_inc(S["lg_sub"], 1)
                dve.wait_ge(S["lg_exp"], exp_call + 1)
                e = tile3(1)
                link(dve.tensor_reduce(rs[0], e, AX_X, ALU.add))
                link(dve.reciprocal(rs[0], rs[0]))
                link(dve.tensor_tensor(val, e, bc(rs[0]), ALU.mult))
            else:
                link(dve.tensor_copy(val, lg))

            def first_max(src, best, hot):
                link(dve.tensor_reduce(best, src, AX_X, ALU.max))
                link(dve.tensor_tensor(tile3(3), src, bc(best), ALU.is_equal))
                link(dve.tensor_tensor(tile3(3), tile3(3), desc, ALU.mult))
                link(dve.tensor_reduce(rs[3], tile3(3), AX_X, ALU.max))
                link(dve.tensor_tensor(hot, tile3(3), bc(rs[3]), ALU.is_equal))

            first_max(val, rs[1], tile3(4))
            out_g = tile3(7)
            if top == 1:
                dve.tensor_copy(out_g, tile3(4)).then_inc(S["gate_ok"], 1)
            else:
                link(dve.scalar_tensor_tensor(out=tile3(5), in0=tile3(4), scalar=-2.0, in1=val, op0=ALU.mult, op1=ALU.add))
                first_max(tile3(5), rs[2], tile3(6))
                link(dve.tensor_tensor(tile3(4), tile3(4), tile3(6), ALU.add))
                link(dve.tensor_tensor(tile3(4), tile3(4), val, ALU.mult))
                link(dve.tensor_tensor(rs[4], rs[1], rs[2], ALU.add))
                link(dve.tensor_scalar(rs[4], rs[4], 1e-9, None, ALU.add))
                link(dve.reciprocal(rs[4], rs[4]))
                dve.scalar_tensor_tensor(out=out_g, in0=tile3(4), scalar=0.5, in1=bc(rs[4]),
                                         op0=ALU.mult, op1=ALU.mult).then_inc(S["gate_ok"], 1)
            dve.wait_ge(S["gate_tr"], call + 1)
            dve.tensor_copy(gate_t[0:TILES * experts], ps[0:TILES * experts, 1, 0:P]).then_inc(S["gate_cp"], 1)

        def sp_gates(sp, call, experts):
            sp.wait_ge(S["gate_cp"], call + 1)
            sp.dma_start(gates_dram[call, 0:TILES * experts, :], gate_t[0:TILES * experts]).then_inc(S["gates_out"], 16)
            sp.wait_ge(S["gates_out"], 16 * call + 16)

        def gate_src(call, experts, r, s):
            rows = gates_dram[call, 0:TILES * experts, :].rearrange("(t r s) p -> s r t p", r=experts // 2, s=2)
            return rows[s, r].partition_broadcast(P)


        ITEMS = [(s, t) for s in range(2) for t in range(NB)]

        def sp_moe(sp, c, pack, cols, experts, slot_free):
            pairs = pack.rearrange("(r s) p n -> s r p n", s=2)
            for s in range(2):
                slot_free(sp, s)
                sp.dma_start(wslot[:, s, 0:cols], pack[s]).then_inc(S[f"w_in{s}"], 16)
            sp_gates(sp, c["moe_call"], experts)
            for s in range(2):
                sp.dma_start(gate_bc[:, s], gate_src(c["moe_call"], experts, 0, s)).then_inc(S[f"gate_in{s}"], 16)
            with sp.Fori(1, experts // 2) as r:
                e = 2 * r
                for s in range(2):
                    sp.wait_ge(S["gated_ok"], c["added"] + 4 * e + 4 * (s - 1))
                    sp.dma_start(wslot[:, s, 0:cols], pairs[s, r]).then_inc(S[f"w_in{s}"], 16)
                    sp.dma_start(gate_bc[:, s], gate_src(c["moe_call"], experts, r, s)).then_inc(S[f"gate_in{s}"], 16)

        def w_count(c, e):
            return 8 * c["w"] + 8 * e + 16

        def pe_down(pe, c, e, item, at):
            s, t = ITEMS[item]
            base = c["added"] + 4 * e
            if item >= 4:
                pe.wait_ge(S["gated_ok"], base + item - 4 + 1)
            elif item == 3:
                pe.wait_ge(S["gated_ok"], base + 1)
            for k in range(FC):
                pe.wait_ge(S["hid_ok"], 4 * base + 4 * item + k + 1)
                mm = pe.matmul(ps[:, 4 + item % 4, :], wslot[:, s, at + k * P:at + (k + 1) * P],
                               hid[:, item % 2, k, :], start=(k == 0), stop=(k == FC - 1))
            mm.then_inc(S["down_mm"], 1)

        def pe_experts0(pe, c):
            with pe.Fori(0, EXPERTS0 // 2) as r:
                e = 2 * r
                hid0 = 4 * (c["added"] + 4 * e)

                def up(item):
                    s, t = ITEMS[item]
                    if t == 0:
                        pe.wait_ge(S[f"w_in{s}"], w_count(c, e))
                    for k in range(FC):
                        if item:
                            pe.wait_ge(S["hid_ok"], hid0 + 4 * (item - 1) + k + 1)
                        pe.matmul(ps[:, k, :], wslot[:, s, A_W1 + k * P:A_W1 + (k + 1) * P], ha[:, t, :],
                                  start=True, stop=True).then_inc(S["up_mm"], 1)

                up(0)
                for item in range(1, 8):
                    up(item)
                    pe_down(pe, c, e, item - 1, A_W2)
                pe_down(pe, c, e, 7, A_W2)
                pe.wait_ge(S["gated_ok"], c["added"] + 4 * e + 7)

        def act_experts0(act, c):
            with act.Fori(0, EXPERTS0 // 2) as r:
                e = 2 * r
                for item, (s, t) in enumerate(ITEMS):
                    for k in range(FC):
                        act.wait_ge(S["up_mm"], 4 * (c["up"] + 4 * e + item) + k + 1)
                        act.activation(hid[:, item % 2, k, :], ps[:, k, :], ACT.Gelu,
                                       bias=wslot[:, s, A_B1 + k:A_B1 + k + 1]).then_inc(S["hid_ok"], 1)

        def dve_gate(dve, c, e, item, bias, dst):
            s, t = ITEMS[item]
            if t == 0:
                dve.wait_ge(S[f"gate_in{s}"], 8 * c["g"] + 8 * e + 16)
            g = gate_bc[:, s, TPB * t:TPB * t + TPB, :].rearrange("p a b -> p (a b)")
            dve.wait_ge(S["down_mm"], c["added"] + 4 * e + item + 1)
            if bias:
                ins = dve.scalar_tensor_tensor(out=gated[:, item % 2, :], in0=ps[:, 4 + item % 4, :],
                                               scalar=wslot[:, s, A_B2:A_B2 + 1], in1=g, op0=ALU.add, op1=ALU.mult)
            else:
                ins = dve.tensor_tensor(gated[:, item % 2, :], ps[:, 4 + item % 4, :], g, ALU.mult)
            ins.then_inc(S["gated_ok"], 1)
            dve.wait_ge(S["gated_ok"], c["added"] + 4 * e + item + 1)
            dve.tensor_tensor(dst[:, t, :], dst[:, t, :], gated[:, item % 2, :], ALU.add).then_inc(S["added"], 1)

        def pe_experts1(pe, c):
            with pe.Fori(0, EXPERTS1 // 2) as r:
                e = 2 * r
                hid0 = 4 * (c["added"] + 4 * e)

                def up(item):
                    s, t = ITEMS[item]
                    if t == 0:
                        pe.wait_ge(S[f"w_in{s}"], w_count(c, e))
                    for k in range(FC):
                        if 4 * item + k >= 2:
                            pe.wait_ge(S["hid_ok"], hid0 + 4 * item + k - 2 + 1)
                        bank = 2 * (k % 2)
                        pe.matmul(ps[:, bank, :], wslot[:, s, C_WV + k * P:C_WV + (k + 1) * P], ha[:, t, :],
                                  start=True, stop=True)
                        pe.matmul(ps[:, bank + 1, :], wslot[:, s, C_WV + F + k * P:C_WV + F + (k + 1) * P],
                                  ha[:, t, :], start=True, stop=True).then_inc(S["gv_mm"], 1)

                up(0)
                for item in range(1, 8):
                    up(item)
                    pe_down(pe, c, e, item - 1, C_PROJ)
                pe_down(pe, c, e, 7, C_PROJ)
                pe.wait_ge(S["gated_ok"], c["added"] + 4 * e + 7)

        def act_experts1(act, c):
            with act.Fori(0, EXPERTS1 // 2) as r:
                e = 2 * r
                for item in range(8):
                    for k in range(FC):
                        act.wait_ge(S["gv_mm"], 4 * (c["moe1"] + 4 * e + item) + k + 1)
                        act.activation(silu[:, k % 2, :], ps[:, 2 * (k % 2), :], ACT.Silu).then_inc(S["silu_ok"], 1)

        def dve_experts1(dve, c, dst):
            with dve.Fori(0, EXPERTS1 // 2) as r:
                e = 2 * r
                def hidden(item):
                    for k in range(FC):
                        dve.wait_ge(S["silu_ok"], 4 * (c["moe1"] + 4 * e + item) + k + 1)
                        dve.tensor_tensor(hid[:, item % 2, k, :], silu[:, k % 2, :], ps[:, 2 * (k % 2) + 1, :],
                                          ALU.mult).then_inc(S["hid_ok"], 1)

                hidden(0)
                for item in range(1, 8):
                    hidden(item)
                    dve_gate(dve, c, e, item - 1, False, dst)
                dve_gate(dve, c, e, 7, False, dst)

        def dve_experts0(dve, c, dst):
            with dve.Fori(0, EXPERTS0 // 2) as r:
                e = 2 * r
                for item in range(8):
                    dve_gate(dve, c, e, item, True, dst)

        ATT_BANK = [5, 6, 7, 4]

        def pe_layers(pe, c):
            n0 = c["ln"] + 1
            with pe.Fori(0, LAYERS // 2) as r:
                l = 2 * r
                for s in range(2):
                    m = 4 * (l + s)
                    w = wslot[:, s, :]
                    nd = n0 + 2 * (l + s)
                    pe.wait_ge(S[f"w_in{s}"], w_count(c, l))
                    for b in range(NB):
                        pe.wait_ge(S["ln_out"], 4 * nd - 4 + b + 1)
                        pe.matmul(ps[:, b, :], w[:, B_WQ:B_WQ + P], ha[:, b, :], start=True,
                                  stop=True).then_inc(S["q_mm"], 1)
                    for b in range(NB):
                        bank = 4 + 2 * (b % 2)
                        if b >= 2:
                            pe.wait_ge(S["kv_ok"], m + b - 2 + 1)
                        for i in range(TPB):
                            mm = pe.matmul(ps[:, bank + i // 2, 256 * (i % 2):256 * (i % 2) + 256],
                                           ha[:, b, i * P:(i + 1) * P], w[:, B_WKV:B_WKV + 2 * P],
                                           start=True, stop=True)
                        mm.then_inc(S["kv_mm"], 1)
                    for b in range(NB):
                        pe.wait_ge(S["kf_ok"], m + b + 1)
                        pe.wait_ge(S["qf_ok"], m + b + 1)
                        for i in range(TPB):
                            mm = pe.matmul(ps[:, b, 0:P + 1], kf[:, b, i, :], v_aug[:, b, i, :],
                                           start=(i == 0), stop=(i == TPB - 1))
                        mm.then_inc(S["kvs_mm"], 1)
                    for b in range(NB):
                        pe.wait_ge(S["kvbd_ok"], m + b + 1)
                        mm = pe.matmul(ps[32 * b:32 * b + 32, 4, :], ks_h[:, b, :], qf[:, b, :], start=True, stop=True,
                                       skip_group_check=True)
                    mm.then_inc(S["den_mm"], 1)
                    for b in range(NB):
                        if b == NB - 1:
                            pe.wait_ge(S["den_ok"], l + s + 1)
                        pe.matmul(ps[:, ATT_BANK[b], :], kv_bd[:, b, :], qf[:, b, :], start=True,
                                  stop=True).then_inc(S["att_mm"], 1)
                    pe.wait_ge(S["rz_ok"], l + s + 1)
                    for b in range(NB):
                        pe.matmul(ps[:, b, :], ccol("head_spread")[32 * b:32 * b + 32], rz[32 * b:32 * b + 32, :],
                                  start=True, stop=True).then_inc(S["z_bc"], 1)
                    for b in range(NB):
                        pe.wait_ge(S["att_ok"], m + b + 1)
                        pe.matmul(ps[:, b, :], w[:, B_WO:B_WO + P], att[:, b, :], start=True,
                                  stop=True).then_inc(S["o_mm"], 1)
                    pe_ln(pe, nd, res, lambda pe, t: pe.wait_ge(S["res1_ok"], m + t + 1))

                    def ff1(b):
                        pe.wait_ge(S["ln_out"], 4 * nd + b + 1)
                        for k in range(FC):
                            if b:
                                pe.wait_ge(S["gelu_ok"], 4 * m + 4 * (b - 1) + k + 1)
                            pe.matmul(ps[:, k, :], w[:, B_W1 + k * P:B_W1 + (k + 1) * P], hb[:, b, :],
                                      start=True, stop=True).then_inc(S["ff1_mm"], 1)

                    def ff2(b):
                        pe.wait_ge(S["ln_rs"], 4 * nd + b + 1)
                        for k in range(FC):
                            pe.wait_ge(S["gelu_ok"], 4 * m + 4 * b + k + 1)
                            mm = pe.matmul(ps[:, 4 + b, :], w[:, B_W2 + k * P:B_W2 + (k + 1) * P],
                                           hid_b[:, b % 2, k, :], start=(k == 0), stop=(k == FC - 1))
                        mm.then_inc(S["ff2_mm"], 1)

                    ff1(0)
                    for b in range(1, NB):
                        ff1(b)
                        ff2(b - 1)
                    ff2(NB - 1)
                    pe_ln(pe, nd + 1, res, lambda pe, t: pe.wait_ge(S["res2_ok"], m + t + 1))

        def act_layers(act, c):
            n0 = c["ln"] + 1
            with act.Fori(0, LAYERS // 2) as r:
                l = 2 * r
                for s in range(2):
                    m = 4 * (l + s)
                    w = wslot[:, s, :]
                    nd = n0 + 2 * (l + s)
                    for b in range(NB):
                        act.wait_ge(S["q_mm"], m + b + 1)
                        act.activation(q_exp[:, b, :], ps[:, b, :], ACT.Exp, bias=w[:, B_BQ:B_BQ + 1])
                        act.activation(q_relu[:, b, :], ps[:, b, :], ACT.Relu,
                                       bias=w[:, B_BQ:B_BQ + 1]).then_inc(S["q_act"], 1)
                    for b in range(NB):
                        act.wait_ge(S["kv_ok"], m + b + 1)
                        act.activation(k_exp[:, b], kf[:, b], ACT.Exp)
                        act.activation(k_relu[:, b], kf[:, b], ACT.Relu).then_inc(S["k_act"], 1)
                    act.wait_ge(S["den_mm"], l + s + 1)
                    act.activation(rz, ps[:, 4, :], ACT.Identity, bias=tiny).then_inc(S["den_ok"], 1)
                    for b in range(NB):
                        act.wait_ge(S["att_mm"], m + b + 1)
                        act.activation(att[:, b, :], ps[:, ATT_BANK[b], :], ACT.Copy).then_inc(S["num_ok"], 1)
                    act_ln(act, nd)
                    for b in range(NB):
                        for k in range(FC):
                            act.wait_ge(S["ff1_mm"], 4 * m + 4 * b + k + 1)
                            act.activation(hid_b[:, b % 2, k, :], ps[:, k, :], ACT.Gelu,
                                           bias=w[:, B_C1 + k:B_C1 + k + 1]).then_inc(S["gelu_ok"], 1)
                    act_ln(act, nd + 1)

        def dve_layers(dve, c):
            n0, m0 = c["ln"] + 1, c["lns"]
            with dve.Fori(0, LAYERS // 2) as r:
                l = 2 * r
                for s in range(2):
                    m = 4 * (l + s)
                    w = wslot[:, s, :]
                    nd, na = n0 + 2 * (l + s), m0 + 2 * (l + s)
                    for b in range(NB):
                        dve.wait_ge(S["q_act"], m + b + 1)
                        dve.scalar_tensor_tensor(out=qf[:, b, :], in0=q_exp[:, b, :], scalar=1.0,
                                                 in1=q_relu[:, b, :], op0=ALU.min, op1=ALU.add).then_inc(S["qf_ok"], 1)
                    bias = w[:, B_KVB:B_KVB + 2 * P].unsqueeze(1).to_broadcast([P, 4, 2 * P])
                    for b in range(NB):
                        bank = 4 + 2 * (b % 2)
                        kv = ps[:, bank:bank + 2, :].rearrange("p a (i n) -> p (a i) n", i=2)
                        dve.wait_ge(S["kv_mm"], m + b + 1)
                        dve.tensor_tensor(kf[:, b], kv[:, :, 0:P], bias[:, :, 0:P], ALU.add)
                        dve.tensor_tensor(v_aug[:, b, :, 0:P], kv[:, :, P:2 * P], bias[:, :, P:2 * P],
                                          ALU.add).then_inc(S["kv_ok"], 1)
                    for b in range(NB):
                        dve.wait_ge(S["k_act"], m + b + 1)
                        dve.scalar_tensor_tensor(out=kf[:, b], in0=k_exp[:, b], scalar=1.0, in1=k_relu[:, b],
                                                 op0=ALU.min, op1=ALU.add).then_inc(S["kf_ok"], 1)
                    for b in range(NB):
                        dve.wait_ge(S["kvs_mm"], m + b + 1)
                        dve.tensor_tensor(kv_bd[:, b, :], ps[:, b, 0:P], block, ALU.mult)
                        dve.tensor_scalar(ks_h[:, b, :], ccol("head_sum"), ps[:, b, P:P + 1], None,
                                          ALU.mult).then_inc(S["kvbd_ok"], 1)
                    dve.wait_ge(S["den_ok"], l + s + 1)
                    dve.reciprocal(rz, rz).then_inc(S["rz_ok"], 1)
                    for b in range(NB):
                        dve.wait_ge(S["z_bc"], m + b + 1)
                        dve.wait_ge(S["num_ok"], m + b + 1)
                        dve.tensor_tensor(att[:, b, :], att[:, b, :], ps[:, b, :],
                                          ALU.mult).then_inc(S["att_ok"], 1)
                    for b in range(NB):
                        dve.wait_ge(S["o_mm"], m + b + 1)
                        dve.scalar_tensor_tensor(out=res[:, b, :], in0=ps[:, b, :], scalar=w[:, B_BO:B_BO + 1],
                                                 in1=ha[:, b, :], op0=ALU.add, op1=ALU.add).then_inc(S["res1_ok"], 1)
                    dve_ln(dve, nd, res, hb, (na, w[:, B_G1:B_G1 + 1], w[:, B_BE1:B_BE1 + 1]))
                    for b in range(NB):
                        dve.wait_ge(S["ff2_mm"], m + b + 1)
                        dve.scalar_tensor_tensor(out=res[:, b, :], in0=ps[:, 4 + b, :], scalar=w[:, B_C2:B_C2 + 1],
                                                 in1=hb[:, b, :], op0=ALU.add, op1=ALU.add).then_inc(S["res2_ok"], 1)
                    dve_ln(dve, nd + 1, res, ha, (na + 1, w[:, B_G2:B_G2 + 1], w[:, B_BE2:B_BE2 + 1]))

        def sp_layers(sp, c, slot_free):
            pairs = pack_b.rearrange("(r s) p n -> s r p n", s=2)
            n0 = c["ln"] + 1
            for s in range(2):
                slot_free(sp, s)
                sp.dma_start(wslot[:, s, 0:B_COLS], pack_b[s]).then_inc(S[f"w_in{s}"], 16)
            with sp.Fori(1, LAYERS // 2) as r:
                l = 2 * r
                for s in range(2):
                    sp.wait_ge(S["ln_out"], 4 * (n0 + 2 * (l + s) - 4) + 8)
                    sp.dma_start(wslot[:, s, 0:B_COLS], pairs[s, r]).then_inc(S[f"w_in{s}"], 16)

        SCALE = DH ** -0.5
        QROWS = 6 * DH
        MROWS = QROWS + 2
        UNITS = [(i, hp) for i in range(TPB) for hp in range(PAIRS)]
        PV_LAG = 3

        def pe_attention(pe, c):
            pe.wait_ge(S["pad_ok"], 2 * c["attn"] + 2)
            with pe.Fori(0, NB) as b:
                q = 4 * c["attn"] + b
                pe.wait_ge(S["hc_ok"], q + 1)
                for i in range(TPB):
                    pe.matmul(ps[:, i, 0:3 * P], hc[:, i * P:(i + 1) * P], pcol("wqkv"), start=True,
                              stop=True).then_inc(S["qkv_mm"], 1)

                def turned(i, kind, bank):
                    to = ps[:, bank, :].bitcast(BF16)
                    for hp in range(PAIRS):
                        at = qk16[:, i, kind * HEADS + 2 * hp:kind * HEADS + 2 * hp + 2, :].rearrange("p h d -> p (h d)")
                        mm = pe.transpose(to[:, hp * P:(hp + 1) * P], at, ident16[:, :])
                    return mm

                for i in range(TPB):
                    pe.wait_ge(S["split_ok"], 4 * q + i + 1)
                    turned(i, 1, 4 + i).then_inc(S["k_tr"], 1)
                    turned(i, 0, i).then_inc(S["q_tr"], 1)
                pe.wait_ge(S["kt_ok"], 4 * q + 4)
                pe.wait_ge(S["qt_ok"], 4 * q + 4)
                for u, (i, hp) in enumerate(UNITS):
                    if u >= 3:
                        pe.wait_ge(S["s1_max"], 32 * q + u - 3 + 1)
                    for jj in range(2):
                        r0 = 64 * jj
                        pe.matmul(ps[:, 2 * (u % 3) + jj, 0:(i + 1) * P], qt_s[r0:r0 + QROWS, hp, i * P:(i + 1) * P],
                                  kt_s[r0:r0 + QROWS, hp, 0:(i + 1) * P], start=True, stop=False)
                    for jj in range(2):
                        mm = pe.matmul(ps[:, 2 * (u % 3) + jj, i * P:(i + 1) * P], ident16[:, :], mask_qk16[:, :],
                                       start=False, stop=True)
                    mm.then_inc(S["s1_mm"], 1)
                for i in range(TPB):
                    pe.wait_ge(S["m_ok"], 4 * q + i + 1)
                    if i >= 2:
                        pe.wait_ge(S["q2_ok"], 4 * q + i - 2 + 1)
                    turned(i, 0, 6 + i % 2).then_inc(S["q2_tr"], 1)

                def scores(u):
                    k, hp = UNITS[u]
                    n = SEQ - k * P
                    if u == 0:
                        pe.wait_ge(S["q2_ok"], 4 * q + 4)
                    for jj in range(2):
                        r0 = 64 * jj
                        mm = pe.matmul(ps[:, 2 * (u % 2) + jj, 0:n], kt_s[r0:r0 + MROWS, hp, k * P:(k + 1) * P],
                                       q2_s[r0:r0 + MROWS, hp, k * P:SEQ], start=True, stop=True)
                    mm.then_inc(S["s2_mm"], 1)

                def values(u):
                    k, hp = UNITS[u]
                    pe.wait_ge(S["sel_ok"], 32 * q + u + 1)
                    for jj in range(2):
                        g, at = (2 * hp + jj) // 4, 32 * ((2 * hp + jj) % 4)
                        mm = pe.matmul(ps[at:at + 32, 4 + g, k * P:SEQ], vc[:, k, 2 * hp + jj, :],
                                       pt[:, u % NPT, jj, 0:SEQ - k * P], start=(k == 0), stop=(k == TPB - 1),
                                       skip_group_check=True)
                    mm.then_inc(S["pv_mm"], 1)

                for u in range(32):
                    if u >= 2:
                        pe.wait_ge(S["exp_ok"], 32 * q + u - 2 + 1)
                    scores(u)
                    if u >= PV_LAG:
                        values(u - PV_LAG)
                for u in range(32 - PV_LAG, 32):
                    values(u)
                pe.wait_ge(S["exp_ok"], 32 * q + 32)
                for g in range(4):
                    pe.wait_ge(S["pvs_ok"], 4 * q + g + 1)
                    for i in range(TPB):
                        mm = pe.transpose(ps[:, i, g * P:(g + 1) * P], pv_s[:, g, i * P:(i + 1) * P], ident)
                mm.then_inc(S["pv_tr"], 1)
                pe.wait_ge(S["y_ok"], q + 1)
                for i in range(TPB):
                    mm = pe.transpose(ps[:, 4, i * P:(i + 1) * P], y_tok[:, i].rearrange("p h d -> p (h d)"), ident)
                mm.then_inc(S["y_tr"], 1)
                pe.wait_ge(S["yt_ok"], q + 1)
                pe.matmul(ps[:, 5, :], pcol("proj"), y_t, start=True, stop=True).then_inc(S["proj_mm"], 1)

        def act_attention(act, c):
            with act.Fori(0, NB) as b:
                q = 4 * c["attn"] + b

                def part(i, which, src):
                    qs, ks = qk16[:, i, 0:HEADS, :], qk16[:, i, HEADS:2 * HEADS, :]
                    n, first = (3, 0) if which == 1 else (2, 3)
                    act.activation(qs[:, :, first * DH:(first + n) * DH].rearrange("p h (r d) -> p h r d", d=DH),
                                   src[:, 0:HEADS, :].unsqueeze(2).to_broadcast([P, HEADS, n, DH]), ACT.Copy)
                    at = (which - 1) * DH
                    ins = act.activation(ks[:, :, at:at + 6 * DH].rearrange("p h (r d) -> p h r d", d=3 * DH)[:, :, :, 0:DH],
                                         src[:, HEADS:2 * HEADS, :].unsqueeze(2).to_broadcast([P, HEADS, 2, DH]), ACT.Copy)
                    if which == 1:
                        ins = act.activation(ks[:, :, 5 * DH:6 * DH], src[:, HEADS:2 * HEADS, :], ACT.Copy)
                    return ins

                for i in range(TPB):
                    act.wait_ge(S["rope_ok"], 4 * q + i + 1)
                    part(i, 1, rope1[:, i % 2]).then_inc(S["part1_ok"], 1)
                    act.wait_ge(S["rest_ok"], 4 * q + i + 1)
                    part(i, 2, rope2[:, i % 2]).then_inc(S["part2_ok"], 1)
                for i in range(TPB):
                    act.wait_ge(S["k_tr"], 4 * q + i + 1)
                    act.activation(kt_s[:, :, i * P:(i + 1) * P],
                                   ps[:, 4 + i, :].bitcast(BF16).rearrange("p (a n) -> p a n", n=P),
                                   ACT.Copy).then_inc(S["kt_ok"], 1)
                for i in range(TPB):
                    act.wait_ge(S["q2_tr"], 4 * q + i + 1)
                    act.activation(q2_s[:, :, i * P:(i + 1) * P],
                                   ps[:, 6 + i % 2, :].bitcast(BF16).rearrange("p (a n) -> p a n", n=P),
                                   ACT.Copy).then_inc(S["q2_ok"], 1)
                for u, (k, hp) in enumerate(UNITS):
                    n = SEQ - k * P
                    act.wait_ge(S["s2_mm"], 32 * q + u + 1)
                    if u >= NPT:
                        act.wait_ge(S["pv_mm"], 32 * q + u - NPT + 1)
                    act.activation(pt[:, u % NPT, :, 0:n], ps[:, 2 * (u % 2):2 * (u % 2) + 2, 0:n], ACT.Exp,
                                   scale=SCALE).then_inc(S["exp_ok"], 1)
                for g in range(4):
                    act.wait_ge(S["pv_mm"], 32 * q + 24 + 2 * g + 2)
                    act.activation(pv_s[:, g, :], ps[:, 4 + g, :], ACT.Copy).then_inc(S["pvs_ok"], 1)
                act.wait_ge(S["y_tr"], q + 1)
                act.activation(y_t, ps[:, 4, :], ACT.Copy).then_inc(S["yt_ok"], 1)

        def dve_attention(dve, c):
            dve.memset(qk16, 0.0).then_inc(S["pad_ok"], 1)
            dve.wait_ge(S["pad_ok"], 2 * c["attn"] + 1)
            dve.memset(qk16[:, :, HEADS:2 * HEADS, QROWS:MROWS], 1.0)
            dve.memset(vc[:, :, :, DH:DH + 1], 1.0)
            dve.memset(vc[:, :, :, DH + 1:32], 0.0).then_inc(S["pad_ok"], 1)
            dve.wait_ge(S["pad_ok"], 2 * c["attn"] + 2)
            w = pcol("conv_c")
            with dve.Fori(0, NB) as b:
                q = 4 * c["attn"] + b
                h = ha[:, b, :]
                dve.tensor_scalar(hc, h, w[:, 2:3], None, ALU.mult).then_inc(S["conv_ok"], 1)
                for lag in (1, 2):
                    dve.wait_ge(S["conv_ok"], 2 * q + lag)
                    dve.scalar_tensor_tensor(out=hc[:, lag:SEQ], in0=ha[:, b, 0:SEQ - lag], scalar=w[:, 2 - lag:3 - lag],
                                             in1=hc[:, lag:SEQ], op0=ALU.mult,
                                             op1=ALU.add).then_inc(S["conv_ok" if lag == 1 else "hc_ok"], 1)
                cos, sin = ccol("cos"), ccol("sin")

                def rope(i):
                    dve.wait_ge(S["qkv_mm"], 4 * q + i + 1)
                    qk = ps[:, i, 0:2 * P].rearrange("p (h d) -> p h d", d=DH)
                    half = DH // 2

                    def row(table, a, n):
                        return table[:, i * DH + a:i * DH + a + n].unsqueeze(1).to_broadcast([P, 2 * HEADS, n])

                    if i >= 2:
                        dve.wait_ge(S["split_ok"], 4 * q + i - 2 + 1)
                    dve.tensor_tensor(rope1[:, i % 2], qk, row(cos, 0, DH), ALU.mult)
                    dve.tensor_tensor(rope2[:, i % 2, :, 0:half], qk[:, :, half:DH], row(sin, 0, half), ALU.mult)
                    dve.tensor_tensor(rope2[:, i % 2, :, half:DH], qk[:, :, 0:half], row(sin, half, half), ALU.mult)
                    dve.tensor_copy(vc[:, i, :, 0:DH], ps[:, i, 2 * P:3 * P].rearrange("p (h d) -> p h d", d=DH))\
                       .then_inc(S["rope_mid"], 1)
                    dve.wait_ge(S["rope_mid"], 4 * q + i + 1)
                    dve.tensor_tensor(rope1[:, i % 2], rope1[:, i % 2], rope2[:, i % 2],
                                      ALU.add).then_inc(S["rope_ok"], 1)

                def rest(i):
                    dve.wait_ge(S["part1_ok"], 4 * q + i + 1)
                    dve.tensor_tensor(rope2[:, i % 2], rope1[:, i % 2], qk16[:, i, :, 0:DH],
                                      ALU.subtract).then_inc(S["rest_ok"], 1)

                def part3(i):
                    dve.wait_ge(S["part2_ok"], 4 * q + i + 1)
                    left = rope2[:, i % 2]
                    dve.tensor_tensor(qk16[:, i, 0:HEADS, 5 * DH:6 * DH], left[:, 0:HEADS, :],
                                      qk16[:, i, 0:HEADS, 3 * DH:4 * DH], ALU.subtract)
                    dve.tensor_tensor(qk16[:, i, HEADS:2 * HEADS, 2 * DH:3 * DH], left[:, HEADS:2 * HEADS, :],
                                      qk16[:, i, HEADS:2 * HEADS, DH:2 * DH], ALU.subtract).then_inc(S["split_ok"], 1)

                rope(0)
                rope(1)
                for i in range(TPB):
                    rest(i)
                    if i >= 1:
                        part3(i - 1)
                    if 1 <= i < TPB - 1:
                        rope(i + 1)
                part3(TPB - 1)
                for i in range(TPB):
                    dve.wait_ge(S["q_tr"], 4 * q + i + 1)
                    dve.tensor_copy(qt_s[:, :, i * P:(i + 1) * P],
                                    ps[:, i, :].bitcast(BF16).rearrange("p (a n) -> p a n", n=P)).then_inc(S["qt_ok"], 1)
                for u, (i, hp) in enumerate(UNITS):
                    dve.wait_ge(S["s1_mm"], 32 * q + u + 1)
                    dve.tensor_reduce(neg_max[:, i, 2 * hp:2 * hp + 2],
                                      ps[:, 2 * (u % 3):2 * (u % 3) + 2, 0:(i + 1) * P], AX_X, ALU.max,
                                      negate=True).then_inc(S["s1_max"], 1)
                    if hp == PAIRS - 1:
                        m1 = qk16[:, i, 0:HEADS, QROWS:QROWS + 1]
                        m2 = qk16[:, i, 0:HEADS, QROWS + 1:QROWS + 2]
                        dve.wait_ge(S["s1_max"], 32 * q + u + 1)
                        dve.tensor_copy(m1, neg_max[:, i, :].unsqueeze(2)).then_inc(S["m1_ok"], 1)
                        dve.wait_ge(S["m1_ok"], 4 * q + i + 1)
                        dve.tensor_tensor(m2, neg_max[:, i, :].unsqueeze(2), m1, ALU.subtract).then_inc(S["m_ok"], 1)
                for u in range(32):
                    edge = pt[:, u % NPT, :, 0:P]
                    dve.wait_ge(S["exp_ok"], 32 * q + u + 1)
                    dve.scalar_tensor_tensor(out=edge, in0=edge, scalar=3e38,
                                             in1=ccol("tri").unsqueeze(1).to_broadcast([P, 2, P]), op0=ALU.min,
                                             op1=ALU.mult).then_inc(S["sel_ok"], 1)
                dve.wait_ge(S["pv_tr"], q + 1)
                pv = ps[:, 0:4, :].rearrange("p i (h d) -> p (i h) d", d=32)
                dve.reciprocal(rden.unsqueeze(2), pv[:, :, DH:DH + 1]).then_inc(S["rden_ok"], 1)
                dve.wait_ge(S["rden_ok"], q + 1)
                dve.tensor_tensor(y_tok.rearrange("p i h d -> p (i h) d"), pv[:, :, 0:DH],
                                  rden.unsqueeze(2).to_broadcast([P, TPB * HEADS, DH]), ALU.mult).then_inc(S["y_ok"], 1)
                dve.wait_ge(S["proj_mm"], q + 1)
                dve.tensor_tensor(hb[:, b, :], hb[:, b, :], ps[:, 5, :], ALU.add).then_inc(S["x1_ok"], 1)

        def dve_conv_d(dve, c):
            w = pcol("conv_d")
            for t in range(NB):
                dve.tensor_scalar(res[:, t, :], ha[:, t, :], w[:, 1:2], None, ALU.mult).then_inc(S["sc_a"], 1)
            for t in range(NB):
                dve.wait_ge(S["sc_a"], t + 1)
                dve.scalar_tensor_tensor(out=res[:, t, 1:SEQ], in0=ha[:, t, 0:SEQ - 1], scalar=w[:, 0:1],
                                         in1=res[:, t, 1:SEQ], op0=ALU.mult, op1=ALU.add).then_inc(S["sc_b"], 1)
            for t in range(NB):
                dve.wait_ge(S["sc_b"], t + 1)
                dve.scalar_tensor_tensor(out=res[:, t, 0:SEQ - 1], in0=ha[:, t, 1:SEQ], scalar=w[:, 2:3],
                                         in1=res[:, t, 0:SEQ - 1], op0=ALU.mult, op1=ALU.add).then_inc(S["sc_c"], 1)

        def pe_ssm(pe, c):
            for t in range(NB):
                pe.wait_ge(S["u_ok"], t + 1)
                pe.matmul(ps[0:2 * NSTATE, t, :], pcol("w_bc"), hb[:, t, :], start=True, stop=True).then_inc(S["bc_mm"], 1)
                pe.matmul(ps[0:DT_RANK, 4 + t, :], pcol("w_dt"), hb[:, t, :], start=True, stop=True).then_inc(S["t1_mm"], 1)
            for t in range(NB):
                pe.wait_ge(S["bc_ok"], t + 1)
                pe.wait_ge(S["t1_ok"], t + 1)
                pe.matmul(ps[:, t, :], pcol("w_dtp")[0:DT_RANK], t1_s[:, t, :], start=True, stop=True).then_inc(S["z_mm"], 1)
            pe.wait_ge(S["diag_ok"], 1)
            for t in range(NB):
                pe.matmul(ps[:, 4 + t, :], diag_d, ha[:, t, :], start=True, stop=False, skip_group_check=True)
            pe.wait_ge(S["z_act"], 4)

            def turn(n):
                def wait(sem, k):
                    if not isinstance(n, int) or 4 * n + k > 0:
                        pe.wait_ge(S[sem], 4 * n + k)

                for j in range(8):
                    s, t = ITEMS[j]
                    if t == 0:
                        pe.wait_ge(S[f"bc_in{s}"], 8 * n + 16)
                    wait("db_ok", j - 1)
                    pe.matmul(ps[:, j % 2, :], ones16[0:3, :], bc_row[:, s, 0, t, :], start=True,
                              stop=True).then_inc(S["bb_mm"], 1)
                    if not isinstance(n, int) or j >= 1:
                        c_row(n, j - 1, wait)
                    if not isinstance(n, int) or j >= 3:
                        sums(j - 3, wait)

            def c_row(n, j, wait):
                s, t = ITEMS[j % 8]
                wait("ch_ok", j - 1)
                pe.matmul(ps[:, 2 + j % 2, :], ones16[0:3, :], bc_row[:, s, 1, t, :], start=True,
                          stop=True).then_inc(S["cb_mm"], 1)

            def sums(j, wait):
                s, t = ITEMS[j % 8]
                wait("ch_ok", j + 1)
                pe.matmul(ps[:, 4 + t, :], ident, ch[:, s, t, :], start=False, stop=False,
                          skip_group_check=True).then_inc(S["sum_mm"], 1)

            turn(0)
            with pe.Fori(1, NSTATE // 2) as r:
                turn(2 * r)

            def last(sem, k):
                pe.wait_ge(S[sem], 4 * NSTATE + k)

            sums(-3, last)
            c_row(NSTATE, -1, last)
            sums(-2, last)
            sums(-1, last)

        def act_ssm(act, c):
            act.activation(a_neg, pcol("a_log"), ACT.Exp).then_inc(S["a_exp"], 1)
            for t in range(NB):
                act.wait_ge(S["sc_c"], t + 1)
                act.activation(hb[:, t, :], res[:, t, :], ACT.Silu).then_inc(S["u_ok"], 1)
            for t in range(NB):
                act.wait_ge(S["bc_mm"], t + 1)
                act.activation(bc_s[:, t, :], ps[0:2 * NSTATE, t, :], ACT.Identity,
                               bias=pcol("b_bc")[0:2 * NSTATE]).then_inc(S["bc_ok"], 1)
                act.wait_ge(S["t1_mm"], t + 1)
                act.activation(t1_s[:, t, :], ps[0:DT_RANK, 4 + t, :], ACT.Identity,
                               bias=pcol("b_dt")[0:DT_RANK]).then_inc(S["t1_ok"], 1)
            for t in range(NB):
                act.wait_ge(S["bc_ok"], t + 1)
                act.activation(bc16[:, 0, t], bc_s[:, t, :], ACT.Copy).then_inc(S["bc_part1"], 1)
            for t in range(NB):
                act.wait_ge(S["bc_rest"], t + 1)
                act.activation(bc16[:, 1, t], bc_s[:, t, :], ACT.Copy).then_inc(S["bc_part2"], 1)
            for t in range(NB):
                act.wait_ge(S["z_mm"], t + 1)
                act.activation(soft_a[:, t, :], ps[:, t, :], ACT.Abs, bias=pcol("b_dtp"))
                act.activation(soft_r[:, t, :], ps[:, t, :], ACT.Relu, bias=pcol("b_dtp")).then_inc(S["z_act"], 1)
            for t in range(NB):
                act.wait_ge(S["z_act"], t + 1)
                act.activation(soft_e[:, t, :], soft_a[:, t, :], ACT.Exp, scale=-1.0).then_inc(S["soft_exp"], 1)
            for t in range(NB):
                act.wait_ge(S["soft_u"], t + 1)
                act.activation(soft_l[:, t, :], soft_a[:, t, :], ACT.Ln).then_inc(S["soft_log"], 1)
            act.wait_ge(S["a_ok"], 1)
            act.wait_ge(S["dt_ok"], 4)
            act.wait_ge(S["bc_split"], 4)

            def decay(r, s):
                act.activation(da[:, s], dt_s[:, :, :], ACT.Exp, scale=a_neg.rearrange("p (r s) -> p s r", s=2)[:, s, :].unsqueeze(2)[:, r, :]).then_inc(S["da_ok"], 1)

            for s in range(2):
                decay(0, s)
            with act.Fori(1, NSTATE // 2) as r:
                n = 2 * r
                for s in range(2):
                    act.wait_ge(S["scan_ok"], 4 * (n + s) - 4)
                    decay(r, s)

        def dve_ssm(dve, c):
            dve.wait_ge(S["a_exp"], 1)
            dve.tensor_scalar(a_neg, a_neg, -1.0, None, ALU.mult).then_inc(S["a_ok"], 1)
            dve.tensor_scalar(diag_d, ident, pcol("dcoef"), None, ALU.mult).then_inc(S["diag_ok"], 1)
            for t in range(NB):
                dve.wait_ge(S["bc_part1"], t + 1)
                dve.tensor_tensor(bc_s[:, t, :], bc_s[:, t, :], bc16[:, 0, t], ALU.subtract).then_inc(S["bc_rest"], 1)
            for t in range(NB):
                dve.wait_ge(S["bc_part2"], t + 1)
                dve.tensor_tensor(bc16[:, 2, t], bc_s[:, t, :], bc16[:, 1, t], ALU.subtract).then_inc(S["bc_split"], 1)
            for t in range(NB):
                dve.wait_ge(S["soft_exp"], t + 1)
                dve.tensor_scalar(soft_a[:, t, :], soft_e[:, t, :], 1.0, None, ALU.add).then_inc(S["soft_u"], 1)
            for t in range(NB):
                dve.wait_ge(S["soft_u"], t + 1)
                dve.scalar_tensor_tensor(out=soft_e[:, t, :], in0=soft_a[:, t, :], scalar=-1.0, in1=soft_e[:, t, :],
                                         op0=ALU.add, op1=ALU.subtract).then_inc(S["soft_d"], 1)
            for t in range(NB):
                dve.wait_ge(S["soft_log"], t + 1)
                dve.wait_ge(S["soft_d"], t + 1)
                dve.tensor_tensor(soft_l[:, t, :], soft_l[:, t, :], soft_e[:, t, :], ALU.subtract).then_inc(S["soft_s"], 1)
            for t in range(NB):
                dve.wait_ge(S["soft_s"], t + 1)
                dve.tensor_tensor(dt_s[:, t, :], soft_l[:, t, :], soft_r[:, t, :], ALU.add).then_inc(S["dt_ok"], 1)
            for t in range(NB):
                dve.wait_ge(S["dt_ok"], t + 1)
                dve.tensor_tensor(dtx[:, t, :], dt_s[:, t, :], ha[:, t, :], ALU.mult).then_inc(S["dtx_ok"], 1)
            dve.wait_ge(S["dtx_ok"], 4)
            dve.wait_ge(S["bc_out"], 16)

            def inputs(n, j):
                s, t = ITEMS[j]
                dve.wait_ge(S["bb_mm"], 4 * n + j + 1)
                dve.tensor_tensor(db[:, s, t, :], dtx[:, t, :], ps[:, j % 2, :], ALU.mult).then_inc(S["db_ok"], 1)

            def states(n, j):
                s, t = ITEMS[j % 8]
                if t == 0:
                    dve.wait_ge(S["da_ok"], n + s + 1)
                dve.wait_ge(S["db_ok"], 4 * n + j + 1)
                dve.tensor_tensor_scan(hst[:, s, t, :], da[:, s, t, :], db[:, s, t, :], 0.0, ALU.mult,
                                       ALU.add).then_inc(S["scan_ok"], 1)

            def outputs(n, j):
                s, t = ITEMS[j % 8]
                dve.wait_ge(S["cb_mm"], 4 * n + j + 1)
                dve.wait_ge(S["scan_ok"], 4 * n + j + 1)
                dve.tensor_tensor(ch[:, s, t, :], hst[:, s, t, :], ps[:, 2 + j % 2, :],
                                  ALU.mult).then_inc(S["ch_ok"], 1)

            def turn(n, first):
                for j in range(8):
                    inputs(n, j)
                    if j >= 1 or not first:
                        states(n, j - 1)
                    if j >= 2 or not first:
                        outputs(n, j - 2)

            turn(0, True)
            with dve.Fori(1, NSTATE // 2) as r:
                turn(2 * r, False)
            states(NSTATE, -1)
            outputs(NSTATE, -2)
            outputs(NSTATE, -1)

        def sp_ssm(sp, c):
            sp.wait_ge(S["bc_split"], 4)
            sp.dma_start(bc_dram.rearrange("a n (t q) -> n a t q", t=NB), bc16).then_inc(S["bc_out"], 16)
            sp.wait_ge(S["bc_out"], 16)
            rows = bc_dram.rearrange("a (w r s) (t q) -> s r a w t q", w=2, s=2, t=NB)
            for s in range(2):
                sp.dma_start(bc_row[:, s], rows[s, 0]).then_inc(S[f"bc_in{s}"], 16)
            with sp.Fori(1, NSTATE // 2) as r:
                n = 2 * r
                for s in range(2):
                    sp.wait_ge(S["cb_mm"], 4 * (n + s) - 4)
                    sp.dma_start(bc_row[:, s], rows[s, r]).then_inc(S[f"bc_in{s}"], 16)

        for extra in ("sc_a", "sc_b", "sc_c", "soft_exp", "soft_d", "soft_s"):
            S[extra] = sem(extra)

        block_ = ctx.enter_context(nc.Block())
        x_tok = res[:, :, :].rearrange("p b (i d) -> p (b i) d", d=P)

        def x_ready(c):
            def wait(eng, t):
                if c["prev"] == "":
                    eng.wait_ge(S["x_cp"], t + 1)
                elif c["prev"] == "A":
                    eng.wait_ge(S["added"], c["added"])
                else:
                    eng.wait_ge(S["x_ok"], 4 * c["x_upd"] - 4 + t + 1)
            return wait

        end = dict(count, prev=stages[-1:])
        order = [(kind, dict(c, prev=stages[i - 1:i] if i else "")) for i, (kind, c) in enumerate(order)]

        @block_.sync
        def _(sp):
            sp.dma_start(x_tok, x_in.rearrange("(i p) d -> p i d", p=P)).then_inc(S["x_in"], 16)
            sp.dma_start(con[:, :], consts).then_inc(S["params_in"], 16)
            sp.dma_start(par[:, :], params).then_inc(S["params_in"], 16)
            for kind, c in order:
                def slot_free(sp, s, c=c):
                    if c["prev"] in ("A", "C"):
                        sp.wait_ge(S["gated_ok"], c["added"] - 4 + 4 * s)
                    elif c["prev"] == "B":
                        sp.wait_ge(S["ln_out"], 4 * (c["ln"] - 1 - 2 * (1 - s)))
                    elif c["prev"] == "D":
                        sp.wait_ge(S["gated_ok"], c["added"])
                if kind == "A":
                    sp_moe(sp, c, pack_a, A_COLS, EXPERTS0, slot_free)
                elif kind == "B":
                    sp_layers(sp, c, slot_free)
                elif kind == "C":
                    sp_moe(sp, c, pack_c, C_COLS, EXPERTS1, slot_free)
                elif kind == "D":
                    sp_ssm(sp, c)
            for t in range(NB):
                sp.wait_ge(S["cp_out"], t + 1)
                sp.dma_start(out.rearrange("(i p) d -> p i d", p=P)[:, TPB * t:TPB * t + TPB, :],
                             x_tok[:, TPB * t:TPB * t + TPB, :]).then_inc(S["x_out"], 16)
            sp.wait_ge(S["x_out"], 64)

        @block_.tensor
        def _(pe):
            pe.wait_ge(S["params_in"], 32)
            pe.wait_ge(S["x_in"], 16)
            for t in range(NB):
                for i in range(TPB):
                    mm = pe.transpose(ps[:, t, i * P:(i + 1) * P], x_tok[:, TPB * t + i, :], ident)
                mm.then_inc(S["x_tr"], 1)
            pe.wait_ge(S["consts16"], 1)
            for kind, c in order:
                n = c["ln"]
                pe_ln(pe, n, x, x_ready(c))
                if kind == "A":
                    pe_router(pe, n, c["moe_call"], pcol("gate"), EXPERTS0)
                    pe.wait_ge(S["gate_cp"], c["moe_call"] + 1)
                    pe_experts0(pe, c)
                elif kind == "B":
                    pe_layers(pe, c)
                    last = n + 2 * LAYERS
                    pe_ln(pe, last + 1, ha, lambda pe, t: pe.wait_ge(S["ln_out"], 4 * last + t + 1))
                elif kind == "C":
                    pe_ln(pe, n + 1, hb, lambda pe, t: pe.wait_ge(S["ln_out"], 4 * n + t + 1))
                    pe.wait_ge(S["ln_out"], 4 * n + 8)
                    pe_attention(pe, c)
                    pe_ln(pe, n + 2, hb, lambda pe, t: pe.wait_ge(S["x1_ok"], 4 * c["attn"] + 4))
                    pe_router(pe, n + 2, c["moe_call"], pcol("router"), EXPERTS1)
                    pe.wait_ge(S["gate_cp"], c["moe_call"] + 1)
                    pe_experts1(pe, c)
                else:
                    pe_ssm(pe, c)
            for t in range(NB):
                x_ready(end)(pe, t)
                for i in range(TPB):
                    mm = pe.transpose(ps[:, t, i * P:(i + 1) * P], x[:, t, i * P:(i + 1) * P], ident)
                mm.then_inc(S["tr_out"], 1)

        @block_.scalar
        def _(act):
            act.wait_ge(S["params_in"], 32)
            exp_call = 0
            for kind, c in order:
                n = c["ln"]
                act_ln(act, n)
                if kind == "A":
                    act_router(act, exp_call)
                    exp_call += 1
                    act_experts0(act, c)
                elif kind == "B":
                    act_layers(act, c)
                    act_ln(act, n + 2 * LAYERS + 1)
                elif kind == "C":
                    act_ln(act, n + 1)
                    act_attention(act, c)
                    act_ln(act, n + 2)
                    act_experts1(act, c)
                else:
                    act_ssm(act, c)

        @block_.vector
        def _(dve):
            dve.wait_ge(S["params_in"], 32)
            dve.tensor_copy(ident16[:, :], ident)
            dve.memset(ones16[:, :], 1.0)
            dve.tensor_copy(mask_qk16[:, :], ccol("mask_qk")).then_inc(S["consts16"], 1)
            for t in range(NB):
                dve.wait_ge(S["x_tr"], t + 1)
                dve.tensor_copy(x[:, t, :], ps[:, t, :]).then_inc(S["x_cp"], 1)
            exp_call = 0
            for kind, c in order:
                n = c["ln"]
                x_ready(c)(dve, NB - 1)
                if kind == "A":
                    dve_ln(dve, n, x, ha)
                    dve_router(dve, c["moe_call"], exp_call, EXPERTS0, 2)
                    exp_call += 1
                    dve_experts0(dve, c, x)
                elif kind == "B":
                    dve_ln(dve, n, x, ha)
                    dve.memset(v_aug[:, :, :, P:P + 1], 1.0)
                    dve_layers(dve, c)
                    last = n + 2 * LAYERS + 1
                    dve_ln(dve, last, ha, hb, (c["lns"] + 2 * LAYERS, pcol("gf"), pcol("bef")))
                    for t in range(NB):
                        dve.wait_ge(S["ln_out"], 4 * last + t + 1)
                        dve.tensor_tensor(x[:, t, :], x[:, t, :], hb[:, t, :], ALU.add).then_inc(S["x_ok"], 1)
                elif kind == "C":
                    dve_ln(dve, n, x, hb)
                    dve.wait_ge(S["ln_out"], 4 * n + 4)
                    dve_ln(dve, n + 1, hb, ha, (c["lns"], pcol("ln1_w"), pcol("ln1_b")))
                    dve.wait_ge(S["ln_out"], 4 * n + 8)
                    dve_attention(dve, c)
                    dve.wait_ge(S["x1_ok"], 4 * c["attn"] + 4)
                    dve_ln(dve, n + 2, hb, ha, (c["lns"] + 1, pcol("ln2_w"), pcol("ln2_b")))
                    dve_router(dve, c["moe_call"], None, EXPERTS1, 1)
                    dve_experts1(dve, c, hb)
                    dve.wait_ge(S["added"], c["added"] + NB * EXPERTS1)
                    for t in range(NB):
                        dve.scalar_tensor_tensor(out=x[:, t, :], in0=hb[:, t, :], scalar=0.5, in1=x[:, t, :],
                                                 op0=ALU.mult, op1=ALU.add).then_inc(S["x_ok"], 1)
                else:
                    dve_ln(dve, n, x, ha)
                    dve.wait_ge(S["ln_out"], 4 * n + 4)
                    dve_conv_d(dve, c)
                    dve_ssm(dve, c)
                    dve.wait_ge(S["sum_mm"], NB * NSTATE)
                    for t in range(NB):
                        dve.tensor_tensor(x[:, t, :], x[:, t, :], ps[:, 4 + t, :], ALU.add).then_inc(S["x_ok"], 1)
            for t in range(NB):
                dve.wait_ge(S["tr_out"], t + 1)
                dve.tensor_copy(x_tok[:, TPB * t:TPB * t + TPB, :].rearrange("p i d -> p (i d)"),
                                ps[:, t, :]).then_inc(S["cp_out"], 1)


def shape_constants():
    at, n = columns(CONSTS)
    c = np.zeros((P, n), np.float32)

    def put(name, v):
        c[:, at[name][0]:at[name][1]] = v

    i = np.arange(P)
    put("ident", np.eye(P))
    put("mean", 1.0 / P)
    put("block", i[:, None] // DH == i[None, :] // DH)
    put("head_sum", i[:, None] // DH == i[None, :32])
    put("head_spread", i[:, None] % 32 == i[None, :] // DH)
    inv = (np.float32(1.0) / np.float32(10000.0) ** (np.arange(0, DH, 2, dtype=np.float32) / np.float32(DH))).astype(np.float32)
    angle = (np.arange(SEQ, dtype=np.float32)[:, None] * inv[None, :]).astype(np.float32)
    angle = np.concatenate([angle, angle], 1).astype(np.float64)
    sign = np.where(np.arange(DH) < DH // 2, -1.0, 1.0)
    put("cos", np.cos(angle).reshape(TPB, P, DH).transpose(1, 0, 2).reshape(P, -1))
    put("sin", (np.sin(angle) * sign).reshape(TPB, P, DH).transpose(1, 0, 2).reshape(P, -1))
    put("desc8", 8.0 - np.arange(8))
    put("desc4", 4.0 - np.arange(4))
    put("mask_qk", np.where(i[None, :] <= i[:, None], 0.0, NEG))
    put("tri", i[None, :] >= i[:, None])
    put("eps", 1e-5)
    put("tiny", 1e-6)
    return c


def kernel(**inputs):
    import numpy as _np
    import concourse.bacc as _bacc
    from concourse.bass_utils import run_bass_kernel_spmd as _run

    a = {k: _np.asarray(v) for k, v in inputs.items()}

    def chunks(w):
        e, r, n = w.shape
        return w.reshape(e, r // P, P, n).transpose(0, 2, 1, 3).reshape(e, P, -1)

    def cols(v):
        return v.reshape(v.shape[0], -1, P).transpose(0, 2, 1)

    g = lambda n: a["L0_attn_" + n]
    pack_a = _np.concatenate([a["L0_ffn_w1"], chunks(a["L0_ffn_w2"]), cols(a["L0_ffn_b1"]), cols(a["L0_ffn_b2"])], 2)
    kv_bias = _np.concatenate([g("bk"), g("bv")], 1)[:, None, :]
    pack_b = _np.concatenate(
        [g("Wq"), g("Wk"), g("Wv"), g("Wo"), g("W1"), chunks(g("W2")), _np.broadcast_to(kv_bias, (LAYERS, P, 2 * P))]
        + [cols(g(n)) for n in ("bq", "bo", "c1", "c2", "g1", "be1", "g2", "be2")], 2)
    pack_c = _np.concatenate([a["L1_ffn_expert_wv"], chunks(a["L1_ffn_expert_proj"])], 2)
    at, n = columns(PARAMS)
    params = _np.zeros((P, n), _np.float32)

    def put(name, v):
        v = v.reshape(v.shape[0], -1)
        params[0:v.shape[0], at[name][0]:at[name][1]] = v

    put("gate", a["L0_ffn_gate_w"].T)
    put("gf", g("gf"))
    put("bef", g("bef"))
    for k in ("ln1_w", "ln1_b", "ln2_w", "ln2_b"):
        put(k, a["L1_ffn_" + k])
    put("conv_c", a["L1_ffn_conv_w"])
    put("wqkv", a["L1_ffn_attn_w"])
    put("proj", a["L1_ffn_proj_w"])
    put("router", a["L1_ffn_router_w"])
    put("conv_d", a["L1_attn_conv_w"].T)
    put("w_bc", a["L1_attn_W_bc"])
    put("b_bc", a["L1_attn_b_bc"])
    put("w_dt", a["L1_attn_W_dt"])
    put("b_dt", a["L1_attn_b_dt"])
    put("w_dtp", a["L1_attn_W_dtp"])
    put("b_dtp", a["L1_attn_b_dtp"])
    put("a_log", a["L1_attn_A_log"])
    put("dcoef", a["L1_attn_Dcoeff"])
    nc = _bacc.Bacc("TRN2", target_bir_lowering=False, num_devices=1)
    arrays = {"x_in": a["L0_attn_x"].reshape(NB * SEQ, P), "pack_a": pack_a, "pack_b": pack_b, "pack_c": pack_c,
              "params_dram": params, "consts_dram": shape_constants()}
    arrays = {k: _np.ascontiguousarray(v) for k, v in arrays.items()}
    args = [nc.dram_tensor(k, v.shape, F32, kind="ExternalInput").ap() for k, v in arrays.items()]
    args.append(nc.dram_tensor("out_dram", (NB * SEQ, P), F32, kind="ExternalOutput").ap())
    build(nc, *args)
    r = _run(nc, [arrays], core_ids=[0])
    return r.results[0]["out_dram"].reshape(NB, SEQ, P)
```

```python
from contextlib import ExitStack

import numpy as np
import concourse.bass as bass
from concourse import mybir

ALU = mybir.AluOpType
ACT = mybir.ActivationFunctionType
F32 = mybir.dt.float32
BF16 = mybir.dt.bfloat16
F32R = mybir.dt.float32r
AX_X = mybir.AxisListType.X

P = 128
NB, SEQ = 4, 512
TILES = NB * SEQ // P
TPB = SEQ // P
F = 512
FC = F // P
EXPERTS0, EXPERTS1 = 8, 4
LAYERS = 8
HEADS, DH = 16, 8
PAIRS = HEADS // 2
NSTATE, DT_RANK = 16, 8
NEG = -1e30

A_W1, A_W2, A_B1, A_B2, A_COLS = 0, 512, 1024, 1028, 1029
B_WQ, B_WKV, B_WO, B_W1, B_W2, B_KVB, B_VEC = 0, 128, 384, 512, 1024, 1536, 1792
B_BQ, B_BO, B_C1, B_C2, B_G1, B_BE1, B_G2, B_BE2, B_COLS = (B_VEC + i for i in (0, 1, 2, 6, 7, 8, 9, 10, 11))
C_WV, C_PROJ, C_COLS = 0, 1024, 1536
A_PIECES, C_PIECES = 2, 3
SLOT_COLS = -(-B_COLS // 8) * 8

PARAMS = [
    ("gate", EXPERTS0), ("gf", 1), ("bef", 1), ("ln1_w", 1), ("ln1_b", 1), ("ln2_w", 1), ("ln2_b", 1),
    ("conv_c", 3), ("wqkv", 3 * P), ("proj", P), ("router", EXPERTS1), ("conv_d", 3), ("w_bc", 2 * NSTATE),
    ("b_bc", 1), ("w_dt", DT_RANK), ("b_dt", 1), ("w_dtp", P), ("b_dtp", 1), ("a_log", NSTATE), ("dcoef", 1),
]
CONSTS = [("ident", P), ("mean", P), ("block", P), ("head_sum", 32), ("head_spread", P),
          ("cos", TPB * DH), ("sin", TPB * DH), ("desc8", 8),
          ("desc4", 4), ("mask_qk", P), ("tri", P), ("eps", 1), ("tiny", 1)]


def columns(table):
    at, out = 0, {}
    for name, n in table:
        out[name] = (at, at + n)
        at += n
    return out, at


def build(nc, x_in, pack_a, pack_b, pack_c, params, consts, out, stages="ABACDC"):
    par_at, par_cols = columns(PARAMS)
    con_at, con_cols = columns(CONSTS)
    with ExitStack() as ctx:
        offset = {}

        def sb(name, shape, dt=F32):
            t = ctx.enter_context(nc.sbuf_tensor(name, shape, dt))
            offset[name] = nc.sbuf_base - int(np.prod(shape[1:])) * (2 if dt == BF16 else 4)
            return t

        def over(name, below, at, shape):
            return nc.alloc_sbuf_tensor_at(name, [P] + shape, F32R, offset=offset[below] + 4 * at)

        gates_dram = nc.dram_tensor("gates_dram", (4, P, P), F32, kind="Internal").ap()
        bc_dram = nc.dram_tensor("bc_dram", (3, 2 * NSTATE, NB * SEQ), BF16, kind="Internal").ap()

        par = sb("par", [P, par_cols])
        con = sb("con", [P, con_cols])
        mask_qk16 = sb("mask_qk16", [P, P], BF16)
        ident16 = sb("ident16", [P, P], BF16)
        ones16 = sb("ones16", [P, P], BF16)
        x = sb("x", [P, NB, SEQ])
        ha = sb("ha", [P, NB, SEQ])
        hb = sb("hb", [P, NB, SEQ])
        res = sb("res", [P, NB, SEQ])
        xc = sb("xc", [P, NB, SEQ])
        sq = sb("sq", [P, NB, SEQ])
        rstd = sb("rstd", [P, NB, SEQ])
        wslot = sb("wslot", [P, 2, SLOT_COLS])
        gate_bc = sb("gate_bc", [P, 2, TILES, P])
        arena = sb("arena", [P, 17 * 1024])
        ps = ctx.enter_context(nc.psum_tensor("ps", [P, 8, 512], F32))

        def pcol(name):
            a, b = par_at[name]
            return par[:, a:b]

        def ccol(name):
            a, b = con_at[name]
            return con[:, a:b]

        def view(at, *shape):
            n = int(np.prod(shape))
            v = arena[:, at:at + n]
            if len(shape) == 1:
                return v
            names = "abcd"[:len(shape)]
            return v.rearrange(f"p ({' '.join(names)}) -> p {' '.join(names)}",
                               **{k: s for k, s in zip(names[1:], shape[1:])})

        def view16(at, *shape):
            n = int(np.prod(shape))
            names = "abcd"[:len(shape)]
            return arena[:, at:at + n // 2].bitcast(BF16).rearrange(
                f"p ({' '.join(names)}) -> p {' '.join(names)}", **{k: s for k, s in zip(names[1:], shape[1:])})

        ident, mean_w, block = ccol("ident"), ccol("mean"), ccol("block")
        eps, tiny = ccol("eps"), ccol("tiny")

        gated = view(4096, 2, SEQ)
        silu = view(5120, 2, SEQ)
        hid32 = view(0, FC, SEQ)
        hid_hi = [over(f"hid_hi{i}", "arena", 9856 + 2048 * i, [FC, SEQ]) for i in range(2)]
        hid_lo = [over(f"hid_lo{i}", "arena", at, [FC, SEQ]) for i, at in enumerate((2048, 6144))]
        x_hi, x_lo = over("x_hi", "res", 0, [NB, SEQ]), over("x_lo", "arena", 13952, [NB, SEQ])
        w_hi = [over("w_hi0", "xc", 0, [SLOT_COLS]), over("w_hi1", "sq", 0, [SLOT_COLS])]
        w_lo = [over(f"w_lo{s}", "wslot", s * SLOT_COLS, [SLOT_COLS]) for s in range(2)]
        rt = [view(8192 + 128 * i, TILES, 8) for i in range(8)]
        rs = [view(8192 + 1024 + 16 * i, TILES) for i in range(8)]
        gate_t = view(8192 + 1536, P)
        q_exp, q_relu = view(0, NB, SEQ), view(2048, NB, SEQ)
        qf = view(4096, NB, SEQ)
        kf = view(6144, NB, TPB, P)
        v_aug = view(8192, NB, TPB, P + 1)
        kv_bd, ks_h = view(10368, NB, P), view(10880, NB, 32)
        hid_b = view(11392, 2, FC, SEQ)
        k_exp, k_relu = view(0, NB, TPB, P), view(2048, NB, TPB, P)
        rz, att = view(0, SEQ), view(2048, NB, SEQ)
        hc, hc_all = view(0, SEQ), res
        qk16 = view16(512, TPB, 2 * HEADS, 64)
        vc = view(4608, TPB, HEADS, 32)
        kt_s, qt_s, q2_s = view16(6656, PAIRS, SEQ), view16(8704, PAIRS, SEQ), view16(10752, PAIRS, SEQ)
        pv_s = view(6656, TPB, SEQ)
        y_tok = view(8704, TPB, HEADS, DH)
        y_t = view(9216, SEQ)
        NPT = 4
        pt = view(12800, NPT, 2, SEQ)
        rope1, rope2 = view(12800, 2, 2 * HEADS, DH), view(13312, 2, 2 * HEADS, DH)
        rden = view(16896, TPB * HEADS)
        neg_max = view(16960, TPB, HEADS)
        dt_s, dtx = xc, sq
        da = view(0, 2, NB, SEQ)
        db = view(4096, 2, NB, SEQ)
        hst = view(8192, 2, NB, SEQ)
        ch = view(12288, 2, NB, SEQ)
        bc_row = sb("bc_row", [3, 2, 2, NB, SEQ], BF16)
        bc_s = view(0, NB, SEQ)[0:2 * NSTATE]
        bc16 = view16(12288, 3, NB, SEQ)[0:2 * NSTATE]
        t1_s = view(2048, NB, SEQ)[0:DT_RANK]
        soft_a, soft_e, soft_l, soft_r = view(4096, NB, SEQ), view(6144, NB, SEQ), view(8192, NB, SEQ), view(10240, NB, SEQ)
        a_neg = view(16384, NSTATE)
        diag_d = view(16400, P)

        names = """consts_in params_in x_in0 x_in1 x_in2 x_in3 w_in0 w_in1 gates_out gate_in0 gate_in1 x_out bc_out bc_in0 bc_in1 x_tr x_cp
            consts16 ln_mean ln_xc ln_sq ln_var ln_log ln_rs ln_scaled ln_out logits lg_sub lg_exp gate_ok
            gate_tr gate_cp dve_chain x_hi_ok x_parts w_hi_ok w_parts hi_ok val_ok up_mm hid_ok down_mm
            gated_ok added gv_mm silu_ok q_mm q_act qf_ok kv_mm kv_ok k_act kf_ok kvs_mm kvbd_ok den_mm
            den_ok att_mm num_ok rz_ok z_bc att_ok o_mm res1_ok ff1_mm gelu_ok ff2_mm res2_ok x_ok conv_all
            hc_ok qkv_mm rope_mid rope_ok part1_ok rest_ok part2_ok split_ok k_tr q_tr kt_ok qt_ok m1_ok
            m_ok sel_ok s1_mm s1_max q2_tr q2_ok s2_mm exp_ok pv_mm pvs_ok pv_tr rden_ok y_ok y_tr yt_ok
            proj_mm x1_ok pad_ok conv_ok tap_mid tap_left tap_right u_ok bc_mm bc_ok bc_part1 bc_rest
            bc_part2 bc_split t1_mm t1_ok z_mm z_act soft_exp soft_u soft_d soft_log soft_s dt_ok dtx_ok
            a_exp a_ok diag_ok bb_mm cb_mm da_ok db_ok scan_ok ch_ok sum_mm tr_out cp_out""".split()
        S = {n: ctx.enter_context(nc.semaphore(n)) for n in names}

        order = []
        count = dict(ln=0, lns=0, x_upd=0, added=0, moe1=0, moe_call=0, w=0, g=0, up=0, attn=0, parts=0)
        for kind in stages:
            order.append((kind, dict(count)))
            if kind == "A":
                count["ln"] += 1
                count["moe_call"] += 1
                count["w"] += EXPERTS0
                count["g"] += EXPERTS0
                count["parts"] += A_PIECES * EXPERTS0
                count["added"] += NB * EXPERTS0
                count["up"] += NB * EXPERTS0
            elif kind == "B":
                count["ln"] += 2 + 2 * LAYERS
                count["lns"] += 1 + 2 * LAYERS
                count["w"] += LAYERS
                count["x_upd"] += 1
            elif kind == "C":
                count["ln"] += 3
                count["lns"] += 2
                count["moe_call"] += 1
                count["w"] += EXPERTS1
                count["g"] += EXPERTS1
                count["parts"] += C_PIECES * EXPERTS1
                count["added"] += NB * EXPERTS1
                count["moe1"] += NB * EXPERTS1
                count["attn"] += 1
                count["x_upd"] += 1
            elif kind == "D":
                count["ln"] += 1
                count["x_upd"] += 1

        def pe_ln(pe, n, src, ready):
            for t in range(NB):
                ready(pe, t)
                pe.matmul(ps[:, t, :], mean_w, src[:, t, :], start=True, stop=True).then_inc(S["ln_mean"], 1)
            for t in range(NB):
                pe.wait_ge(S["ln_sq"], 4 * n + t + 1)
                pe.matmul(ps[:, 4 + t, :], mean_w, sq[:, t, :], start=True, stop=True).then_inc(S["ln_var"], 1)

        def act_ln(act, n):
            act.preload_act_table_set("natural_log_exp_and_others")
            for t in range(NB):
                act.wait_ge(S["ln_xc"], 4 * n + t + 1)
                act.activation(sq[:, t, :], xc[:, t, :], ACT.Square).then_inc(S["ln_sq"], 1)

            def root(t):
                act.wait_ge(S["ln_log"], 4 * n + t + 1)
                act.activation(rstd[:, t, :], rstd[:, t, :], ACT.Exp, scale=-0.5).then_inc(S["ln_rs"], 1)

            for t in range(NB):
                act.wait_ge(S["ln_var"], 4 * n + t + 1)
                act.activation(rstd[:, t, :], ps[:, 4 + t, :], ACT.Ln, bias=eps).then_inc(S["ln_log"], 1)
                root(t)

        def dve_ln(dve, n, src, dst, affine=None):
            for t in range(NB):
                dve.wait_ge(S["ln_mean"], 4 * n + t + 1)
                dve.tensor_tensor(xc[:, t, :], src[:, t, :], ps[:, t, :], ALU.subtract).then_inc(S["ln_xc"], 1)

            def shift(t):
                m, g, b = affine
                dve.wait_ge(S["ln_scaled"], 4 * m + t + 1)
                dve.tensor_scalar(dst[:, t, :], dst[:, t, :], b, None, ALU.add).then_inc(S["ln_out"], 1)

            for t in range(NB):
                dve.wait_ge(S["ln_rs"], 4 * n + t + 1)
                if affine is None:
                    dve.tensor_tensor(dst[:, t, :], xc[:, t, :], rstd[:, t, :], ALU.mult).then_inc(S["ln_out"], 1)
                else:
                    dve.scalar_tensor_tensor(out=dst[:, t, :], in0=xc[:, t, :], scalar=affine[1], in1=rstd[:, t, :],
                                             op0=ALU.mult, op1=ALU.mult).then_inc(S["ln_scaled"], 1)
                    shift(t)

        def pe_router(pe, n, call, w, experts):
            pe.wait_ge(S["ln_out"], 4 * n + 4)
            for i in range(TILES):
                mm = pe.matmul(ps[:, 0, experts * i:experts * (i + 1)],
                               ha[:, i // TPB, (i % TPB) * P:(i % TPB + 1) * P], w, start=True, stop=True)
            mm.then_inc(S["logits"], 1)
            pe.wait_ge(S["gate_ok"], call + 1)
            pe.transpose(ps[0:TILES * experts, 1, 0:P], gates_view(experts), ident).then_inc(S["gate_tr"], 1)

        def gates_view(experts):
            return arena[:, 8192 + 128 * 7:8192 + 128 * 7 + TILES * experts]

        def act_router(act, call):
            if call is not None:
                act.wait_ge(S["lg_sub"], call + 1)
                act.activation(rt[1], rt[0], ACT.Exp).then_inc(S["lg_exp"], 1)

        chain = [0]

        def dve_router(dve, call, exp_call, experts, top):
            def link(ins):
                chain[0] += 1
                ins.then_inc(S["dve_chain"], 1)
                dve.wait_ge(S["dve_chain"], chain[0])

            def bc(v):
                return v.unsqueeze(2).to_broadcast([P, TILES, experts])

            def tile3(i):
                return arena[:, 8192 + 128 * i:8192 + 128 * i + TILES * experts].rearrange("p (t e) -> p t e", e=experts)

            desc = ccol("desc8" if experts == 8 else "desc4").unsqueeze(1).to_broadcast([P, TILES, experts])
            dve.wait_ge(S["logits"], call + 1)
            lg = ps[:, 0, 0:TILES * experts].rearrange("p (t e) -> p t e", e=experts)
            val = tile3(0)
            if top == 2:
                link(dve.tensor_reduce(rs[0], lg, AX_X, ALU.max))
                dve.tensor_tensor(val, lg, bc(rs[0]), ALU.subtract).then_inc(S["lg_sub"], 1)
                dve.wait_ge(S["lg_exp"], exp_call + 1)
                e = tile3(1)
                link(dve.tensor_reduce(rs[0], e, AX_X, ALU.add))
                link(dve.reciprocal(rs[0], rs[0]))
                link(dve.tensor_tensor(val, e, bc(rs[0]), ALU.mult))
            else:
                link(dve.tensor_copy(val, lg))

            def first_max(src, best, hot):
                link(dve.tensor_reduce(best, src, AX_X, ALU.max))
                link(dve.tensor_tensor(tile3(3), src, bc(best), ALU.is_equal))
                link(dve.tensor_tensor(tile3(3), tile3(3), desc, ALU.mult))
                link(dve.tensor_reduce(rs[3], tile3(3), AX_X, ALU.max))
                link(dve.tensor_tensor(hot, tile3(3), bc(rs[3]), ALU.is_equal))

            first_max(val, rs[1], tile3(4))
            out_g = tile3(7)
            if top == 1:
                dve.tensor_copy(out_g, tile3(4)).then_inc(S["gate_ok"], 1)
            else:
                link(dve.scalar_tensor_tensor(out=tile3(5), in0=tile3(4), scalar=-2.0, in1=val, op0=ALU.mult, op1=ALU.add))
                first_max(tile3(5), rs[2], tile3(6))
                link(dve.tensor_tensor(tile3(4), tile3(4), tile3(6), ALU.add))
                link(dve.tensor_tensor(tile3(4), tile3(4), val, ALU.mult))
                link(dve.tensor_tensor(rs[4], rs[1], rs[2], ALU.add))
                link(dve.tensor_scalar(rs[4], rs[4], 1e-9, None, ALU.add))
                link(dve.reciprocal(rs[4], rs[4]))
                dve.scalar_tensor_tensor(out=out_g, in0=tile3(4), scalar=0.5, in1=bc(rs[4]),
                                         op0=ALU.mult, op1=ALU.mult).then_inc(S["gate_ok"], 1)
            dve.wait_ge(S["gate_tr"], call + 1)
            dve.tensor_copy(gate_t[0:TILES * experts], ps[0:TILES * experts, 1, 0:P]).then_inc(S["gate_cp"], 1)

        def sp_gates(sp, call, experts):
            sp.wait_ge(S["gate_cp"], call + 1)
            sp.dma_start(gates_dram[call, 0:TILES * experts, :], gate_t[0:TILES * experts]).then_inc(S["gates_out"], 16)
            sp.wait_ge(S["gates_out"], 16 * call + 16)

        def gate_src(call, experts, r, s):
            rows = gates_dram[call, 0:TILES * experts, :].rearrange("(t r s) p -> s r t p", r=experts // 2, s=2)
            return rows[s, r].partition_broadcast(P)


        ITEMS = [(s, t) for s in range(2) for t in range(NB)]

        def sp_moe(sp, c, pack, cols, experts, slot_free):
            pairs = pack.rearrange("(r s) p n -> s r p n", s=2)
            for s in range(2):
                slot_free(sp, s)
                sp.dma_start(wslot[:, s, 0:cols], pack[s]).then_inc(S[f"w_in{s}"], 16)
            sp_gates(sp, c["moe_call"], experts)
            for s in range(2):
                sp.dma_start(gate_bc[:, s], gate_src(c["moe_call"], experts, 0, s)).then_inc(S[f"gate_in{s}"], 16)
            with sp.Fori(1, experts // 2) as r:
                e = 2 * r
                for s in range(2):
                    sp.wait_ge(S["gated_ok"], c["added"] + 4 * e + 4 * (s - 1))
                    sp.dma_start(wslot[:, s, 0:cols], pairs[s, r]).then_inc(S[f"w_in{s}"], 16)
                    sp.dma_start(gate_bc[:, s], gate_src(c["moe_call"], experts, r, s)).then_inc(S[f"gate_in{s}"], 16)

        def w_count(c, e):
            return 8 * c["w"] + 8 * e + 16

        def products(pe, bank, w_at, s, hi, lo, start, stop):
            w1, w2 = (w[s][:, w_at:w_at + P] for w in (w_hi, w_lo))
            pe.matmul(ps[:, bank, :], w1, hi, start=start, stop=False)
            pe.matmul(ps[:, bank, :], w1, lo, start=False, stop=False)
            return pe.matmul(ps[:, bank, :], w2, hi, start=False, stop=stop)

        def pe_down(pe, base, item, k, w_at):
            s, t = ITEMS[item]
            if k == 0 and item >= 3:
                pe.wait_ge(S["gated_ok"], base + max(item - 4, 0) + 1)
            pe.wait_ge(S["hid_ok"], 4 * (base + item) + k + 1)
            mm = products(pe, 4 + item % 4, w_at + k * P, s, hid_hi[item % 2][:, k, :],
                          hid_lo[item % 2][:, k, :], k == 0, k == FC - 1)
            if k == FC - 1:
                mm.then_inc(S["down_mm"], 1)

        def pe_blocks(pe, base, up, w_at):
            for item in range(9):
                for k in range(FC):
                    if item < 8:
                        up(item, k)
                    if item:
                        pe_down(pe, base, item - 1, k, w_at)

        def pe_experts0(pe, c):
            pe.wait_ge(S["x_parts"], 4 * c["moe_call"] + 4)
            with pe.Fori(0, EXPERTS0 // 2) as r:
                e = 2 * r
                base = c["added"] + 4 * e

                def up(item, k):
                    s, t = ITEMS[item]
                    if t == 0 and k == 0:
                        pe.wait_ge(S["w_parts"], c["parts"] + A_PIECES * (e + s + 1))
                    if item:
                        pe.wait_ge(S["hi_ok"], 4 * (base + item - 1) + k + 1)
                    products(pe, k, A_W1 + k * P, s, x_hi[:, t, :], x_lo[:, t, :], True, True)\
                        .then_inc(S["up_mm"], 1)

                pe_blocks(pe, base, up, A_W2)
                pe.wait_ge(S["gated_ok"], base + 7)

        def act_experts0(act, c):
            with act.Fori(0, EXPERTS0 // 2) as r:
                e = 2 * r
                for item, (s, t) in enumerate(ITEMS):
                    n = 4 * (c["added"] + 4 * e + item)
                    for k in range(FC):
                        act.wait_ge(S["up_mm"], 4 * (c["up"] + 4 * e + item) + k + 1)
                        bias = wslot[:, s, A_B1 + k:A_B1 + k + 1]
                        act.activation(hid_hi[item % 2][:, k, :], ps[:, k, :], ACT.Gelu, bias=bias)
                        if item:
                            act.wait_ge(S["hid_ok"], n - 4 + k + 1)
                        act.activation(hid32[:, k, :], ps[:, k, :], ACT.Gelu, bias=bias).then_inc(S["hi_ok"], 1)

        def dve_gate(dve, c, e, item, bias, dst):
            s, t = ITEMS[item]
            if t == 0:
                dve.wait_ge(S[f"gate_in{s}"], 8 * c["g"] + 8 * e + 16)
            g = gate_bc[:, s, TPB * t:TPB * t + TPB, :].rearrange("p a b -> p (a b)")
            dve.wait_ge(S["down_mm"], c["added"] + 4 * e + item + 1)
            if bias:
                ins = dve.scalar_tensor_tensor(out=gated[:, item % 2, :], in0=ps[:, 4 + item % 4, :],
                                               scalar=wslot[:, s, A_B2:A_B2 + 1], in1=g, op0=ALU.add, op1=ALU.mult)
            else:
                ins = dve.tensor_tensor(gated[:, item % 2, :], ps[:, 4 + item % 4, :], g, ALU.mult)
            ins.then_inc(S["gated_ok"], 1)
            dve.wait_ge(S["gated_ok"], c["added"] + 4 * e + item + 1)
            dve.tensor_tensor(dst[:, t, :], dst[:, t, :], gated[:, item % 2, :], ALU.add).then_inc(S["added"], 1)

        def act_split(act, n, src):
            for t in range(NB):
                act.wait_ge(S["ln_out"], 4 * n + t + 1)
                act.activation(x_hi[:, t, :], src[:, t, :], ACT.Copy).then_inc(S["x_hi_ok"], 1)

        def dve_split(dve, src, call):
            for t in range(NB):
                dve.wait_ge(S["x_hi_ok"], 4 * call + t + 1)
                dve.tensor_tensor(x_lo[:, t, :], src[:, t, :], x_hi[:, t, :].bitcast(F32),
                                  ALU.subtract).then_inc(S["x_parts"], 1)

        def dve_weights(dve, c, pieces, e, s, piece):
            cut = slice(SEQ * piece, SEQ * piece + SEQ)
            if piece == 0:
                dve.wait_ge(S[f"w_in{s}"], w_count(c, e))
            dve.tensor_copy(w_hi[s][:, cut], wslot[:, s, cut]).then_inc(S["w_hi_ok"], 1)
            dve.wait_ge(S["w_hi_ok"], c["parts"] + pieces * (e + s) + piece + 1)
            dve.tensor_tensor(w_lo[s][:, cut], wslot[:, s, cut], w_hi[s][:, cut].bitcast(F32),
                              ALU.subtract).then_inc(S["w_parts"], 1)

        def dve_low(dve, n, item, k):
            dve.wait_ge(S["hi_ok"], n)
            dve.tensor_tensor(hid_lo[item % 2][:, k, :], hid32[:, k, :], hid_hi[item % 2][:, k, :].bitcast(F32),
                              ALU.subtract).then_inc(S["hid_ok"], 1)

        def dve_experts0(dve, c, dst):
            def turn(e, more):
                for item in range(8):
                    for k in range(FC):
                        dve_low(dve, 4 * (c["added"] + 4 * e + item) + k + 1, item, k)
                    if item:
                        dve_gate(dve, c, e, item - 1, True, dst)
                    if item in (0, 1):
                        dve_weights(dve, c, A_PIECES, e, 1, item)
                    if item in (5, 6) and more:
                        dve_weights(dve, c, A_PIECES, e + 2, 0, item - 5)
                dve_gate(dve, c, e, 7, True, dst)

            with dve.Fori(0, EXPERTS0 // 2 - 1) as r:
                turn(2 * r, True)
            turn(EXPERTS0 - 2, False)

        def pe_experts1(pe, c):
            pe.wait_ge(S["x_parts"], 4 * c["moe_call"] + 4)
            with pe.Fori(0, EXPERTS1 // 2) as r:
                e = 2 * r
                base = c["added"] + 4 * e

                def up(item, k):
                    s, t = ITEMS[item]
                    if t == 0 and k == 0:
                        pe.wait_ge(S["w_parts"], c["parts"] + C_PIECES * (e + s + 1))
                    if 4 * item + k >= 2:
                        pe.wait_ge(S["val_ok"], 4 * (c["moe1"] + 4 * e + item) + k - 2 + 1)
                    bank = 2 * (k % 2)
                    products(pe, bank, C_WV + k * P, s, x_hi[:, t, :], x_lo[:, t, :], True, True)
                    products(pe, bank + 1, C_WV + F + k * P, s, x_hi[:, t, :], x_lo[:, t, :], True, True)\
                        .then_inc(S["gv_mm"], 1)

                pe_blocks(pe, base, up, C_PROJ)
                pe.wait_ge(S["gated_ok"], base + 7)

        def act_experts1(act, c):
            with act.Fori(0, EXPERTS1 // 2) as r:
                e = 2 * r
                first = 4 * (c["moe1"] + 4 * e)

                def upper(n):
                    item, k = n // FC, n % FC
                    act.wait_ge(S["val_ok"], first + n + 1)
                    act.activation(hid_hi[item % 2][:, k, :], hid32[:, k, :], ACT.Copy).then_inc(S["hi_ok"], 1)

                for n in range(8 * FC):
                    act.wait_ge(S["gv_mm"], first + n + 1)
                    act.activation(silu[:, n % 2, :], ps[:, 2 * (n % 2), :], ACT.Silu).then_inc(S["silu_ok"], 1)
                    if n:
                        upper(n - 1)
                upper(8 * FC - 1)

        def dve_experts1(dve, c, dst):
            def turn(e, more):
                first = 4 * (c["moe1"] + 4 * e)
                hi = 4 * (c["added"] + 4 * e)

                def low(n):
                    dve_low(dve, hi + n + 1, n // FC, n % FC)

                for n in range(8 * FC):
                    item, k = n // FC, n % FC
                    dve.wait_ge(S["silu_ok"], first + n + 1)
                    if item:
                        dve.wait_ge(S["hid_ok"], hi + n - FC + 1)
                    dve.tensor_tensor(hid32[:, k, :], silu[:, n % 2, :], ps[:, 2 * (n % 2) + 1, :],
                                      ALU.mult).then_inc(S["val_ok"], 1)
                    if n >= 1:
                        low(n - 1)
                    if k == 1 and item:
                        dve_gate(dve, c, e, item - 1, False, dst)
                    if n in (FC, 2 * FC, 3 * FC):
                        dve_weights(dve, c, C_PIECES, e, 1, n // FC - 1)
                    if n in (5 * FC, 6 * FC, 7 * FC) and more:
                        dve_weights(dve, c, C_PIECES, e + 2, 0, n // FC - 5)
                low(8 * FC - 1)
                dve_gate(dve, c, e, 7, False, dst)

            with dve.Fori(0, EXPERTS1 // 2 - 1) as r:
                turn(2 * r, True)
            turn(EXPERTS1 - 2, False)

        ATT_BANK = [5, 6, 7, 4]

        def pe_layers(pe, c):
            n0 = c["ln"] + 1
            with pe.Fori(0, LAYERS // 2) as r:
                l = 2 * r
                for s in range(2):
                    m = 4 * (l + s)
                    w = wslot[:, s, :]
                    nd = n0 + 2 * (l + s)
                    pe.wait_ge(S[f"w_in{s}"], w_count(c, l))
                    for b in range(NB):
                        pe.wait_ge(S["ln_out"], 4 * nd - 4 + b + 1)
                        pe.matmul(ps[:, b, :], w[:, B_WQ:B_WQ + P], ha[:, b, :], start=True,
                                  stop=True).then_inc(S["q_mm"], 1)
                    for b in range(NB):
                        bank = 4 + 2 * (b % 2)
                        if b >= 2:
                            pe.wait_ge(S["kv_ok"], m + b - 2 + 1)
                        for i in range(TPB):
                            mm = pe.matmul(ps[:, bank + i // 2, 256 * (i % 2):256 * (i % 2) + 256],
                                           ha[:, b, i * P:(i + 1) * P], w[:, B_WKV:B_WKV + 2 * P],
                                           start=True, stop=True)
                        mm.then_inc(S["kv_mm"], 1)
                    for b in range(NB):
                        pe.wait_ge(S["kf_ok"], m + b + 1)
                        pe.wait_ge(S["qf_ok"], m + b + 1)
                        for i in range(TPB):
                            mm = pe.matmul(ps[:, b, 0:P + 1], kf[:, b, i, :], v_aug[:, b, i, :],
                                           start=(i == 0), stop=(i == TPB - 1))
                        mm.then_inc(S["kvs_mm"], 1)
                    for b in range(NB):
                        pe.wait_ge(S["kvbd_ok"], m + b + 1)
                        mm = pe.matmul(ps[32 * b:32 * b + 32, 4, :], ks_h[:, b, :], qf[:, b, :], start=True, stop=True,
                                       skip_group_check=True)
                    mm.then_inc(S["den_mm"], 1)
                    for b in range(NB):
                        if b == NB - 1:
                            pe.wait_ge(S["den_ok"], l + s + 1)
                        pe.matmul(ps[:, ATT_BANK[b], :], kv_bd[:, b, :], qf[:, b, :], start=True,
                                  stop=True).then_inc(S["att_mm"], 1)
                    pe.wait_ge(S["rz_ok"], l + s + 1)
                    for b in range(NB):
                        pe.matmul(ps[:, b, :], ccol("head_spread")[32 * b:32 * b + 32], rz[32 * b:32 * b + 32, :],
                                  start=True, stop=True).then_inc(S["z_bc"], 1)
                    for b in range(NB):
                        pe.wait_ge(S["att_ok"], m + b + 1)
                        pe.matmul(ps[:, b, :], w[:, B_WO:B_WO + P], att[:, b, :], start=True,
                                  stop=True).then_inc(S["o_mm"], 1)
                    pe_ln(pe, nd, res, lambda pe, t: pe.wait_ge(S["res1_ok"], m + t + 1))

                    def ff1(b):
                        pe.wait_ge(S["ln_out"], 4 * nd + b + 1)
                        for k in range(FC):
                            if b:
                                pe.wait_ge(S["gelu_ok"], 4 * m + 4 * (b - 1) + k + 1)
                            pe.matmul(ps[:, k, :], w[:, B_W1 + k * P:B_W1 + (k + 1) * P], hb[:, b, :],
                                      start=True, stop=True).then_inc(S["ff1_mm"], 1)

                    def ff2(b):
                        pe.wait_ge(S["ln_rs"], 4 * nd + b + 1)
                        for k in range(FC):
                            pe.wait_ge(S["gelu_ok"], 4 * m + 4 * b + k + 1)
                            mm = pe.matmul(ps[:, 4 + b, :], w[:, B_W2 + k * P:B_W2 + (k + 1) * P],
                                           hid_b[:, b % 2, k, :], start=(k == 0), stop=(k == FC - 1))
                        mm.then_inc(S["ff2_mm"], 1)

                    ff1(0)
                    for b in range(1, NB):
                        ff1(b)
                        ff2(b - 1)
                    ff2(NB - 1)
                    pe_ln(pe, nd + 1, res, lambda pe, t: pe.wait_ge(S["res2_ok"], m + t + 1))

        def act_layers(act, c):
            n0 = c["ln"] + 1
            with act.Fori(0, LAYERS // 2) as r:
                l = 2 * r
                for s in range(2):
                    m = 4 * (l + s)
                    w = wslot[:, s, :]
                    nd = n0 + 2 * (l + s)
                    for b in range(NB):
                        act.wait_ge(S["q_mm"], m + b + 1)
                        act.activation(q_exp[:, b, :], ps[:, b, :], ACT.Exp, bias=w[:, B_BQ:B_BQ + 1])
                        act.activation(q_relu[:, b, :], ps[:, b, :], ACT.Relu,
                                       bias=w[:, B_BQ:B_BQ + 1]).then_inc(S["q_act"], 1)
                    for b in range(NB):
                        act.wait_ge(S["kv_ok"], m + b + 1)
                        act.activation(k_exp[:, b], kf[:, b], ACT.Exp)
                        act.activation(k_relu[:, b], kf[:, b], ACT.Relu).then_inc(S["k_act"], 1)
                    act.wait_ge(S["den_mm"], l + s + 1)
                    act.activation(rz, ps[:, 4, :], ACT.Identity, bias=tiny).then_inc(S["den_ok"], 1)
                    for b in range(NB):
                        act.wait_ge(S["att_mm"], m + b + 1)
                        act.activation(att[:, b, :], ps[:, ATT_BANK[b], :], ACT.Copy).then_inc(S["num_ok"], 1)
                    act_ln(act, nd)
                    for b in range(NB):
                        for k in range(FC):
                            act.wait_ge(S["ff1_mm"], 4 * m + 4 * b + k + 1)
                            act.activation(hid_b[:, b % 2, k, :], ps[:, k, :], ACT.Gelu,
                                           bias=w[:, B_C1 + k:B_C1 + k + 1]).then_inc(S["gelu_ok"], 1)
                    act_ln(act, nd + 1)

        def dve_layers(dve, c):
            n0, m0 = c["ln"] + 1, c["lns"]
            with dve.Fori(0, LAYERS // 2) as r:
                l = 2 * r
                for s in range(2):
                    m = 4 * (l + s)
                    w = wslot[:, s, :]
                    nd, na = n0 + 2 * (l + s), m0 + 2 * (l + s)
                    for b in range(NB):
                        dve.wait_ge(S["q_act"], m + b + 1)
                        dve.scalar_tensor_tensor(out=qf[:, b, :], in0=q_exp[:, b, :], scalar=1.0,
                                                 in1=q_relu[:, b, :], op0=ALU.min, op1=ALU.add).then_inc(S["qf_ok"], 1)
                    bias = w[:, B_KVB:B_KVB + 2 * P].unsqueeze(1).to_broadcast([P, 4, 2 * P])

                    def keys(b):
                        dve.wait_ge(S["k_act"], m + b + 1)
                        dve.scalar_tensor_tensor(out=kf[:, b], in0=k_exp[:, b], scalar=1.0, in1=k_relu[:, b],
                                                 op0=ALU.min, op1=ALU.add).then_inc(S["kf_ok"], 1)

                    for b in range(NB):
                        bank = 4 + 2 * (b % 2)
                        kv = ps[:, bank:bank + 2, :].rearrange("p a (i n) -> p (a i) n", i=2)
                        dve.wait_ge(S["kv_mm"], m + b + 1)
                        dve.tensor_tensor(kf[:, b], kv[:, :, 0:P], bias[:, :, 0:P], ALU.add)
                        dve.tensor_tensor(v_aug[:, b, :, 0:P], kv[:, :, P:2 * P], bias[:, :, P:2 * P],
                                          ALU.add).then_inc(S["kv_ok"], 1)
                        if b >= 2:
                            keys(b - 2)
                    keys(2)
                    keys(3)
                    for b in range(NB):
                        dve.wait_ge(S["kvs_mm"], m + b + 1)
                        dve.tensor_tensor(kv_bd[:, b, :], ps[:, b, 0:P], block, ALU.mult)
                        dve.tensor_scalar(ks_h[:, b, :], ccol("head_sum"), ps[:, b, P:P + 1], None,
                                          ALU.mult).then_inc(S["kvbd_ok"], 1)
                    dve.wait_ge(S["den_ok"], l + s + 1)
                    dve.reciprocal(rz, rz).then_inc(S["rz_ok"], 1)
                    for b in range(NB):
                        dve.wait_ge(S["z_bc"], m + b + 1)
                        dve.wait_ge(S["num_ok"], m + b + 1)
                        dve.tensor_tensor(att[:, b, :], att[:, b, :], ps[:, b, :],
                                          ALU.mult).then_inc(S["att_ok"], 1)
                    for b in range(NB):
                        dve.wait_ge(S["o_mm"], m + b + 1)
                        dve.scalar_tensor_tensor(out=res[:, b, :], in0=ps[:, b, :], scalar=w[:, B_BO:B_BO + 1],
                                                 in1=ha[:, b, :], op0=ALU.add, op1=ALU.add).then_inc(S["res1_ok"], 1)
                    dve_ln(dve, nd, res, hb, (na, w[:, B_G1:B_G1 + 1], w[:, B_BE1:B_BE1 + 1]))
                    for b in range(NB):
                        dve.wait_ge(S["ff2_mm"], m + b + 1)
                        dve.scalar_tensor_tensor(out=res[:, b, :], in0=ps[:, 4 + b, :], scalar=w[:, B_C2:B_C2 + 1],
                                                 in1=hb[:, b, :], op0=ALU.add, op1=ALU.add).then_inc(S["res2_ok"], 1)
                    dve_ln(dve, nd + 1, res, ha, (na + 1, w[:, B_G2:B_G2 + 1], w[:, B_BE2:B_BE2 + 1]))

        def sp_layers(sp, c, slot_free):
            pairs = pack_b.rearrange("(r s) p n -> s r p n", s=2)
            n0 = c["ln"] + 1
            for s in range(2):
                slot_free(sp, s)
                sp.dma_start(wslot[:, s, 0:B_COLS], pack_b[s]).then_inc(S[f"w_in{s}"], 16)
            with sp.Fori(1, LAYERS // 2) as r:
                l = 2 * r
                for s in range(2):
                    sp.wait_ge(S["ln_out"], 4 * (n0 + 2 * (l + s) - 4) + 8)
                    sp.dma_start(wslot[:, s, 0:B_COLS], pairs[s, r]).then_inc(S[f"w_in{s}"], 16)

        SCALE = DH ** -0.5
        QROWS = 6 * DH
        MROWS = QROWS + 2
        UNITS = [(i, hp) for i in range(TPB) for hp in range(PAIRS)]
        DOWN = list(reversed(range(TPB)))
        MAX_UNITS = [(i, hp) for i in DOWN for hp in range(PAIRS)]
        PV_LAG = 3

        def pe_attention(pe, c):
            pe.wait_ge(S["pad_ok"], 2 * c["attn"] + 2)
            with pe.Fori(0, NB) as b:
                q = 4 * c["attn"] + b
                pe.wait_ge(S["hc_ok"], q + 1)
                for i in range(TPB):
                    pe.matmul(ps[:, i, 0:3 * P], hc[:, i * P:(i + 1) * P], pcol("wqkv"), start=True,
                              stop=True).then_inc(S["qkv_mm"], 1)

                def turned(i, kind, bank):
                    to = ps[:, bank, :].bitcast(BF16)
                    for hp in range(PAIRS):
                        at = qk16[:, i, kind * HEADS + 2 * hp:kind * HEADS + 2 * hp + 2, :].rearrange("p h d -> p (h d)")
                        mm = pe.transpose(to[:, hp * P:(hp + 1) * P], at, ident16[:, :])
                    return mm

                for i in range(TPB):
                    pe.wait_ge(S["split_ok"], 4 * q + i + 1)
                    turned(i, 1, 4 + i).then_inc(S["k_tr"], 1)
                    turned(i, 0, i).then_inc(S["q_tr"], 1)
                pe.wait_ge(S["kt_ok"], 4 * q + 4)
                pe.wait_ge(S["qt_ok"], 4 * q + 4)
                def queries_again(at):
                    pe.wait_ge(S["m_ok"], 4 * q + at + 1)
                    if at >= 2:
                        pe.wait_ge(S["q2_ok"], 4 * q + at - 2 + 1)
                    turned(DOWN[at], 0, 6 + at % 2).then_inc(S["q2_tr"], 1)

                for u, (i, hp) in enumerate(MAX_UNITS):
                    if u >= 3:
                        pe.wait_ge(S["s1_max"], 32 * q + u - 3 + 1)
                    for jj in range(2):
                        r0 = 64 * jj
                        pe.matmul(ps[:, 2 * (u % 3) + jj, 0:(i + 1) * P], qt_s[r0:r0 + QROWS, hp, i * P:(i + 1) * P],
                                  kt_s[r0:r0 + QROWS, hp, 0:(i + 1) * P], start=True, stop=False)
                    for jj in range(2):
                        mm = pe.matmul(ps[:, 2 * (u % 3) + jj, i * P:(i + 1) * P], ident16[:, :], mask_qk16[:, :],
                                       start=False, stop=True)
                    mm.then_inc(S["s1_mm"], 1)
                    if u > PAIRS and hp == PAIRS - 1:
                        queries_again(u // PAIRS - 1)
                queries_again(TPB - 1)

                def scores(u):
                    k, hp = UNITS[u]
                    n = SEQ - k * P
                    if u == 0:
                        pe.wait_ge(S["q2_ok"], 4 * q + 4)
                    for jj in range(2):
                        r0 = 64 * jj
                        mm = pe.matmul(ps[:, 2 * (u % 2) + jj, 0:n], kt_s[r0:r0 + MROWS, hp, k * P:(k + 1) * P],
                                       q2_s[r0:r0 + MROWS, hp, k * P:SEQ], start=True, stop=True)
                    mm.then_inc(S["s2_mm"], 1)

                def values(u):
                    k, hp = UNITS[u]
                    pe.wait_ge(S["sel_ok"], 32 * q + u + 1)
                    for jj in range(2):
                        g, at = (2 * hp + jj) // 4, 32 * ((2 * hp + jj) % 4)
                        mm = pe.matmul(ps[at:at + 32, 4 + g, k * P:SEQ], vc[:, k, 2 * hp + jj, :],
                                       pt[:, u % NPT, jj, 0:SEQ - k * P], start=(k == 0), stop=(k == TPB - 1),
                                       skip_group_check=True)
                    mm.then_inc(S["pv_mm"], 1)

                for u in range(32):
                    if u >= 2:
                        pe.wait_ge(S["exp_ok"], 32 * q + u - 2 + 1)
                    scores(u)
                    if u >= PV_LAG:
                        values(u - PV_LAG)
                for u in range(32 - PV_LAG, 32):
                    values(u)
                pe.wait_ge(S["exp_ok"], 32 * q + 32)
                for g in range(4):
                    pe.wait_ge(S["pvs_ok"], 4 * q + g + 1)
                    for i in range(TPB):
                        mm = pe.transpose(ps[:, i, g * P:(g + 1) * P], pv_s[:, g, i * P:(i + 1) * P], ident)
                mm.then_inc(S["pv_tr"], 1)
                pe.wait_ge(S["y_ok"], q + 1)
                for i in range(TPB):
                    mm = pe.transpose(ps[:, 4, i * P:(i + 1) * P], y_tok[:, i].rearrange("p h d -> p (h d)"), ident)
                mm.then_inc(S["y_tr"], 1)
                pe.wait_ge(S["yt_ok"], q + 1)
                pe.matmul(ps[:, 5, :], pcol("proj"), y_t, start=True, stop=True).then_inc(S["proj_mm"], 1)

        def act_attention(act, c):
            with act.Fori(0, NB) as b:
                q = 4 * c["attn"] + b

                def part(i, which, src):
                    qs, ks = qk16[:, i, 0:HEADS, :], qk16[:, i, HEADS:2 * HEADS, :]
                    n, first = (3, 0) if which == 1 else (2, 3)
                    act.activation(qs[:, :, first * DH:(first + n) * DH].rearrange("p h (r d) -> p h r d", d=DH),
                                   src[:, 0:HEADS, :].unsqueeze(2).to_broadcast([P, HEADS, n, DH]), ACT.Copy)
                    at = (which - 1) * DH
                    ins = act.activation(ks[:, :, at:at + 6 * DH].rearrange("p h (r d) -> p h r d", d=3 * DH)[:, :, :, 0:DH],
                                         src[:, HEADS:2 * HEADS, :].unsqueeze(2).to_broadcast([P, HEADS, 2, DH]), ACT.Copy)
                    if which == 1:
                        ins = act.activation(ks[:, :, 5 * DH:6 * DH], src[:, HEADS:2 * HEADS, :], ACT.Copy)
                    return ins

                act.wait_ge(S["conv_all"], q + 1)
                act.activation(hc, hc_all[:, b, :], ACT.Copy).then_inc(S["hc_ok"], 1)
                for i in range(TPB):
                    act.wait_ge(S["rope_ok"], 4 * q + i + 1)
                    part(i, 1, rope1[:, i % 2]).then_inc(S["part1_ok"], 1)
                    act.wait_ge(S["rest_ok"], 4 * q + i + 1)
                    part(i, 2, rope2[:, i % 2]).then_inc(S["part2_ok"], 1)
                for i in range(TPB):
                    act.wait_ge(S["k_tr"], 4 * q + i + 1)
                    act.activation(kt_s[:, :, i * P:(i + 1) * P],
                                   ps[:, 4 + i, :].bitcast(BF16).rearrange("p (a n) -> p a n", n=P),
                                   ACT.Copy).then_inc(S["kt_ok"], 1)
                for at, i in enumerate(DOWN):
                    act.wait_ge(S["q2_tr"], 4 * q + at + 1)
                    act.activation(q2_s[:, :, i * P:(i + 1) * P],
                                   ps[:, 6 + at % 2, :].bitcast(BF16).rearrange("p (a n) -> p a n", n=P),
                                   ACT.Copy).then_inc(S["q2_ok"], 1)
                for u, (k, hp) in enumerate(UNITS):
                    n = SEQ - k * P
                    act.wait_ge(S["s2_mm"], 32 * q + u + 1)
                    if u >= NPT:
                        act.wait_ge(S["pv_mm"], 32 * q + u - NPT + 1)
                    act.activation(pt[:, u % NPT, :, 0:n], ps[:, 2 * (u % 2):2 * (u % 2) + 2, 0:n], ACT.Exp,
                                   scale=SCALE).then_inc(S["exp_ok"], 1)
                for g in range(4):
                    act.wait_ge(S["pv_mm"], 32 * q + 24 + 2 * g + 2)
                    act.activation(pv_s[:, g, :], ps[:, 4 + g, :], ACT.Copy).then_inc(S["pvs_ok"], 1)
                act.wait_ge(S["y_tr"], q + 1)
                act.activation(y_t, ps[:, 4, :], ACT.Copy).then_inc(S["yt_ok"], 1)

        def pool_conv(pool, c):
            w = pcol("conv_c")
            for b in range(NB):
                q = 4 * c["attn"] + b
                pool.wait_ge(S["ln_out"], 4 * c["ln"] + 4 + b + 1)
                h, to = ha[:, b, :], hc_all[:, b, :]
                pool.tensor_scalar(to, h, w[:, 2:3], None, ALU.mult)
                for lag, tap in ((1, xc), (2, sq)):
                    pool.tensor_scalar(tap[:, b, :], h, w[:, 2 - lag:3 - lag], None, ALU.mult)\
                        .then_inc(S["conv_ok"], 1)
                for lag, tap in ((1, xc), (2, sq)):
                    pool.wait_ge(S["conv_ok"], 3 * q + 1 + lag)
                    pool.tensor_tensor(to[:, lag:SEQ], to[:, lag:SEQ], tap[:, b, 0:SEQ - lag],
                                       ALU.add).then_inc(S["conv_ok" if lag == 1 else "conv_all"], 1)

        def dve_attention(dve, c):
            dve.memset(qk16, 0.0).then_inc(S["pad_ok"], 1)
            dve.wait_ge(S["pad_ok"], 2 * c["attn"] + 1)
            dve.memset(qk16[:, :, HEADS:2 * HEADS, QROWS:MROWS], 1.0)
            dve.memset(vc[:, :, :, DH:DH + 1], 1.0)
            dve.memset(vc[:, :, :, DH + 1:32], 0.0).then_inc(S["pad_ok"], 1)
            dve.wait_ge(S["pad_ok"], 2 * c["attn"] + 2)
            with dve.Fori(0, NB) as b:
                q = 4 * c["attn"] + b
                cos, sin = ccol("cos"), ccol("sin")

                def rope(i):
                    dve.wait_ge(S["qkv_mm"], 4 * q + i + 1)
                    qk = ps[:, i, 0:2 * P].rearrange("p (h d) -> p h d", d=DH)
                    half = DH // 2

                    def row(table, a, n):
                        return table[:, i * DH + a:i * DH + a + n].unsqueeze(1).to_broadcast([P, 2 * HEADS, n])

                    if i >= 2:
                        dve.wait_ge(S["split_ok"], 4 * q + i - 2 + 1)
                    dve.tensor_tensor(rope1[:, i % 2], qk, row(cos, 0, DH), ALU.mult)
                    dve.tensor_tensor(rope2[:, i % 2, :, 0:half], qk[:, :, half:DH], row(sin, 0, half), ALU.mult)
                    dve.tensor_tensor(rope2[:, i % 2, :, half:DH], qk[:, :, 0:half], row(sin, half, half), ALU.mult)
                    dve.tensor_copy(vc[:, i, :, 0:DH], ps[:, i, 2 * P:3 * P].rearrange("p (h d) -> p h d", d=DH))\
                       .then_inc(S["rope_mid"], 1)
                    dve.wait_ge(S["rope_mid"], 4 * q + i + 1)
                    dve.tensor_tensor(rope1[:, i % 2], rope1[:, i % 2], rope2[:, i % 2],
                                      ALU.add).then_inc(S["rope_ok"], 1)

                def rest(i):
                    dve.wait_ge(S["part1_ok"], 4 * q + i + 1)
                    dve.tensor_tensor(rope2[:, i % 2], rope1[:, i % 2], qk16[:, i, :, 0:DH],
                                      ALU.subtract).then_inc(S["rest_ok"], 1)

                def part3(i):
                    dve.wait_ge(S["part2_ok"], 4 * q + i + 1)
                    left = rope2[:, i % 2]
                    dve.tensor_tensor(qk16[:, i, 0:HEADS, 5 * DH:6 * DH], left[:, 0:HEADS, :],
                                      qk16[:, i, 0:HEADS, 3 * DH:4 * DH], ALU.subtract)
                    dve.tensor_tensor(qk16[:, i, HEADS:2 * HEADS, 2 * DH:3 * DH], left[:, HEADS:2 * HEADS, :],
                                      qk16[:, i, HEADS:2 * HEADS, DH:2 * DH], ALU.subtract).then_inc(S["split_ok"], 1)

                rope(0)
                rope(1)
                for i in range(TPB):
                    rest(i)
                    if i >= 1:
                        part3(i - 1)
                    if 1 <= i < TPB - 1:
                        rope(i + 1)
                part3(TPB - 1)
                for i in range(TPB):
                    dve.wait_ge(S["q_tr"], 4 * q + i + 1)
                    dve.tensor_copy(qt_s[:, :, i * P:(i + 1) * P],
                                    ps[:, i, :].bitcast(BF16).rearrange("p (a n) -> p a n", n=P)).then_inc(S["qt_ok"], 1)
                for u, (i, hp) in enumerate(MAX_UNITS):
                    dve.wait_ge(S["s1_mm"], 32 * q + u + 1)
                    dve.tensor_reduce(neg_max[:, i, 2 * hp:2 * hp + 2],
                                      ps[:, 2 * (u % 3):2 * (u % 3) + 2, 0:(i + 1) * P], AX_X, ALU.max,
                                      negate=True).then_inc(S["s1_max"], 1)
                    if hp == PAIRS - 1:
                        m1 = qk16[:, i, 0:HEADS, QROWS:QROWS + 1]
                        m2 = qk16[:, i, 0:HEADS, QROWS + 1:QROWS + 2]
                        dve.wait_ge(S["s1_max"], 32 * q + u + 1)
                        dve.tensor_copy(m1, neg_max[:, i, :].unsqueeze(2)).then_inc(S["m1_ok"], 1)
                        dve.wait_ge(S["m1_ok"], 4 * q + u // PAIRS + 1)
                        dve.tensor_tensor(m2, neg_max[:, i, :].unsqueeze(2), m1, ALU.subtract).then_inc(S["m_ok"], 1)
                for u in range(32):
                    edge = pt[:, u % NPT, :, 0:P]
                    dve.wait_ge(S["exp_ok"], 32 * q + u + 1)
                    dve.scalar_tensor_tensor(out=edge, in0=edge, scalar=3e38,
                                             in1=ccol("tri").unsqueeze(1).to_broadcast([P, 2, P]), op0=ALU.min,
                                             op1=ALU.mult).then_inc(S["sel_ok"], 1)
                dve.wait_ge(S["pv_tr"], q + 1)
                pv = ps[:, 0:4, :].rearrange("p i (h d) -> p (i h) d", d=32)
                dve.reciprocal(rden.unsqueeze(2), pv[:, :, DH:DH + 1]).then_inc(S["rden_ok"], 1)
                dve.wait_ge(S["rden_ok"], q + 1)
                dve.tensor_tensor(y_tok.rearrange("p i h d -> p (i h) d"), pv[:, :, 0:DH],
                                  rden.unsqueeze(2).to_broadcast([P, TPB * HEADS, DH]), ALU.mult).then_inc(S["y_ok"], 1)
                dve.wait_ge(S["proj_mm"], q + 1)
                dve.tensor_tensor(hb[:, b, :], hb[:, b, :], ps[:, 5, :], ALU.add).then_inc(S["x1_ok"], 1)

        def dve_conv_d(dve, c):
            w = pcol("conv_d")
            for t in range(NB):
                dve.tensor_scalar(res[:, t, :], ha[:, t, :], w[:, 1:2], None, ALU.mult).then_inc(S["tap_mid"], 1)
            for t in range(NB):
                dve.wait_ge(S["tap_mid"], t + 1)
                dve.scalar_tensor_tensor(out=res[:, t, 1:SEQ], in0=ha[:, t, 0:SEQ - 1], scalar=w[:, 0:1],
                                         in1=res[:, t, 1:SEQ], op0=ALU.mult, op1=ALU.add).then_inc(S["tap_left"], 1)
            for t in range(NB):
                dve.wait_ge(S["tap_left"], t + 1)
                dve.scalar_tensor_tensor(out=res[:, t, 0:SEQ - 1], in0=ha[:, t, 1:SEQ], scalar=w[:, 2:3],
                                         in1=res[:, t, 0:SEQ - 1], op0=ALU.mult, op1=ALU.add).then_inc(S["tap_right"], 1)

        def pe_ssm(pe, c):
            for t in range(NB):
                pe.wait_ge(S["u_ok"], t + 1)
                pe.matmul(ps[0:2 * NSTATE, t, :], pcol("w_bc"), hb[:, t, :], start=True, stop=True).then_inc(S["bc_mm"], 1)
                pe.matmul(ps[0:DT_RANK, 4 + t, :], pcol("w_dt"), hb[:, t, :], start=True, stop=True).then_inc(S["t1_mm"], 1)
            for t in range(NB):
                pe.wait_ge(S["bc_ok"], t + 1)
                pe.wait_ge(S["t1_ok"], t + 1)
                pe.matmul(ps[:, t, :], pcol("w_dtp")[0:DT_RANK], t1_s[:, t, :], start=True, stop=True).then_inc(S["z_mm"], 1)
            pe.wait_ge(S["diag_ok"], 1)
            for t in range(NB):
                pe.matmul(ps[:, 4 + t, :], diag_d, ha[:, t, :], start=True, stop=False, skip_group_check=True)
            pe.wait_ge(S["z_act"], 4)

            def turn(n):
                def wait(sem, k):
                    if not isinstance(n, int) or 4 * n + k > 0:
                        pe.wait_ge(S[sem], 4 * n + k)

                for j in range(8):
                    s, t = ITEMS[j]
                    if t == 0:
                        pe.wait_ge(S[f"bc_in{s}"], 8 * n + 16)
                    wait("db_ok", j - 1)
                    pe.matmul(ps[:, j % 2, :], ones16[0:3, :], bc_row[:, s, 0, t, :], start=True,
                              stop=True).then_inc(S["bb_mm"], 1)
                    if not isinstance(n, int) or j >= 1:
                        c_row(n, j - 1, wait)
                    if not isinstance(n, int) or j >= 3:
                        sums(j - 3, wait)

            def c_row(n, j, wait):
                s, t = ITEMS[j % 8]
                wait("ch_ok", j - 1)
                pe.matmul(ps[:, 2 + j % 2, :], ones16[0:3, :], bc_row[:, s, 1, t, :], start=True,
                          stop=True).then_inc(S["cb_mm"], 1)

            def sums(j, wait):
                s, t = ITEMS[j % 8]
                wait("ch_ok", j + 1)
                pe.matmul(ps[:, 4 + t, :], ident, ch[:, s, t, :], start=False, stop=False,
                          skip_group_check=True).then_inc(S["sum_mm"], 1)

            turn(0)
            with pe.Fori(1, NSTATE // 2) as r:
                turn(2 * r)

            def last(sem, k):
                pe.wait_ge(S[sem], 4 * NSTATE + k)

            sums(-3, last)
            c_row(NSTATE, -1, last)
            sums(-2, last)
            sums(-1, last)

        def act_ssm(act, c):
            act.activation(a_neg, pcol("a_log"), ACT.Exp).then_inc(S["a_exp"], 1)
            for t in range(NB):
                act.wait_ge(S["tap_right"], t + 1)
                act.activation(hb[:, t, :], res[:, t, :], ACT.Silu).then_inc(S["u_ok"], 1)
            for t in range(NB):
                act.wait_ge(S["bc_mm"], t + 1)
                act.activation(bc_s[:, t, :], ps[0:2 * NSTATE, t, :], ACT.Identity,
                               bias=pcol("b_bc")[0:2 * NSTATE]).then_inc(S["bc_ok"], 1)
                act.wait_ge(S["t1_mm"], t + 1)
                act.activation(t1_s[:, t, :], ps[0:DT_RANK, 4 + t, :], ACT.Identity,
                               bias=pcol("b_dt")[0:DT_RANK]).then_inc(S["t1_ok"], 1)
            for t in range(NB):
                act.wait_ge(S["bc_ok"], t + 1)
                act.activation(bc16[:, 0, t], bc_s[:, t, :], ACT.Copy).then_inc(S["bc_part1"], 1)
            for t in range(NB):
                act.wait_ge(S["bc_rest"], t + 1)
                act.activation(bc16[:, 1, t], bc_s[:, t, :], ACT.Copy).then_inc(S["bc_part2"], 1)
            for t in range(NB):
                act.wait_ge(S["z_mm"], t + 1)
                act.activation(soft_a[:, t, :], ps[:, t, :], ACT.Abs, bias=pcol("b_dtp"))
                act.activation(soft_r[:, t, :], ps[:, t, :], ACT.Relu, bias=pcol("b_dtp")).then_inc(S["z_act"], 1)
            for t in range(NB):
                act.wait_ge(S["z_act"], t + 1)
                act.activation(soft_e[:, t, :], soft_a[:, t, :], ACT.Exp, scale=-1.0).then_inc(S["soft_exp"], 1)
            for t in range(NB):
                act.wait_ge(S["soft_u"], t + 1)
                act.activation(soft_l[:, t, :], soft_a[:, t, :], ACT.Ln).then_inc(S["soft_log"], 1)
            act.wait_ge(S["a_ok"], 1)
            act.wait_ge(S["dt_ok"], 4)
            act.wait_ge(S["bc_split"], 4)

            def decay(r, s):
                rate = a_neg.rearrange("p (r s) -> p s r", s=2)[:, s, :].unsqueeze(2)[:, r, :]
                act.activation(da[:, s], dt_s[:, :, :], ACT.Exp, scale=rate).then_inc(S["da_ok"], 1)

            for s in range(2):
                decay(0, s)
            with act.Fori(1, NSTATE // 2) as r:
                n = 2 * r
                for s in range(2):
                    act.wait_ge(S["scan_ok"], 4 * (n + s) - 4)
                    decay(r, s)

        def dve_ssm(dve, c):
            dve.wait_ge(S["a_exp"], 1)
            dve.tensor_scalar(a_neg, a_neg, -1.0, None, ALU.mult).then_inc(S["a_ok"], 1)
            dve.tensor_scalar(diag_d, ident, pcol("dcoef"), None, ALU.mult).then_inc(S["diag_ok"], 1)
            for t in range(NB):
                dve.wait_ge(S["bc_part1"], t + 1)
                dve.tensor_tensor(bc_s[:, t, :], bc_s[:, t, :], bc16[:, 0, t], ALU.subtract).then_inc(S["bc_rest"], 1)
            for t in range(NB):
                dve.wait_ge(S["bc_part2"], t + 1)
                dve.tensor_tensor(bc16[:, 2, t], bc_s[:, t, :], bc16[:, 1, t], ALU.subtract).then_inc(S["bc_split"], 1)
            for t in range(NB):
                dve.wait_ge(S["soft_exp"], t + 1)
                dve.tensor_scalar(soft_a[:, t, :], soft_e[:, t, :], 1.0, None, ALU.add).then_inc(S["soft_u"], 1)
            for t in range(NB):
                dve.wait_ge(S["soft_u"], t + 1)
                dve.scalar_tensor_tensor(out=soft_e[:, t, :], in0=soft_a[:, t, :], scalar=-1.0, in1=soft_e[:, t, :],
                                         op0=ALU.add, op1=ALU.subtract).then_inc(S["soft_d"], 1)
            for t in range(NB):
                dve.wait_ge(S["soft_log"], t + 1)
                dve.wait_ge(S["soft_d"], t + 1)
                dve.tensor_tensor(soft_l[:, t, :], soft_l[:, t, :], soft_e[:, t, :], ALU.subtract).then_inc(S["soft_s"], 1)
            for t in range(NB):
                dve.wait_ge(S["soft_s"], t + 1)
                dve.tensor_tensor(dt_s[:, t, :], soft_l[:, t, :], soft_r[:, t, :], ALU.add).then_inc(S["dt_ok"], 1)
            for t in range(NB):
                dve.wait_ge(S["dt_ok"], t + 1)
                dve.tensor_tensor(dtx[:, t, :], dt_s[:, t, :], ha[:, t, :], ALU.mult).then_inc(S["dtx_ok"], 1)
            dve.wait_ge(S["dtx_ok"], 4)
            dve.wait_ge(S["bc_out"], 16)

            def inputs(n, j):
                s, t = ITEMS[j]
                dve.wait_ge(S["bb_mm"], 4 * n + j + 1)
                dve.tensor_tensor(db[:, s, t, :], dtx[:, t, :], ps[:, j % 2, :], ALU.mult).then_inc(S["db_ok"], 1)

            def states(n, j):
                s, t = ITEMS[j % 8]
                if t == 0:
                    dve.wait_ge(S["da_ok"], n + s + 1)
                dve.wait_ge(S["db_ok"], 4 * n + j + 1)
                dve.tensor_tensor_scan(hst[:, s, t, :], da[:, s, t, :], db[:, s, t, :], 0.0, ALU.mult,
                                       ALU.add).then_inc(S["scan_ok"], 1)

            def outputs(n, j):
                s, t = ITEMS[j % 8]
                dve.wait_ge(S["cb_mm"], 4 * n + j + 1)
                dve.wait_ge(S["scan_ok"], 4 * n + j + 1)
                dve.tensor_tensor(ch[:, s, t, :], hst[:, s, t, :], ps[:, 2 + j % 2, :],
                                  ALU.mult).then_inc(S["ch_ok"], 1)

            def turn(n, first):
                for j in range(8):
                    inputs(n, j)
                    if j >= 1 or not first:
                        states(n, j - 1)
                    if j >= 2 or not first:
                        outputs(n, j - 2)

            turn(0, True)
            with dve.Fori(1, NSTATE // 2) as r:
                turn(2 * r, False)
            states(NSTATE, -1)
            outputs(NSTATE, -2)
            outputs(NSTATE, -1)

        def sp_ssm(sp, c):
            sp.wait_ge(S["bc_split"], 4)
            sp.dma_start(bc_dram.rearrange("a n (t q) -> n a t q", t=NB), bc16).then_inc(S["bc_out"], 16)
            sp.wait_ge(S["bc_out"], 16)
            rows = bc_dram.rearrange("a (w r s) (t q) -> s r a w t q", w=2, s=2, t=NB)
            for s in range(2):
                sp.dma_start(bc_row[:, s], rows[s, 0]).then_inc(S[f"bc_in{s}"], 16)
            with sp.Fori(1, NSTATE // 2) as r:
                n = 2 * r
                for s in range(2):
                    sp.wait_ge(S["cb_mm"], 4 * (n + s) - 4)
                    sp.dma_start(bc_row[:, s], rows[s, r]).then_inc(S[f"bc_in{s}"], 16)

        block_ = ctx.enter_context(nc.Block())
        x_tok = res[:, :, :].rearrange("p b (i d) -> p (b i) d", d=P)

        def x_ready(c):
            def wait(eng, t):
                if c["prev"] == "":
                    eng.wait_ge(S["x_cp"], t + 1)
                elif c["prev"] == "A":
                    eng.wait_ge(S["added"], c["added"])
                else:
                    eng.wait_ge(S["x_ok"], 4 * c["x_upd"] - 4 + t + 1)
            return wait

        end = dict(count, prev=stages[-1:])
        order = [(kind, dict(c, prev=stages[i - 1:i] if i else "")) for i, (kind, c) in enumerate(order)]

        @block_.sync
        def _(sp):
            sp.dma_start(con[:, :], consts).then_inc(S["consts_in"], 16)
            for t in range(NB):
                tiles = slice(TPB * t, TPB * t + TPB)
                sp.dma_start(x_tok[:, tiles, :],
                             x_in.rearrange("(i p) d -> p i d", p=P)[:, tiles, :]).then_inc(S[f"x_in{t}"], 16)
            sp.dma_start(par[:, :], params).then_inc(S["params_in"], 16)
            for kind, c in order:
                def slot_free(sp, s, c=c):
                    if c["prev"] in ("A", "C"):
                        sp.wait_ge(S["gated_ok"], c["added"] - 4 + 4 * s)
                    elif c["prev"] == "B":
                        sp.wait_ge(S["ln_out"], 4 * (c["ln"] - 1 - 2 * (1 - s)))
                    elif c["prev"] == "D":
                        sp.wait_ge(S["gated_ok"], c["added"])
                if kind == "A":
                    sp_moe(sp, c, pack_a, A_COLS, EXPERTS0, slot_free)
                elif kind == "B":
                    sp_layers(sp, c, slot_free)
                elif kind == "C":
                    sp_moe(sp, c, pack_c, C_COLS, EXPERTS1, slot_free)
                elif kind == "D":
                    sp_ssm(sp, c)
            for t in range(NB):
                sp.wait_ge(S["cp_out"], t + 1)
                sp.dma_start(out.rearrange("(i p) d -> p i d", p=P)[:, TPB * t:TPB * t + TPB, :],
                             x_tok[:, TPB * t:TPB * t + TPB, :]).then_inc(S["x_out"], 16)
            sp.wait_ge(S["x_out"], 64)

        @block_.tensor
        def _(pe):
            pe.wait_ge(S["consts_in"], 16)
            for t in range(NB):
                pe.wait_ge(S[f"x_in{t}"], 16)
                for i in range(TPB):
                    mm = pe.transpose(ps[:, t, i * P:(i + 1) * P], x_tok[:, TPB * t + i, :], ident)
                mm.then_inc(S["x_tr"], 1)
            pe.wait_ge(S["params_in"], 16)
            pe.wait_ge(S["consts16"], 1)
            for kind, c in order:
                n = c["ln"]
                pe_ln(pe, n, x, x_ready(c))
                if kind == "A":
                    pe_router(pe, n, c["moe_call"], pcol("gate"), EXPERTS0)
                    pe.wait_ge(S["gate_cp"], c["moe_call"] + 1)
                    pe_experts0(pe, c)
                elif kind == "B":
                    pe_layers(pe, c)
                    last = n + 2 * LAYERS
                    pe_ln(pe, last + 1, ha, lambda pe, t: pe.wait_ge(S["ln_out"], 4 * last + t + 1))
                elif kind == "C":
                    pe_ln(pe, n + 1, hb, lambda pe, t: pe.wait_ge(S["ln_out"], 4 * n + t + 1))
                    pe.wait_ge(S["ln_out"], 4 * n + 8)
                    pe_attention(pe, c)
                    pe_ln(pe, n + 2, hb, lambda pe, t: pe.wait_ge(S["x1_ok"], 4 * c["attn"] + 4))
                    pe_router(pe, n + 2, c["moe_call"], pcol("router"), EXPERTS1)
                    pe.wait_ge(S["gate_cp"], c["moe_call"] + 1)
                    pe_experts1(pe, c)
                else:
                    pe_ssm(pe, c)
            for t in range(NB):
                x_ready(end)(pe, t)
                for i in range(TPB):
                    mm = pe.transpose(ps[:, t, i * P:(i + 1) * P], x[:, t, i * P:(i + 1) * P], ident)
                mm.then_inc(S["tr_out"], 1)

        @block_.gpsimd
        def _(pool):
            pool.wait_ge(S["params_in"], 16)
            for kind, c in order:
                if kind == "C":
                    pool_conv(pool, c)

        @block_.scalar
        def _(act):
            act.wait_ge(S["consts_in"], 16)
            act.wait_ge(S["params_in"], 16)
            exp_call = 0
            for kind, c in order:
                n = c["ln"]
                act_ln(act, n)
                if kind == "A":
                    act_split(act, n, ha)
                    act_router(act, exp_call)
                    exp_call += 1
                    act_experts0(act, c)
                elif kind == "B":
                    act_layers(act, c)
                    act_ln(act, n + 2 * LAYERS + 1)
                elif kind == "C":
                    act_ln(act, n + 1)
                    act_attention(act, c)
                    act_ln(act, n + 2)
                    act_split(act, n + 2, ha)
                    act_experts1(act, c)
                else:
                    act_ssm(act, c)

        @block_.vector
        def _(dve):
            dve.wait_ge(S["consts_in"], 16)
            dve.tensor_copy(ident16[:, :], ident)
            dve.memset(ones16[:, :], 1.0)
            dve.tensor_copy(mask_qk16[:, :], ccol("mask_qk")).then_inc(S["consts16"], 1)
            for t in range(NB):
                dve.wait_ge(S["x_tr"], t + 1)
                dve.tensor_copy(x[:, t, :], ps[:, t, :]).then_inc(S["x_cp"], 1)
            dve.wait_ge(S["params_in"], 16)
            exp_call = 0
            for kind, c in order:
                n = c["ln"]
                x_ready(c)(dve, NB - 1)
                if kind == "A":
                    dve_ln(dve, n, x, ha)
                    dve.wait_ge(S["ln_out"], 4 * n + 4)
                    for piece in range(A_PIECES):
                        dve_weights(dve, c, A_PIECES, 0, 0, piece)
                    dve_split(dve, ha, c["moe_call"])
                    dve_router(dve, c["moe_call"], exp_call, EXPERTS0, 2)
                    exp_call += 1
                    dve_experts0(dve, c, x)
                elif kind == "B":
                    dve_ln(dve, n, x, ha)
                    dve.memset(v_aug[:, :, :, P:P + 1], 1.0)
                    dve_layers(dve, c)
                    last = n + 2 * LAYERS + 1
                    dve_ln(dve, last, ha, hb, (c["lns"] + 2 * LAYERS, pcol("gf"), pcol("bef")))
                    for t in range(NB):
                        dve.wait_ge(S["ln_out"], 4 * last + t + 1)
                        dve.tensor_tensor(x[:, t, :], x[:, t, :], hb[:, t, :], ALU.add).then_inc(S["x_ok"], 1)
                elif kind == "C":
                    dve_ln(dve, n, x, hb)
                    dve.wait_ge(S["ln_out"], 4 * n + 4)
                    dve_ln(dve, n + 1, hb, ha, (c["lns"], pcol("ln1_w"), pcol("ln1_b")))
                    dve.wait_ge(S["ln_out"], 4 * n + 8)
                    dve_attention(dve, c)
                    dve.wait_ge(S["x1_ok"], 4 * c["attn"] + 4)
                    dve_ln(dve, n + 2, hb, ha, (c["lns"] + 1, pcol("ln2_w"), pcol("ln2_b")))
                    dve.wait_ge(S["ln_out"], 4 * n + 12)
                    for piece in range(C_PIECES):
                        dve_weights(dve, c, C_PIECES, 0, 0, piece)
                    dve_split(dve, ha, c["moe_call"])
                    dve_router(dve, c["moe_call"], None, EXPERTS1, 1)
                    dve_experts1(dve, c, hb)
                    dve.wait_ge(S["added"], c["added"] + NB * EXPERTS1)
                    for t in range(NB):
                        dve.scalar_tensor_tensor(out=x[:, t, :], in0=hb[:, t, :], scalar=0.5, in1=x[:, t, :],
                                                 op0=ALU.mult, op1=ALU.add).then_inc(S["x_ok"], 1)
                else:
                    dve_ln(dve, n, x, ha)
                    dve.wait_ge(S["ln_out"], 4 * n + 4)
                    dve_conv_d(dve, c)
                    dve_ssm(dve, c)
                    dve.wait_ge(S["sum_mm"], NB * NSTATE)
                    for t in range(NB):
                        dve.tensor_tensor(x[:, t, :], x[:, t, :], ps[:, 4 + t, :], ALU.add).then_inc(S["x_ok"], 1)
            for t in range(NB):
                dve.wait_ge(S["tr_out"], t + 1)
                dve.tensor_copy(x_tok[:, TPB * t:TPB * t + TPB, :].rearrange("p i d -> p (i d)"),
                                ps[:, t, :]).then_inc(S["cp_out"], 1)


def shape_constants():
    at, n = columns(CONSTS)
    c = np.zeros((P, n), np.float32)

    def put(name, v):
        c[:, at[name][0]:at[name][1]] = v

    i = np.arange(P)
    put("ident", np.eye(P))
    put("mean", 1.0 / P)
    put("block", i[:, None] // DH == i[None, :] // DH)
    put("head_sum", i[:, None] // DH == i[None, :32])
    put("head_spread", i[:, None] % 32 == i[None, :] // DH)
    inv = (np.float32(1.0) / np.float32(10000.0) ** (np.arange(0, DH, 2, dtype=np.float32) / np.float32(DH))).astype(np.float32)
    angle = (np.arange(SEQ, dtype=np.float32)[:, None] * inv[None, :]).astype(np.float32)
    angle = np.concatenate([angle, angle], 1).astype(np.float64)
    sign = np.where(np.arange(DH) < DH // 2, -1.0, 1.0)
    put("cos", np.cos(angle).reshape(TPB, P, DH).transpose(1, 0, 2).reshape(P, -1))
    put("sin", (np.sin(angle) * sign).reshape(TPB, P, DH).transpose(1, 0, 2).reshape(P, -1))
    put("desc8", 8.0 - np.arange(8))
    put("desc4", 4.0 - np.arange(4))
    put("mask_qk", np.where(i[None, :] <= i[:, None], 0.0, NEG))
    put("tri", i[None, :] >= i[:, None])
    put("eps", 1e-5)
    put("tiny", 1e-6)
    return c


def kernel(**inputs):
    import numpy as _np
    import concourse.bacc as _bacc
    from concourse.bass_utils import run_bass_kernel_spmd as _run

    a = {k: _np.asarray(v) for k, v in inputs.items()}

    def chunks(w):
        e, r, n = w.shape
        return w.reshape(e, r // P, P, n).transpose(0, 2, 1, 3).reshape(e, P, -1)

    def cols(v):
        return v.reshape(v.shape[0], -1, P).transpose(0, 2, 1)

    g = lambda n: a["L0_attn_" + n]
    pack_a = _np.concatenate([a["L0_ffn_w1"], chunks(a["L0_ffn_w2"]), cols(a["L0_ffn_b1"]), cols(a["L0_ffn_b2"])], 2)
    kv_bias = _np.concatenate([g("bk"), g("bv")], 1)[:, None, :]
    pack_b = _np.concatenate(
        [g("Wq"), g("Wk"), g("Wv"), g("Wo"), g("W1"), chunks(g("W2")), _np.broadcast_to(kv_bias, (LAYERS, P, 2 * P))]
        + [cols(g(n)) for n in ("bq", "bo", "c1", "c2", "g1", "be1", "g2", "be2")], 2)
    pack_c = _np.concatenate([a["L1_ffn_expert_wv"], chunks(a["L1_ffn_expert_proj"])], 2)
    at, n = columns(PARAMS)
    params = _np.zeros((P, n), _np.float32)

    def put(name, v):
        v = v.reshape(v.shape[0], -1)
        params[0:v.shape[0], at[name][0]:at[name][1]] = v

    put("gate", a["L0_ffn_gate_w"].T)
    put("gf", g("gf"))
    put("bef", g("bef"))
    for k in ("ln1_w", "ln1_b", "ln2_w", "ln2_b"):
        put(k, a["L1_ffn_" + k])
    put("conv_c", a["L1_ffn_conv_w"])
    put("wqkv", a["L1_ffn_attn_w"])
    put("proj", a["L1_ffn_proj_w"])
    put("router", a["L1_ffn_router_w"])
    put("conv_d", a["L1_attn_conv_w"].T)
    put("w_bc", a["L1_attn_W_bc"])
    put("b_bc", a["L1_attn_b_bc"])
    put("w_dt", a["L1_attn_W_dt"])
    put("b_dt", a["L1_attn_b_dt"])
    put("w_dtp", a["L1_attn_W_dtp"])
    put("b_dtp", a["L1_attn_b_dtp"])
    put("a_log", a["L1_attn_A_log"])
    put("dcoef", a["L1_attn_Dcoeff"])
    nc = _bacc.Bacc("TRN2", target_bir_lowering=False, num_devices=1)
    arrays = {"x_in": a["L0_attn_x"].reshape(NB * SEQ, P), "pack_a": pack_a, "pack_b": pack_b, "pack_c": pack_c,
              "params_dram": params, "consts_dram": shape_constants()}
    arrays = {k: _np.ascontiguousarray(v) for k, v in arrays.items()}
    args = [nc.dram_tensor(k, v.shape, F32, kind="ExternalInput").ap() for k, v in arrays.items()]
    args.append(nc.dram_tensor("out_dram", (NB * SEQ, P), F32, kind="ExternalOutput").ap())
    build(nc, *args)
    r = _run(nc, [arrays], core_ids=[0])
    return r.results[0]["out_dram"].reshape(NB, SEQ, P)
```
